# Optimizing a Trainium2 kernel written in Bass

```python
import numpy as np
import jax
import jax.numpy as jnp

def _softmax(x, axis=-1):
    return jax.nn.softmax(x, axis=axis)

def _gelu(x):
    return jax.nn.gelu(x, approximate=True)

def _silu(x):
    return jax.nn.silu(x)

def _sigmoid(x):
    return jax.nn.sigmoid(x)

def _layernorm(x, axis=-1, eps=1e-05):
    m = jnp.mean(x, axis=axis, keepdims=True)
    v = jnp.var(x, axis=axis, keepdims=True)
    return (x - m) / jnp.sqrt(v + eps)

def _scatter_add(tgt, idx, src, axis=0):
    return tgt.at[idx].add(src)

def _segment_sum(src, seg, n):
    return jax.ops.segment_sum(src, seg, n)
kernel_name = 'mk_conv_attn_hybrid_d4_conv_nchw512_r4_3b1ea1'

def setup_inputs(seed: int=0):
    np.random.seed(seed)
    _w = jnp.asarray

    def _rec_inputs():
        import jax
        import jax.numpy as jnp
        _gk = jax.random.key(seed)
        x = -8.268e-05 + 0.9999 * jax.random.normal(jax.random.fold_in(_gk, 1), (256, 128, 7, 7), jnp.float32)
        return x
    x = _rec_inputs()

    def _L0_conv_setup():
        import jax, jax.numpy as jnp
        import numpy as np
        HEADS = 8
        DIM_HEAD = 16
        C = 128
        WIN = 7
        EPS = 1e-05

        def _rel_pos_bias(rel_table, H, W):
            hh = jnp.arange(H)
            ww = jnp.arange(W)
            hi = jnp.repeat(hh, W)
            wi = jnp.tile(ww, H)
            dh = hi[:, None] - hi[None, :] + (H - 1)
            dw = wi[:, None] - wi[None, :] + (W - 1)
            bias = rel_table[dh, dw]
            return jnp.transpose(bias, (2, 0, 1))
        key = jax.random.key(seed)
        ks = jax.random.split(key, 6)
        B = 512
        inner = HEADS * DIM_HEAD
        x = jax.random.normal(ks[0], (B, C, WIN, WIN), dtype=jnp.float32)
        gamma = jnp.ones((C,), dtype=jnp.float32)
        beta = jnp.zeros((C,), dtype=jnp.float32)
        w_qkv = jax.random.normal(ks[1], (C, 3 * inner), dtype=jnp.float32) / np.sqrt(C)
        rel_table = jax.random.normal(ks[2], (2 * WIN - 1, 2 * WIN - 1, HEADS), dtype=jnp.float32)
        w_out = jax.random.normal(ks[3], (inner, C), dtype=jnp.float32) / np.sqrt(inner)
        b_out = jnp.zeros((C,), dtype=jnp.float32)
        return {'x': x, 'gamma': gamma, 'beta': beta, 'w_qkv': w_qkv, 'rel_table': rel_table, 'w_out': w_out, 'b_out': b_out}
    _L0_conv_all = _L0_conv_setup()
    _L0_conv_in = {k: v for k, v in _L0_conv_all.items() if k in ('gamma', 'beta', 'w_qkv', 'rel_table', 'w_out', 'b_out')}
    del _L0_conv_all

    def _L1_conv_setup():
        import jax, jax.numpy as jnp
        import numpy as np
        NUM_GROUPS = 32
        EPS = 1e-06

        def group_norm(x, scale, bias):
            b, c, h, w = x.shape
            g = min(NUM_GROUPS, c)
            xr = x.reshape(b, g, c // g, h, w)
            mean = xr.mean(axis=(2, 3, 4), keepdims=True)
            var = xr.var(axis=(2, 3, 4), keepdims=True)
            xn = ((xr - mean) * jax.lax.rsqrt(var + EPS)).reshape(b, c, h, w)
            return xn * scale[None, :, None, None] + bias[None, :, None, None]

        def conv1x1(x, w, b):
            return jnp.einsum('bchw,oc->bohw', x, w) + b[None, :, None, None]
        key = jax.random.key(seed)
        ks = jax.random.split(key, 10)
        B, C, H, W = (4, 128, 16, 16)
        s = 1.0 / np.sqrt(C)
        return {'x': jax.random.normal(ks[0], (B, C, H, W), dtype=jnp.float32), 'gn_scale': jnp.ones((C,), jnp.float32), 'gn_bias': jnp.zeros((C,), jnp.float32), 'wq': jax.random.normal(ks[1], (C, C), jnp.float32) * s, 'bq': jnp.zeros((C,), jnp.float32), 'wk': jax.random.normal(ks[2], (C, C), jnp.float32) * s, 'bk': jnp.zeros((C,), jnp.float32), 'wv': jax.random.normal(ks[3], (C, C), jnp.float32) * s, 'bv': jnp.zeros((C,), jnp.float32), 'wp': jax.random.normal(ks[4], (C, C), jnp.float32) * s, 'bp': jnp.zeros((C,), jnp.float32)}
    _L1_conv_all = _L1_conv_setup()
    _L1_conv_in = {k: v for k, v in _L1_conv_all.items() if k in ('gn_scale', 'gn_bias', 'wq', 'bq', 'wk', 'bk', 'wv', 'bv', 'wp', 'bp')}
    del _L1_conv_all

    def _L2_attn_setup():
        import jax, jax.numpy as jnp
        import numpy as np
        B, N, D = (8, 512, 128)
        key = jax.random.key(seed)
        x = jax.random.normal(key, (B, N, D), dtype=jnp.float32)
        return {'x': x}
    _L2_attn_all = _L2_attn_setup()
    _L2_attn_in = {k: v for k, v in _L2_attn_all.items() if k in ()}
    del _L2_attn_all

    def _L2_ffn_setup():
        import jax, jax.numpy as jnp
        import numpy as np
        NUM_EXPERTS = 8
        TOP_K = 2
        key = jax.random.key(seed)
        ks = jax.random.split(key, 5)
        B, N, E, H, X = (8, 512, 128, 192, NUM_EXPERTS)
        s_in = 0.02
        return {'x': jax.random.normal(ks[0], (B, N, E), dtype=jnp.float32), 'Wg': jax.random.normal(ks[1], (E, X), dtype=jnp.float32) * s_in, 'bg': jnp.zeros((X,), dtype=jnp.float32), 'W1': jax.random.normal(ks[2], (X, E, H), dtype=jnp.float32) * (1.0 / np.sqrt(E)), 'b1': jnp.zeros((X, H), dtype=jnp.float32), 'W2': jax.random.normal(ks[3], (X, H, E), dtype=jnp.float32) * (1.0 / np.sqrt(H)), 'b2': jnp.zeros((X, E), dtype=jnp.float32)}
    _L2_ffn_all = _L2_ffn_setup()
    _L2_ffn_in = {k: v for k, v in _L2_ffn_all.items() if k in ('Wg', 'bg', 'W1', 'b1', 'W2', 'b2')}
    del _L2_ffn_all

    def _L3_attn_setup():
        import jax, jax.numpy as jnp
        import numpy as np
        B, S, D = (2, 512, 128)
        H = 8
        HD = D // H
        SCALES = (1, 2, 4)

        def _positional_encoding(seq_len, d):
            pos = jnp.arange(seq_len, dtype=jnp.float32)[:, None]
            inv = 10000.0 ** (jnp.arange(0, d, 2, dtype=jnp.float32) / d)
            ang = pos / inv
            return jnp.concatenate([jnp.sin(ang), jnp.cos(ang)], axis=-1)
        key = jax.random.key(seed)
        ks = jax.random.split(key, 7)
        std = 1.0 / np.sqrt(D)
        return {'x': jax.random.normal(ks[0], (B, S, D), dtype=jnp.float32), 'Wq': jax.random.normal(ks[1], (D, D), dtype=jnp.float32) * std, 'bq': jax.random.normal(ks[2], (D,), dtype=jnp.float32) * std, 'Wk': jax.random.normal(ks[3], (D, D), dtype=jnp.float32) * std, 'bk': jax.random.normal(ks[4], (D,), dtype=jnp.float32) * std, 'Wv': jax.random.normal(ks[5], (D, D), dtype=jnp.float32) * std, 'bv': jax.random.normal(ks[6], (D,), dtype=jnp.float32) * std}
    _L3_attn_all = _L3_attn_setup()
    _L3_attn_in = {k: v for k, v in _L3_attn_all.items() if k in ('Wq', 'bq', 'Wk', 'bk', 'Wv', 'bv')}
    del _L3_attn_all

    def _L3_ffn_setup():
        import jax, jax.numpy as jnp
        import numpy as np
        TOP_K = 2

        def _moe_forward(x, Wr, br, W1, b1, W2, b2):
            leading = x.shape[:-1]
            d = x.shape[-1]
            E = Wr.shape[0]
            xf = x.reshape(-1, d)
            N = xf.shape[0]
            logits = xf @ Wr.T + br
            routing = jax.nn.softmax(logits, axis=-1)
            sel_w, sel_idx = jax.lax.top_k(routing, TOP_K)
            sel_w = sel_w / jnp.sum(sel_w, axis=-1, keepdims=True)
            combine = jnp.zeros((N, E), dtype=xf.dtype).at[jnp.arange(N)[:, None], sel_idx].add(sel_w)
            h = jax.nn.gelu(jnp.einsum('nd,edf->enf', xf, W1) + b1[:, None, :])
            y = jnp.einsum('enf,efd->end', h, W2) + b2[:, None, :]
            out = jnp.einsum('ne,end->nd', combine, y)
            return out.reshape(*leading, d)
        key = jax.random.key(seed)
        ks = jax.random.split(key, 7)
        d_model, d_ff, E = (128, 512, 8)
        B, S = (2, 512)
        std = 0.02
        return {'x': jax.random.normal(ks[0], (B, S, d_model), dtype=jnp.float32), 'Wr': jax.random.normal(ks[1], (E, d_model), dtype=jnp.float32) * std, 'br': jnp.zeros((E,), dtype=jnp.float32), 'W1': jax.random.normal(ks[2], (E, d_model, d_ff), dtype=jnp.float32) * (1.0 / np.sqrt(d_model)), 'b1': jnp.zeros((E, d_ff), dtype=jnp.float32), 'W2': jax.random.normal(ks[3], (E, d_ff, d_model), dtype=jnp.float32) * (1.0 / np.sqrt(d_ff)), 'b2': jnp.zeros((E, d_model), dtype=jnp.float32)}
    _L3_ffn_all = _L3_ffn_setup()
    _L3_ffn_in = {k: v for k, v in _L3_ffn_all.items() if k in ('Wr', 'br', 'W1', 'b1', 'W2', 'b2')}
    del _L3_ffn_all
    return {'x': x, 'L0_conv_gamma': _L0_conv_in['gamma'], 'L0_conv_beta': _L0_conv_in['beta'], 'L0_conv_w_qkv': _L0_conv_in['w_qkv'], 'L0_conv_rel_table': _L0_conv_in['rel_table'], 'L0_conv_w_out': _L0_conv_in['w_out'], 'L0_conv_b_out': _L0_conv_in['b_out'], 'L1_conv_gn_scale': _L1_conv_in['gn_scale'], 'L1_conv_gn_bias': _L1_conv_in['gn_bias'], 'L1_conv_wq': _L1_conv_in['wq'], 'L1_conv_bq': _L1_conv_in['bq'], 'L1_conv_wk': _L1_conv_in['wk'], 'L1_conv_bk': _L1_conv_in['bk'], 'L1_conv_wv': _L1_conv_in['wv'], 'L1_conv_bv': _L1_conv_in['bv'], 'L1_conv_wp': _L1_conv_in['wp'], 'L1_conv_bp': _L1_conv_in['bp'], 'L2_ffn_Wg': _L2_ffn_in['Wg'], 'L2_ffn_bg': _L2_ffn_in['bg'], 'L2_ffn_W1': _L2_ffn_in['W1'], 'L2_ffn_b1': _L2_ffn_in['b1'], 'L2_ffn_W2': _L2_ffn_in['W2'], 'L2_ffn_b2': _L2_ffn_in['b2'], 'L3_attn_Wq': _L3_attn_in['Wq'], 'L3_attn_bq': _L3_attn_in['bq'], 'L3_attn_Wk': _L3_attn_in['Wk'], 'L3_attn_bk': _L3_attn_in['bk'], 'L3_attn_Wv': _L3_attn_in['Wv'], 'L3_attn_bv': _L3_attn_in['bv'], 'L3_ffn_Wr': _L3_ffn_in['Wr'], 'L3_ffn_br': _L3_ffn_in['br'], 'L3_ffn_W1': _L3_ffn_in['W1'], 'L3_ffn_b1': _L3_ffn_in['b1'], 'L3_ffn_W2': _L3_ffn_in['W2'], 'L3_ffn_b2': _L3_ffn_in['b2']}

def reference(x, L0_conv_gamma, L0_conv_beta, L0_conv_w_qkv, L0_conv_rel_table, L0_conv_w_out, L0_conv_b_out, L1_conv_gn_scale, L1_conv_gn_bias, L1_conv_wq, L1_conv_bq, L1_conv_wk, L1_conv_bk, L1_conv_wv, L1_conv_bv, L1_conv_wp, L1_conv_bp, L2_ffn_Wg, L2_ffn_bg, L2_ffn_W1, L2_ffn_b1, L2_ffn_W2, L2_ffn_b2, L3_attn_Wq, L3_attn_bq, L3_attn_Wk, L3_attn_bk, L3_attn_Wv, L3_attn_bv, L3_ffn_Wr, L3_ffn_br, L3_ffn_W1, L3_ffn_b1, L3_ffn_W2, L3_ffn_b2):
    import jax
    import jax.numpy as jnp

    def _L0_conv_ref(x, gamma, beta, w_qkv, rel_table, w_out, b_out):
        import jax, jax.numpy as jnp
        import numpy as np
        HEADS = 8
        DIM_HEAD = 16
        C = 128
        WIN = 7
        EPS = 1e-05

        def _rel_pos_bias(rel_table, H, W):
            hh = jnp.arange(H)
            ww = jnp.arange(W)
            hi = jnp.repeat(hh, W)
            wi = jnp.tile(ww, H)
            dh = hi[:, None] - hi[None, :] + (H - 1)
            dw = wi[:, None] - wi[None, :] + (W - 1)
            bias = rel_table[dh, dw]
            return jnp.transpose(bias, (2, 0, 1))
        B, Cc, H, W = x.shape
        N = H * W
        shortcut = x
        xs = jnp.transpose(x.reshape(B, Cc, N), (0, 2, 1))
        mu = jnp.mean(xs, axis=-1, keepdims=True)
        var = jnp.var(xs, axis=-1, keepdims=True)
        xn = (xs - mu) * jax.lax.rsqrt(var + EPS) * gamma + beta
        qkv = xn @ w_qkv
        q, k, v = jnp.split(qkv, 3, axis=-1)

        def heads(t):
            return jnp.transpose(t.reshape(B, N, HEADS, DIM_HEAD), (0, 2, 1, 3))
        q, k, v = (heads(q), heads(k), heads(v))
        scale = DIM_HEAD ** (-0.5)
        dots = jnp.einsum('bhnd,bhmd->bhnm', q, k) * scale
        dots = dots + _rel_pos_bias(rel_table, H, W)[None]
        attn = jax.nn.softmax(dots, axis=-1)
        out = jnp.einsum('bhnm,bhmd->bhnd', attn, v)
        out = jnp.transpose(out, (0, 2, 1, 3)).reshape(B, N, HEADS * DIM_HEAD)
        out = out @ w_out + b_out
        out = jnp.transpose(out, (0, 2, 1)).reshape(B, Cc, H, W)
        return out + shortcut

    def _L1_conv_ref(x, gn_scale, gn_bias, wq, bq, wk, bk, wv, bv, wp, bp):
        import jax, jax.numpy as jnp
        import numpy as np
        NUM_GROUPS = 32
        EPS = 1e-06

        def group_norm(x, scale, bias):
            b, c, h, w = x.shape
            g = min(NUM_GROUPS, c)
            xr = x.reshape(b, g, c // g, h, w)
            mean = xr.mean(axis=(2, 3, 4), keepdims=True)
            var = xr.var(axis=(2, 3, 4), keepdims=True)
            xn = ((xr - mean) * jax.lax.rsqrt(var + EPS)).reshape(b, c, h, w)
            return xn * scale[None, :, None, None] + bias[None, :, None, None]

        def conv1x1(x, w, b):
            return jnp.einsum('bchw,oc->bohw', x, w) + b[None, :, None, None]
        b, c, h, w = x.shape
        h_ = group_norm(x, gn_scale, gn_bias)
        q = conv1x1(h_, wq, bq).reshape(b, c, h * w)
        k = conv1x1(h_, wk, bk).reshape(b, c, h * w)
        v = conv1x1(h_, wv, bv).reshape(b, c, h * w)
        scale = jnp.asarray(c, x.dtype) ** (-0.5)
        scores = jnp.einsum('bci,bcj->bij', q, k) * scale
        attn = jax.nn.softmax(scores, axis=-1)
        out = jnp.einsum('bij,bcj->bci', attn, v).reshape(b, c, h, w)
        out = conv1x1(out, wp, bp)
        return x + out

    def _L2_attn_ref(x):
        import jax, jax.numpy as jnp
        import numpy as np
        B, N, D = (8, 512, 128)
        scores = jnp.einsum('bnd,bmd->bnm', x, x)
        atten = jax.nn.softmax(scores, axis=-1)
        out = jnp.einsum('bnm,bmd->bnd', atten, x)
        return out

    def _L2_ffn_ref(x, Wg, bg, W1, b1, W2, b2):
        import jax, jax.numpy as jnp
        import numpy as np
        NUM_EXPERTS = 8
        TOP_K = 2
        scores = jnp.einsum('bne,ex->bnx', x, Wg) + bg
        topk_vals, topk_idx = jax.lax.top_k(scores, TOP_K)
        gates = jax.nn.softmax(topk_vals, axis=-1)
        h = jnp.einsum('bne,xeh->bnxh', x, W1) + b1
        h = jax.nn.gelu(h, approximate=False)
        expert_out = jnp.einsum('bnxh,xhe->bnxe', h, W2) + b2
        onehot = jax.nn.one_hot(topk_idx, NUM_EXPERTS, dtype=x.dtype)
        combine = jnp.einsum('bnk,bnkx->bnx', gates, onehot)
        out = jnp.einsum('bnx,bnxe->bne', combine, expert_out)
        return out

    def _L3_attn_ref(x, Wq, bq, Wk, bk, Wv, bv):
        import jax, jax.numpy as jnp
        import numpy as np
        B, S, D = (2, 512, 128)
        H = 8
        HD = D // H
        SCALES = (1, 2, 4)

        def _positional_encoding(seq_len, d):
            pos = jnp.arange(seq_len, dtype=jnp.float32)[:, None]
            inv = 10000.0 ** (jnp.arange(0, d, 2, dtype=jnp.float32) / d)
            ang = pos / inv
            return jnp.concatenate([jnp.sin(ang), jnp.cos(ang)], axis=-1)
        b, s, d = x.shape
        x = x + _positional_encoding(s, d)[None]
        q = x @ Wq + bq
        k = x @ Wk + bk
        v = x @ Wv + bv
        qh = q.reshape(b, s, H, HD).transpose(0, 2, 1, 3)
        scale = HD ** (-0.5)
        outs = []
        for sc in SCALES:
            kh = k[:, ::sc].reshape(b, -1, H, HD).transpose(0, 2, 1, 3)
            vh = v[:, ::sc].reshape(b, -1, H, HD).transpose(0, 2, 1, 3)
            scores = jnp.einsum('bhqd,bhkd->bhqk', qh, kh) * scale
            w = jax.nn.softmax(scores, axis=-1)
            outs.append(jnp.einsum('bhqk,bhkd->bhqd', w, vh))
        out = jnp.mean(jnp.stack(outs, axis=-2), axis=-2)
        return out.transpose(0, 2, 1, 3).reshape(b, s, d)

    def _L3_ffn_ref(x, Wr, br, W1, b1, W2, b2):
        import jax, jax.numpy as jnp
        import numpy as np
        TOP_K = 2

        def _moe_forward(x, Wr, br, W1, b1, W2, b2):
            leading = x.shape[:-1]
            d = x.shape[-1]
            E = Wr.shape[0]
            xf = x.reshape(-1, d)
            N = xf.shape[0]
            logits = xf @ Wr.T + br
            routing = jax.nn.softmax(logits, axis=-1)
            sel_w, sel_idx = jax.lax.top_k(routing, TOP_K)
            sel_w = sel_w / jnp.sum(sel_w, axis=-1, keepdims=True)
            combine = jnp.zeros((N, E), dtype=xf.dtype).at[jnp.arange(N)[:, None], sel_idx].add(sel_w)
            h = jax.nn.gelu(jnp.einsum('nd,edf->enf', xf, W1) + b1[:, None, :])
            y = jnp.einsum('enf,efd->end', h, W2) + b2[:, None, :]
            out = jnp.einsum('ne,end->nd', combine, y)
            return out.reshape(*leading, d)
        return _moe_forward(x, Wr, br, W1, b1, W2, b2)

    def _gn(v, G=32, eps=1e-05):
        B_, C_, H_, W_ = v.shape
        g = v.reshape(B_, G, C_ // G, H_, W_)
        m = jnp.mean(g, axis=(2, 3, 4), keepdims=True)
        s = jnp.var(g, axis=(2, 3, 4), keepdims=True)
        return ((g - m) / jnp.sqrt(s + eps)).reshape(v.shape)

    def _ln_c(v, eps=1e-06):
        m = jnp.mean(v, axis=1, keepdims=True)
        s = jnp.var(v, axis=1, keepdims=True)
        return (v - m) / jnp.sqrt(s + eps)

    def _ln_t(v, eps=1e-05):
        m = jnp.mean(v, axis=-1, keepdims=True)
        s = jnp.var(v, axis=-1, keepdims=True)
        return (v - m) / jnp.sqrt(s + eps)

    def _to_tokens(v):
        B_, C_, H_, W_ = v.shape
        return v.reshape(B_, C_, H_ * W_).transpose(0, 2, 1)

    def _from_tokens(t, like):
        B_, C_, H_, W_ = like.shape
        return t.transpose(0, 2, 1).reshape(B_, C_, H_, W_)
    x = _L0_conv_ref(x, L0_conv_gamma, L0_conv_beta, L0_conv_w_qkv, L0_conv_rel_table, L0_conv_w_out, L0_conv_b_out)
    x = _L1_conv_ref(x, L1_conv_gn_scale, L1_conv_gn_bias, L1_conv_wq, L1_conv_bq, L1_conv_wk, L1_conv_bk, L1_conv_wv, L1_conv_bv, L1_conv_wp, L1_conv_bp)
    t = _to_tokens(x)
    t = t + _L2_attn_ref(_ln_t(t))
    t = t + _L2_ffn_ref(_ln_t(t), L2_ffn_Wg, L2_ffn_bg, L2_ffn_W1, L2_ffn_b1, L2_ffn_W2, L2_ffn_b2)
    t = t + _L3_attn_ref(_ln_t(t), L3_attn_Wq, L3_attn_bq, L3_attn_Wk, L3_attn_bk, L3_attn_Wv, L3_attn_bv)
    t = t + _L3_ffn_ref(_ln_t(t), L3_ffn_Wr, L3_ffn_br, L3_ffn_W1, L3_ffn_b1, L3_ffn_W2, L3_ffn_b2)
    x = _from_tokens(t, x)
    return x

_drawn_inputs = setup_inputs


def setup_inputs(seed=0):
    import zlib

    import numpy as np

    out = dict(_drawn_inputs(seed))
    spreads = {'L0_conv_gamma': (1.0, 0.2),
     'L0_conv_beta': (0.0, 0.1),
     'L0_conv_b_out': (0.0, 0.1),
     'L1_conv_gn_scale': (1.0, 0.2),
     'L1_conv_gn_bias': (0.0, 0.1),
     'L1_conv_bq': (0.0, 0.1),
     'L1_conv_bk': (0.0, 0.8),
     'L1_conv_bv': (0.0, 0.1),
     'L1_conv_bp': (0.0, 0.1),
     'L2_ffn_bg': (0.0, 0.1),
     'L2_ffn_b1': (0.0, 0.1),
     'L2_ffn_b2': (0.0, 0.1),
     'L3_ffn_br': (0.0, 0.1),
     'L3_ffn_b1': (0.0, 0.39),
     'L3_ffn_b2': (0.0, 0.1)}
    factors = {'L3_attn_bq': 2.889, 'L3_attn_bk': 8.0}
    for name, (base, spread) in spreads.items():
        noise = np.random.default_rng([zlib.crc32(name.encode()), seed]).standard_normal(out[name].shape)
        drawn = base * np.exp(spread * noise) if base else spread * noise
        out[name] = jnp.asarray(drawn.astype(out[name].dtype))
    for name, factor in factors.items():
        out[name] = (out[name] * factor).astype(out[name].dtype)
    return out
```

```python
from contextlib import ExitStack

import concourse.bass as bass
from concourse import mybir

F32 = mybir.dt.float32
F32R = mybir.dt.float32r
U32 = mybir.dt.uint32
ALU = mybir.AluOpType
ACT = mybir.ActivationFunctionType
AX_X = mybir.AxisListType.X

C = 128
N = 49
IMAGES = 256
GI = 8
T = GI * N
NG = IMAGES // GI
PAIRS = GI // 2
HEADS = 8
HD = 16
HP = HEADS // 2
S2 = 2 * N
B1 = 64
R = B1 + N
EXPERTS = 8
TT = T // 4
EXP_SET = "natural_log_exp_and_others"


def due(count):
    assert isinstance(count, int) or count.min_val > 0, "a wait that could be for nothing"
    return not isinstance(count, int) or count > 0


def over_groups(eng, body, head=2, tail=2):
    for g in range(head):
        body(g, g % 2)
    with eng.Fori(head // 2, (NG - tail) // 2) as i:
        for j in range(2):
            body(i * 2 + j, j)
    for g in range(NG - tail, NG):
        body(g, g % 2)


def exists(g):
    return not isinstance(g, int) or g < NG


def cols(g):
    return bass.ds(g * T, T) if not isinstance(g, int) else slice(g * T, g * T + T)


def bcast(ap, shape):
    return ap.to_broadcast(shape)


class PhaseSemaphores:

    def __init__(self, nc, prefix):
        self.nc, self.prefix, self.held = nc, prefix, []

    def __enter__(self):
        return self

    def __call__(self, name):
        self.held.append(self.nc.alloc_semaphore(name=f"{self.prefix}_{name}"))
        return self.held[-1]

    def __exit__(self, *error):
        if error[0] is None:
            self.nc.clear_and_free_semaphores(self.held)
            self.nc.all_engine_barrier()


class Shared:
    pass


def load_constants(nc, loads):
    with PhaseSemaphores(nc, "constants") as sem, nc.Block() as block:
        loaded = sem("loaded")

        @block.sync
        def _(sp):
            for dst, src in loads:
                sp.dma_start(dst, src).then_inc(loaded, 16)
            sp.wait_ge(loaded, 16 * len(loads))


def heads_phase(nc, sh, a, kind, x_in):
    window = kind == "window"
    scales = [1] if window else [1, 2, 4]
    widths = [len(range(0, N, s)) for s in scales]
    offs = [HEADS * sum(widths[:i]) for i in range(len(scales))]
    SW = HEADS * sum(widths)
    NS = len(scales)
    X, ident, mean_w = sh.X, sh.ident, sh.mean_w
    with ExitStack() as ctx:
        def sb(name, shape, dt=F32):
            return ctx.enter_context(nc.sbuf_tensor(f"{kind}_{name}", shape, dt))

        sem = ctx.enter_context(PhaseSemaphores(nc, kind))

        pj = [ctx.enter_context(nc.psum_tensor(f"{kind}_pj{i}", [C, 512], F32)) for i in range(2)]
        vps = ctx.enter_context(nc.psum_tensor(f"{kind}_vps", [C, 4, C], F32))
        sps = [ctx.enter_context(nc.psum_tensor(f"{kind}_sps{i}", [C, 512], F32)) for i in range(2)]
        ptps = ctx.enter_context(nc.psum_tensor(f"{kind}_ptps", [C, 512], F32))
        ops_ = [ctx.enter_context(nc.psum_tensor(f"{kind}_ops{i}", [C, 512], F32)) for i in range(2)]

        w = sb("w", [C, 3 * C])
        wo = sb("wo", [C, C]) if window else None
        b_in = sb("b_in", [C, 8])
        b_use = sb("b_use", [C, 4])
        cen = [sb(f"cen{i}", [C, T]) for i in range(2)]
        sq = sb("sq", [C, T])
        rs = sb("rs", [C, T])
        xn = [sb(f"xn{i}", [C, T]) for i in range(2)]
        twice = sb("twice", [C, GI, 2, N])
        qt = [sb(f"qt{i}", [C, T]) for i in range(2)]
        kt = sb("kt", [C, T])
        kbd = [sb(f"kbd{i}", [C, GI, HEADS, N]) for i in range(2)]
        vbd = [sb(f"vbd{i}", [S2, GI, C]) for i in range(2)]
        sc = [sb(f"sc{i}", [R, SW]) for i in range(2)]
        pr = [sb(f"pr{i}", [R, SW]) for i in range(4)]
        mx = [sb(f"mx{i}", [R, NS * HEADS]) for i in range(2)]
        sm = [sb(f"sm{i}", [R, NS * HEADS]) for i in range(2)]
        rc = [sb(f"rc{i}", [R, NS * HEADS]) for i in range(2)]
        pt = [sb(f"pt{i}", [S2, HP * R]) for i in range(2)]
        ot = sb("ot", [C, T])
        relb = sb("relb", [R, HEADS * N]) if window else None

        if window:
            loads = [(w[:, :], a["L0_conv_w_qkv"]), (wo[:, :], a["L0_conv_w_out"]), (b_in[:, 3:4], a["L0_conv_b_out"]),
                     (b_in[:, 4:5], a["L0_conv_gamma"]), (b_in[:, 5:6], a["L0_conv_beta"]), (relb[0:N, :], a["L0_conv_rel_bias"]),
                     (relb[N:B1, :], a["c_zeros"]), (relb[B1:R, :], a["L0_conv_rel_bias"])]
        else:
            loads = [(w[:, 0:C], a["L3_attn_Wq"]), (w[:, C:2 * C], a["L3_attn_Wk"]), (w[:, 2 * C:3 * C], a["L3_attn_Wv"]),
                     (b_in[:, 0:1], a["L3_attn_bq"]), (b_in[:, 1:2], a["L3_attn_bk"]), (b_in[:, 2:3], a["L3_attn_bv"])]
        wloaded, wready, bmm = sem("weights_loaded"), sem("weights_ready"), sem("bias_products")
        x_loaded = [sem(f"x_loaded{i}") for i in range(2)]
        mean_done, cen_done, sq_done, var_done = sem("mean"), sem("centred"), sem("squared"), sem("variance")
        ln_done, rs_done, xn_done, pos_done = sem("logvar"), sem("rstd"), sem("normed"), sem("positioned")
        q_mm, k_mm, q_done, k_done, kbd_done = sem("q_mm"), sem("k_mm"), sem("q_out"), sem("k_out"), sem("kbd")
        v_mm, v_done, twice_done = sem("v_mm"), sem("v_out"), sem("twice")
        s_mm, add_done, max_done, sub_done, exp_done = sem("s_mm"), sem("biased"), sem("maxed"), sem("shifted"), sem("exped")
        sum_done, rec_done, prob_done, merged = sem("summed"), sem("recip"), sem("probs"), sem("merged")
        t_mm, t_done, pv_mm, o_done, out_mm, res_done = sem("t_mm"), sem("t_out"), sem("pv_mm"), sem("o_out"), sem("out_mm"), sem("residual")
        mid_done = sem("merged_mid")

        xn_ready = xn_done if window else pos_done
        final_probs = prob_done if window else merged

        block = ctx.enter_context(nc.Block())

        @block.sync
        def _(sp):
            for dst, src in loads:
                sp.dma_start(dst, src).then_inc(wloaded, 16)
            if window:
                def load(g, j):
                    if due(16 * ((g - j) // 2) if isinstance(g, int) else (g - j) * 8):
                        sp.wait_ge(x_loaded[j], 16 * ((g - j) // 2) if isinstance(g, int) else (g - j) * 8)
                    dst = X[:, cols(g)].rearrange("c (b n) -> c b n", n=N)
                    src = x_in[bass.ds(g * GI, GI)] if not isinstance(g, int) else x_in[g * GI:(g + 1) * GI]
                    sp.dma_start(dst, src.rearrange("b c n -> c b n")).then_inc(x_loaded[j], 16)

                over_groups(sp, load)
                for j in range(2):
                    sp.wait_ge(x_loaded[j], 16 * (NG // 2))

        def landed(eng, g, j):
            if window:
                if due(16 * (g // 2 + 1) if isinstance(g, int) else (g - j) * 8 + 16):
                    eng.wait_ge(x_loaded[j], 16 * (g // 2 + 1) if isinstance(g, int) else (g - j) * 8 + 16)

        @block.tensor
        def _(pe):
            pe.wait_ge(wloaded, 16 * len(loads))
            if window:
                for m in range(3):
                    last = pe.matmul(ops_[0][:, m:m + 1], w[:, m * C:(m + 1) * C], b_in[:, 5:6], start=(m == 0), stop=True,
                                     skip_group_check=True)
                last.then_inc(bmm, 1)
                pe.wait_ge(wready, 2)
                pe.matmul(ops_[0][:, 3:4], wo[:, :], b_use[:, 2:3], start=True, stop=True,
                          skip_group_check=True).then_inc(bmm, 1)
            pe.wait_ge(wready, 3)

            def mean(g, j):
                if not exists(g):
                    return
                landed(pe, g, j)
                if due(g):
                    pe.wait_ge(q_done, g)
                pe.matmul(pj[0][:, 0:T], mean_w[:, :], X[:, cols(g)], start=True, stop=True).then_inc(mean_done, 1)

            def var(g, j):
                if not exists(g):
                    return
                pe.wait_ge(sq_done, g + 1)
                pe.wait_ge(cen_done, g + 1)
                pe.matmul(pj[0][:, 0:T], mean_w[:, :], sq[:, :], start=True, stop=True).then_inc(var_done, 1)

            def qk(g, j):
                if not exists(g):
                    return
                pe.wait_ge(xn_ready, g + 1)
                pe.wait_ge(ln_done, g + 1)
                pe.matmul(pj[0][:, 0:T], w[:, 0:C], xn[j][:, :], start=True, stop=True).then_inc(q_mm, 1)
                if due((g - 2) if window else 0):
                    pe.wait_ge(res_done, (g - 2) if window else 0)
                if due(g):
                    pe.wait_ge(k_done, g)
                pe.matmul(pj[1][:, 0:T], w[:, C:2 * C], xn[j][:, :], start=True, stop=True).then_inc(k_mm, 1)

            def val(g, j, half):
                if not exists(g):
                    return
                pe.wait_ge(v_done, g * 2 + half)
                pe.wait_ge(twice_done, g + 1)
                for b in range(4):
                    last = pe.matmul(vps[0:S2, b, :], twice[:, 4 * half + b].rearrange("c r n -> c (r n)"), w[:, 2 * C:3 * C],
                                     start=True, stop=True, skip_group_check=True)
                last.then_inc(v_mm, 1)

            def scores(g, j, p):
                if not exists(g):
                    return
                n = g * PAIRS + p
                pe.wait_ge(q_done, g + 1)
                pe.wait_ge(kbd_done, n + 1)
                if due(n - 1):
                    pe.wait_ge((add_done if window else sub_done), n - 1)
                for im, m in ((0, B1), (1, N)):
                    a = (2 * p + im) * N
                    last = pe.matmul(sps[p % 2][B1 * im:B1 * im + m, 0:HEADS * N], qt[j][:, a:a + m],
                                     kbd[j][:, 2 * p + im].rearrange("c h n -> c (h n)"), start=True, stop=True)
                last.then_inc(s_mm, 1)

            def turn(n, p):
                if isinstance(n, int) and n < 0:
                    return
                pe.wait_ge(final_probs, n + 1)
                if due(n):
                    pe.wait_ge(t_done, n)
                for hp in range(HP):
                    last = pe.transpose(ptps[0:S2, hp * R:(hp + 1) * R], pr[p][:, hp * S2:(hp + 1) * S2], ident[0:R, 0:R])
                last.then_inc(t_mm, 1)

            def values(g, n, j, p):
                if isinstance(n, int) and n < 0:
                    return
                pe.wait_ge(t_done, n + 1)
                pe.wait_ge(v_done, g * 2 + 1 + p // 2)
                if p == 0:
                    if due(g - 1):
                        pe.wait_ge(o_done, g - 1)
                for im in range(2):
                    a = (2 * p + im) * N
                    for hp in range(HP):
                        last = pe.matmul(ops_[j][32 * hp:32 * hp + 32, a:a + N], vbd[j][:, 2 * p + im, 32 * hp:32 * hp + 32],
                                         pt[p % 2][:, hp * R + B1 * im:hp * R + B1 * im + N], start=True, stop=True,
                                         skip_group_check=True)
                last.then_inc(pv_mm, 1)

            def out(g):
                if not window or (isinstance(g, int) and g < 0):
                    return
                pe.wait_ge(o_done, g + 1)
                pe.wait_ge(k_done, g + 3 if exists(g + 2) else NG)
                if due(g):
                    pe.wait_ge(res_done, g)
                pe.matmul(pj[1][:, 0:T], wo[:, :], ot[:, :], start=True, stop=True).then_inc(out_mm, 1)

            mean(0, 0)
            var(0, 0)
            qk(0, 0)
            val(0, 0, 0)
            val(0, 0, 1)
            mean(1, 1)
            var(1, 1)
            scores(0, 0, 0)
            scores(0, 0, 1)

            def body(g, j):
                for p in range(PAIRS):
                    n = g * PAIRS + p
                    if p < 2:
                        scores(g, j, p + 2)
                    else:
                        scores(g + 1, 1 - j, p - 2)
                    if p < 2:
                        if not (isinstance(g, int) and g == 0):
                            values(g - 1, n - 2, 1 - j, p + 2)
                    else:
                        values(g, n - 2, j, p - 2)
                    if p == 0:
                        qk(g + 1, 1 - j)
                    if p == 1:
                        val(g + 1, 1 - j, 0)
                    if p == 2:
                        val(g + 1, 1 - j, 1)
                        mean(g + 2, j)
                        out(g - 1)
                    if p == 3:
                        var(g + 2, j)
                    turn(n - 1, (p - 1) % 4)

            over_groups(pe, body)
            last_n = NG * PAIRS
            values(NG - 1, last_n - 2, 1, 2)
            turn(last_n - 1, 3)
            values(NG - 1, last_n - 1, 1, 3)
            out(NG - 1)

        @block.vector
        def _(dve):
            dve.wait_ge(wloaded, 16 * len(loads))
            if window:
                dve.wait_ge(bmm, 1)
                dve.tensor_copy(b_use[:, 0:3], ops_[0][:, 0:3]).then_inc(wready, 1)
                dve.tensor_scalar(w[:, :], w[:, :], b_in[:, 4:5], None, ALU.mult).then_inc(wready, 1)
                dve.wait_ge(bmm, 2)
                dve.tensor_tensor(b_use[:, 3:4], ops_[0][:, 3:4], b_in[:, 3:4], ALU.add).then_inc(wready, 1)
                dve.tensor_scalar(b_use[:, 0:1], b_use[:, 0:1], HD ** -0.5, None, ALU.mult).then_inc(wready, 1)
            else:
                dve.tensor_copy(b_use[:, 1:3], b_in[:, 1:3]).then_inc(wready, 3)
                dve.tensor_scalar(b_use[:, 0:1], b_in[:, 0:1], HD ** -0.5, None, ALU.mult).then_inc(wready, 1)

            def centre(g, j):
                if not exists(g):
                    return
                dve.wait_ge(mean_done, g + 1)
                landed(dve, g, j)
                if due(g - 1):
                    dve.wait_ge(sq_done, g - 1)
                if due(g - 1):
                    dve.wait_ge(xn_done, g - 1)
                dve.tensor_tensor(cen[j][:, :], X[:, cols(g)], pj[0][:, 0:T], ALU.subtract).then_inc(cen_done, 1)

            def norm(g, j):
                if not exists(g):
                    return
                dve.wait_ge(rs_done, g + 1)
                if due(g * 2 - 2):
                    dve.wait_ge(v_mm, g * 2 - 2)
                if due(g - 1):
                    dve.wait_ge(twice_done, g - 1)
                if not window:
                    if due(g - 1):
                        dve.wait_ge(pos_done, g - 1)
                dve.tensor_tensor(xn[j][:, :], cen[j][:, :], rs[:, :], ALU.mult).then_inc(xn_done, 1)
                if not window:
                    dve.wait_ge(xn_done, g + 1)
                    v = xn[j][:, :].rearrange("c (b n) -> c b n", n=N)
                    dve.tensor_tensor(v, v, sh.pos[:, :][:, None, :].to_broadcast([C, GI, N]), ALU.add).then_inc(pos_done, 1)

            def val(g, j, half):
                if not exists(g):
                    return
                dve.wait_ge(v_mm, g * 2 + half + 1)
                if due(g * PAIRS - 2 * PAIRS + 2 * half + 2):
                    dve.wait_ge(pv_mm, g * PAIRS - 2 * PAIRS + 2 * half + 2)
                dve.tensor_tensor(vbd[j][:, 4 * half:4 * half + 4, :], vps[0:S2, :, :],
                                  sh.vmask[:, :][:, None, :].to_broadcast([S2, 4, C]), ALU.mult).then_inc(v_done, 1)

            def sview(ap, i):
                return ap[:, offs[i]:offs[i] + HEADS * widths[i]].rearrange("q (h k) -> q h k", h=HEADS)

            def picked(ap, i):
                return ap[0:R, 0:HEADS * N].rearrange("q (h k) -> q h k", h=HEADS)[:, :, 0:N:scales[i]]

            def shift(g, j, p):
                if not exists(g):
                    return
                n = g * PAIRS + p
                k = p % 2
                dve.wait_ge(s_mm, n + 1)
                if due(n - 1):
                    dve.wait_ge(exp_done, n - 1)
                if window:
                    dve.tensor_tensor(sc[k][:, :], sps[k][0:R, 0:HEADS * N], relb[:, :], ALU.add).then_inc(add_done, 1)
                    dve.wait_ge(add_done, n + 1)
                    if due(n - 1):
                        dve.wait_ge(sub_done, n - 1)
                    dve.tensor_reduce(mx[k][:, :], sview(sc[k], 0), AX_X, ALU.max).then_inc(max_done, 1)
                    dve.wait_ge(max_done, n + 1)
                    v = sview(sc[k], 0)
                    dve.tensor_tensor(v, v, mx[k][:, :][:, :, None].to_broadcast([R, HEADS, N]), ALU.subtract).then_inc(sub_done, 1)
                else:
                    if due(n - 1):
                        dve.wait_ge(sub_done, n - 1)
                    for i in range(NS):
                        last = dve.tensor_reduce(mx[k][:, i * HEADS:(i + 1) * HEADS], picked(sps[k], i), AX_X, ALU.max)
                    last.then_inc(max_done, 1)
                    dve.wait_ge(max_done, n + 1)
                    for i in range(NS):
                        last = dve.tensor_tensor(sview(sc[k], i), picked(sps[k], i),
                                                 mx[k][:, i * HEADS:(i + 1) * HEADS][:, :, None].to_broadcast([R, HEADS, widths[i]]),
                                                 ALU.subtract)
                    last.then_inc(sub_done, 1)

            def total(n, p):
                k = p % 2
                dve.wait_ge(exp_done, n + 1)
                if due(n - 1):
                    dve.wait_ge(rec_done, n - 1)
                for i in range(NS):
                    last = dve.tensor_reduce(sm[k][:, i * HEADS:(i + 1) * HEADS], sview(pr[p], i), AX_X, ALU.add)
                last.then_inc(sum_done, 1)
                dve.wait_ge(sum_done, n + 1)
                if due(n - 1):
                    dve.wait_ge(prob_done, n - 1)
                dve.reciprocal(rc[k][:, :], sm[k][:, :]).then_inc(rec_done, 1)

            def outputs(g, j):
                if isinstance(g, int) and g < 0:
                    return
                if window:
                    dve.wait_ge(out_mm, g + 1)
                    dve.scalar_tensor_tensor(out=X[:, cols(g)], in0=pj[1][:, 0:T], scalar=b_use[:, 3:4], in1=X[:, cols(g)],
                                             op0=ALU.add, op1=ALU.add).then_inc(res_done, 1)
                else:
                    dve.wait_ge(o_done, g + 1)
                    dve.tensor_tensor(X[:, cols(g)], X[:, cols(g)], ot[:, :], ALU.add).then_inc(res_done, 1)

            centre(0, 0)
            norm(0, 0)
            val(0, 0, 0)
            val(0, 0, 1)
            centre(1, 1)
            norm(1, 1)
            shift(0, 0, 0)

            def body(g, j):
                for p in range(PAIRS):
                    if p < 3:
                        shift(g, j, p + 1)
                    else:
                        shift(g + 1, 1 - j, 0)
                    total(g * PAIRS + p, p)
                    if p == 1:
                        val(g + 1, 1 - j, 0)
                    if p == 2:
                        val(g + 1, 1 - j, 1)
                        centre(g + 2, j)
                        outputs(g - 1, 1 - j)
                    if p == 3:
                        norm(g + 2, j)

            over_groups(dve, body)
            outputs(NG - 1, 1)
            dve.wait_ge(res_done, NG)

        @block.gpsimd
        def _(pool):
            def keys(g, j, p):
                if not exists(g):
                    return
                pool.wait_ge(k_done, g + 1)
                if due(g * PAIRS - 2 * PAIRS + p + 1):
                    pool.wait_ge(s_mm, g * PAIRS - 2 * PAIRS + p + 1)
                a = 2 * p * N
                pool.tensor_tensor(kbd[j][:, 2 * p:2 * p + 2],
                                   kt[:, a:a + S2].rearrange("c (b n) -> c b n", n=N)[:, :, None, :].to_broadcast([C, 2, HEADS, N]),
                                   sh.kmask[:, :][:, None, :, None].to_broadcast([C, 2, HEADS, N]), ALU.mult).then_inc(kbd_done, 1)

            def probs(n, p):
                pool.wait_ge(rec_done, n + 1)
                for i in range(NS):
                    v = pr[p][:, offs[i]:offs[i] + HEADS * widths[i]].rearrange("q (h k) -> q h k", h=HEADS)
                    last = pool.tensor_tensor(v, v, rc[p % 2][:, i * HEADS:(i + 1) * HEADS][:, :, None].to_broadcast([R, HEADS, widths[i]]),
                                              ALU.mult)
                last.then_inc(prob_done, 1)
                if not window:
                    full = pr[p][:, 0:HEADS * N].rearrange("q (h k) -> q h k", h=HEADS)
                    for i, (s_wait, s_sig) in ((1, (prob_done, mid_done)), (2, (mid_done, merged))):
                        pool.wait_ge(s_wait, n + 1)
                        v = pr[p][:, offs[i]:offs[i] + HEADS * widths[i]].rearrange("q (h k) -> q h k", h=HEADS)
                        d = full[:, :, 0:N:scales[i]]
                        pool.tensor_tensor(d, d, v, ALU.add).then_inc(s_sig, 1)

            for p in range(PAIRS):
                keys(0, 0, p)

            def body(g, j):
                for p in range(PAIRS):
                    probs(g * PAIRS + p, p)
                    keys(g + 1, 1 - j, p)

            over_groups(pool, body)

        @block.scalar
        def _(act):
            act.preload_act_table_set(EXP_SET)
            act.wait_ge(wready, 4)

            def square(g, j):
                if not exists(g):
                    return
                act.wait_ge(cen_done, g + 1)
                if due(g):
                    act.wait_ge(var_done, g)
                act.activation(sq[:, :], cen[j][:, :], ACT.Square).then_inc(sq_done, 1)

            def rstd(g, j):
                if not exists(g):
                    return
                act.wait_ge(var_done, g + 1)
                if due(g):
                    act.wait_ge(xn_done, g)
                act.activation(rs[:, :], pj[0][:, 0:T], ACT.Ln, bias=sh.eps5[:, 0:1]).then_inc(ln_done, 1)
                act.wait_ge(ln_done, g + 1)
                act.activation(rs[:, :], rs[:, :], ACT.Exp, scale=-0.5).then_inc(rs_done, 1)

            def q_out(g, j):
                if not exists(g):
                    return
                act.wait_ge(q_mm, g + 1)
                if due(g * PAIRS - PAIRS):
                    act.wait_ge(s_mm, g * PAIRS - PAIRS)
                act.activation(qt[j][:, :], pj[0][:, 0:T], ACT.Identity, bias=b_use[:, 0:1], scale=HD ** -0.5).then_inc(q_done, 1)
                act.wait_ge(k_mm, g + 1)
                if due(g * PAIRS):
                    act.wait_ge(kbd_done, g * PAIRS)
                act.activation(kt[:, :], pj[1][:, 0:T], ACT.Identity, bias=b_use[:, 1:2]).then_inc(k_done, 1)
                if due(g * 2):
                    act.wait_ge(v_mm, g * 2)
                act.activation(twice[:, :, :, :], xn[j][:, :].rearrange("c (b n) -> c b n", n=N)[:, :, None, :].to_broadcast([C, GI, 2, N]),
                               ACT.Copy).then_inc(twice_done, 1)

            def expo(g, j, p):
                if not exists(g):
                    return
                n = g * PAIRS + p
                act.wait_ge(sub_done, n + 1)
                if due(n - 3):
                    act.wait_ge(t_mm, n - 3)
                act.activation(pr[p][:, :], sc[p % 2][:, :], ACT.Exp).then_inc(exp_done, 1)

            def turned(n, p):
                if isinstance(n, int) and n < 0:
                    return
                act.wait_ge(t_mm, n + 1)
                if due(n - 1):
                    act.wait_ge(pv_mm, n - 1)
                act.activation(pt[p % 2][:, :], ptps[0:S2, 0:HP * R], ACT.Copy).then_inc(t_done, 1)

            def o_out(g, j):
                if isinstance(g, int) and g < 0:
                    return
                act.wait_ge(pv_mm, (g + 1) * PAIRS)
                if window:
                    if due(g):
                        act.wait_ge(out_mm, g)
                    act.activation(ot[:, :], ops_[j][:, 0:T], ACT.Copy).then_inc(o_done, 1)
                else:
                    if due(g):
                        act.wait_ge(res_done, g)
                    act.activation(ot[:, :], ops_[j][:, 0:T], ACT.Identity, bias=b_use[:, 2:3],
                                   scale=1.0 / NS).then_inc(o_done, 1)

            square(0, 0)
            rstd(0, 0)
            q_out(0, 0)
            square(1, 1)
            rstd(1, 1)
            expo(0, 0, 0)

            def body(g, j):
                for p in range(PAIRS):
                    n = g * PAIRS + p
                    if p == 0:
                        q_out(g + 1, 1 - j)
                    turned(n - 1, (p - 1) % 4)
                    if p < 3:
                        expo(g, j, p + 1)
                    else:
                        expo(g + 1, 1 - j, 0)
                    if p == 1:
                        o_out(g - 1, 1 - j)
                    if p == 2:
                        square(g + 2, j)
                    if p == 3:
                        rstd(g + 2, j)

            over_groups(act, body)
            turned(NG * PAIRS - 1, 3)
            o_out(NG - 1, 1)


def single_phase(nc, sh, a, kind):
    conv = kind == "conv"
    X, ident, mean_w = sh.X, sh.ident, sh.mean_w
    with ExitStack() as ctx:
        def sb(name, shape, dt=F32):
            return ctx.enter_context(nc.sbuf_tensor(f"{kind}_{name}", shape, dt))

        def ps(name, shape):
            return ctx.enter_context(nc.psum_tensor(f"{kind}_{name}", shape, F32))

        sem = ctx.enter_context(PhaseSemaphores(nc, kind))

        st = ps("st", [C, 512])
        pjq, pjk = ps("pjq", [C, 512]), ps("pjk", [C, 512])
        vps = ps("vps", [C, GI, C])
        sps, ptps, ops_ = ps("sps", [C, 512]), ps("ptps", [C, 512]), ps("ops", [C, 512])
        if conv:
            w = sb("w", [C, 4 * C])
            b_in = sb("b_in", [C, 6])
            b_use = sb("b_use", [C, 4])
            csum = sb("csum", [C, GI])
            loads = [(w[:, i * C:(i + 1) * C], a[f"L1_conv_{n}"]) for i, n in enumerate(("wq", "wk", "wv", "wp"))]
            loads += [(b_in[:, i:i + 1], a[f"L1_conv_{n}"]) for i, n in enumerate(("bq", "bk", "bv", "bp", "gn_scale", "gn_bias"))]
            ssum = sb("ssum", [C, GI])
        cen = [sb(f"cen{i}", [C, T]) for i in range(2)]
        sq = sb("sq", [C, T])
        rs = sb("rs", [C, GI if conv else T])
        xn = [sb(f"xn{i}", [C, T]) for i in range(2)]
        qt = sb("qt", [C, T]) if conv else None
        kt = sb("kt", [C, T]) if conv else None
        vt = sb("vt", [N, GI, C])
        sc = sb("sc", [R, PAIRS * N])
        pr = sb("pr", [R, PAIRS * N])
        mx, sm, rc = sb("mx", [R, PAIRS]), sb("sm", [R, PAIRS]), sb("rc", [R, PAIRS])
        pt = sb("pt", [N, PAIRS * R])
        ot = sb("ot", [C, T]) if conv else None

        wloaded, wready, bmm = sem("weights_loaded"), sem("weights_ready"), sem("bias_products")
        csum_done, mean_done, cen_done, sq_done, ssum_done = sem("csum"), sem("mean"), sem("centred"), sem("squared"), sem("ssum")
        var_done, ln_done, rs_done, xn_done = sem("variance"), sem("logvar"), sem("rstd"), sem("normed")
        q_mm, k_mm, q_done, k_done, v_mm, v_done = sem("q_mm"), sem("k_mm"), sem("q_out"), sem("k_out"), sem("v_mm"), sem("v_out")
        s_mm, max_done, sub_done, exp_done = sem("s_mm"), sem("maxed"), sem("shifted"), sem("exped")
        sum_done, rec_done, prob_done = sem("summed"), sem("recip"), sem("probs")
        t_mm, t_done, pv_mm, o_done, out_mm, res_done = sem("t_mm"), sem("t_out"), sem("pv_mm"), sem("o_out"), sem("out_mm"), sem("residual")
        k_ready = k_done if conv else xn_done
        final_mm = out_mm if conv else pv_mm
        vt_read = pv_mm

        block = ctx.enter_context(nc.Block())

        def images(ap):
            return ap.rearrange("c (b n) -> c b n", n=N)

        if conv:
            @block.sync
            def _(sp):
                for dst, src in loads:
                    sp.dma_start(dst, src).then_inc(wloaded, 16)

        @block.tensor
        def _(pe):
            if conv:
                pe.wait_ge(wloaded, 16 * len(loads))
                for m in range(3):
                    last = pe.matmul(sps[:, m:m + 1], w[:, m * C:(m + 1) * C], b_in[:, 5:6], start=(m == 0), stop=True,
                                     skip_group_check=True)
                last.then_inc(bmm, 1)
                pe.wait_ge(wready, 2)
                pe.matmul(sps[:, 3:4], w[:, 3 * C:4 * C], b_use[:, 2:3], start=True, stop=True,
                          skip_group_check=True).then_inc(bmm, 1)
                pe.wait_ge(wready, 3)

            def mean(g, j):
                if not exists(g):
                    return
                if due(g):
                    pe.wait_ge(ln_done, g)
                if conv:
                    pe.wait_ge(csum_done, g + 1)
                    pe.matmul(st[:, 0:GI], sh.group_w[:, :], csum[:, :], start=True, stop=True).then_inc(mean_done, 1)
                else:
                    if not (isinstance(g, int) and g < 2):
                        if due(g):
                            pe.wait_ge(xn_done, g)
                        if due(2 * (g - 1)):
                            pe.wait_ge(v_done, 2 * (g - 1))
                        if due(g - 1):
                            pe.wait_ge(prob_done, g - 1)
                        if due(g - 2):
                            pe.wait_ge(t_done, g - 2)
                    pe.matmul(st[:, 0:T], mean_w[:, :], X[:, cols(g)], start=True, stop=True).then_inc(mean_done, 1)

            def var(g, j):
                if not exists(g):
                    return
                pe.wait_ge(cen_done, g + 1)
                if conv:
                    pe.wait_ge(ssum_done, g + 1)
                    pe.matmul(st[:, 0:GI], sh.group_w[:, :], ssum[:, :], start=True, stop=True).then_inc(var_done, 1)
                else:
                    pe.wait_ge(sq_done, g + 1)
                    pe.matmul(st[:, 0:T], mean_w[:, :], sq[:, :], start=True, stop=True).then_inc(var_done, 1)

            def project(g, j):
                if not exists(g):
                    return
                if conv or isinstance(g, int):
                    pe.wait_ge(xn_done, g + 1)
                    if due(2 * g):
                        pe.wait_ge(v_done, 2 * g)
                if conv:
                    if due(g - 1):
                        pe.wait_ge(res_done, g - 1)
                    if due(g):
                        pe.wait_ge(prob_done, g)
                    if due(g - 1):
                        pe.wait_ge(t_done, g - 1)
                    pe.matmul(pjq[:, 0:T], w[:, 0:C], xn[j][:, :], start=True, stop=True).then_inc(q_mm, 1)
                    if due(g):
                        pe.wait_ge(k_done, g)
                    pe.matmul(pjk[:, 0:T], w[:, C:2 * C], xn[j][:, :], start=True, stop=True).then_inc(k_mm, 1)
                for b in range(GI):
                    a = b * N
                    if conv:
                        last = pe.matmul(vps[0:N, b, :], xn[j][:, a:a + N], w[:, 2 * C:3 * C], start=True, stop=True,
                                         skip_group_check=True)
                    else:
                        last = pe.transpose(vps[0:N, b, :], xn[j][:, a:a + N], ident[:, :])
                    if b % 4 == 3:
                        last.then_inc(v_mm, 1)

            def scores(g, j):
                if not exists(g):
                    return
                pe.wait_ge(k_ready, g + 1)
                if conv:
                    pe.wait_ge(q_done, g + 1)
                if due(g):
                    pe.wait_ge(sub_done, g)
                q, k = (qt, kt) if conv else (xn[j], xn[j])
                for p in range(PAIRS):
                    for im, m in ((0, B1), (1, N)):
                        a = (2 * p + im) * N
                        last = pe.matmul(sps[B1 * im:B1 * im + m, p * N:(p + 1) * N], q[:, a:a + m], k[:, a:a + N],
                                         start=True, stop=True, skip_group_check=True)
                last.then_inc(s_mm, 1)

            def turn(g):
                if isinstance(g, int):
                    pe.wait_ge(prob_done, g + 1)
                    if due(g):
                        pe.wait_ge(t_done, g)
                for p in range(PAIRS):
                    last = pe.transpose(ptps[0:N, p * R:(p + 1) * R], pr[:, p * N:(p + 1) * N], ident[0:R, 0:R])
                last.then_inc(t_mm, 1)

            def values(g):
                pe.wait_ge(t_done, g + 1)
                pe.wait_ge(v_done, 2 * g + 2)
                if due(g):
                    pe.wait_ge(o_done if conv else res_done, g)
                for b in range(GI):
                    last = pe.matmul(ops_[:, b * N:(b + 1) * N], vt[:, b, :], pt[:, (b // 2) * R + B1 * (b % 2):(b // 2) * R + B1 * (b % 2) + N],
                                     start=True, stop=True, skip_group_check=True)
                last.then_inc(pv_mm, 1)

            def out(g):
                if not conv:
                    return
                pe.wait_ge(o_done, g + 1)
                pe.wait_ge(q_done, g + 2 if exists(g + 1) else NG)
                if due(g):
                    pe.wait_ge(res_done, g)
                pe.matmul(pjq[:, 0:T], w[:, 3 * C:4 * C], ot[:, :], start=True, stop=True).then_inc(out_mm, 1)

            mean(0, 0)
            var(0, 0)
            project(0, 0)
            mean(1, 1)
            scores(0, 0)
            var(1, 1)

            def body(g, j):
                mean(g + 2, j)
                project(g + 1, 1 - j)
                turn(g)
                scores(g + 1, 1 - j)
                values(g)
                var(g + 2, j)
                out(g)

            over_groups(pe, body)

        @block.vector
        def _(dve):
            if conv:
                dve.wait_ge(wloaded, 16 * len(loads))
                dve.wait_ge(bmm, 1)
                dve.tensor_tensor(b_use[:, 0:3], sps[:, 0:3], b_in[:, 0:3], ALU.add).then_inc(wready, 1)
                dve.tensor_scalar(w[:, 0:3 * C], w[:, 0:3 * C], b_in[:, 4:5], None, ALU.mult).then_inc(wready, 1)
                dve.wait_ge(bmm, 2)
                dve.tensor_tensor(b_use[:, 3:4], sps[:, 3:4], b_in[:, 3:4], ALU.add).then_inc(wready, 1)
                dve.tensor_scalar(b_use[:, 0:1], b_use[:, 0:1], C ** -0.5, None, ALU.mult).then_inc(wready, 1)

            def sums(g, j):
                if not exists(g) or not conv:
                    return
                if due(g):
                    dve.wait_ge(mean_done, g)
                dve.tensor_reduce(csum[:, :], images(X[:, cols(g)]), AX_X, ALU.add).then_inc(csum_done, 1)

            def centre(g, j):
                if not exists(g):
                    return
                dve.wait_ge(mean_done, g + 1)
                if due(g - 1):
                    dve.wait_ge(sq_done, g - 1)
                if due(g - 1):
                    dve.wait_ge(xn_done, g - 1)
                if conv:
                    dve.tensor_tensor(images(cen[j][:, :]), images(X[:, cols(g)]), st[:, 0:GI][:, :, None].to_broadcast([C, GI, N]),
                                      ALU.subtract).then_inc(cen_done, 1)
                else:
                    dve.tensor_tensor(cen[j][:, :], X[:, cols(g)], st[:, 0:T], ALU.subtract).then_inc(cen_done, 1)

            def squares(g, j):
                if not exists(g) or not conv:
                    return
                dve.wait_ge(sq_done, g + 1)
                if due(g):
                    dve.wait_ge(var_done, g)
                dve.tensor_reduce(ssum[:, :], images(sq[:, :]), AX_X, ALU.add).then_inc(ssum_done, 1)

            def norm(g, j):
                if not exists(g):
                    return
                dve.wait_ge(rs_done, g + 1)
                if due(2 * g - 2):
                    dve.wait_ge(v_mm, 2 * g - 2)
                if due(g - 1):
                    dve.wait_ge(s_mm, g - 1)
                if conv:
                    dve.tensor_tensor(images(xn[j][:, :]), images(cen[j][:, :]), rs[:, :][:, :, None].to_broadcast([C, GI, N]),
                                      ALU.mult).then_inc(xn_done, 1)
                else:
                    dve.tensor_tensor(xn[j][:, :], cen[j][:, :], rs[:, :], ALU.mult).then_inc(xn_done, 1)

            def v_out(g, j):
                if not exists(g):
                    return
                if due(g):
                    dve.wait_ge(vt_read, g)
                for half in range(2):
                    dve.wait_ge(v_mm, 2 * g + half + 1)
                    dve.tensor_copy(vt[:, 4 * half:4 * half + 4, :], vps[0:N, 4 * half:4 * half + 4, :]).then_inc(v_done, 1)

            def pairs(ap):
                return ap.rearrange("q (p k) -> q p k", k=N)

            def shift(g, j):
                if not exists(g):
                    return
                dve.wait_ge(s_mm, g + 1)
                if due(g):
                    dve.wait_ge(sub_done, g)
                dve.tensor_reduce(mx[:, :], pairs(sps[0:R, 0:PAIRS * N]), AX_X, ALU.max).then_inc(max_done, 1)
                dve.wait_ge(max_done, g + 1)
                if due(g):
                    dve.wait_ge(exp_done, g)
                dve.tensor_tensor(pairs(sc[:, :]), pairs(sps[0:R, 0:PAIRS * N]), mx[:, :][:, :, None].to_broadcast([R, PAIRS, N]),
                                  ALU.subtract).then_inc(sub_done, 1)

            def probs(g, j):
                if not exists(g):
                    return
                dve.wait_ge(exp_done, g + 1)
                if due(g):
                    dve.wait_ge(rec_done, g)
                dve.tensor_reduce(sm[:, :], pairs(pr[:, :]), AX_X, ALU.add).then_inc(sum_done, 1)
                dve.wait_ge(sum_done, g + 1)
                if due(g):
                    dve.wait_ge(prob_done, g)
                dve.reciprocal(rc[:, :], sm[:, :]).then_inc(rec_done, 1)
                dve.wait_ge(rec_done, g + 1)
                dve.tensor_tensor(pairs(pr[:, :]), pairs(pr[:, :]), rc[:, :][:, :, None].to_broadcast([R, PAIRS, N]),
                                  ALU.mult).then_inc(prob_done, 1)

            def residual(g):
                dve.wait_ge(final_mm, g + 1)
                if conv:
                    dve.scalar_tensor_tensor(out=X[:, cols(g)], in0=pjq[:, 0:T], scalar=b_use[:, 3:4], in1=X[:, cols(g)],
                                             op0=ALU.add, op1=ALU.add).then_inc(res_done, 1)
                else:
                    dve.tensor_tensor(X[:, cols(g)], ops_[:, 0:T], X[:, cols(g)], ALU.add).then_inc(res_done, 1)

            sums(0, 0)
            centre(0, 0)
            squares(0, 0)
            norm(0, 0)
            sums(1, 1)
            centre(1, 1)
            v_out(0, 0)
            squares(1, 1)
            shift(0, 0)
            norm(1, 1)
            probs(0, 0)
            sums(2, 0)

            def body(g, j):
                centre(g + 2, j)
                shift(g + 1, 1 - j)
                squares(g + 2, j)
                v_out(g + 1, 1 - j)
                probs(g + 1, 1 - j)
                norm(g + 2, j)
                residual(g)
                sums(g + 3, 1 - j)

            over_groups(dve, body, tail=4)
            dve.wait_ge(res_done, NG)

        @block.scalar
        def _(act):
            act.preload_act_table_set(EXP_SET)
            if conv:
                act.wait_ge(wready, 4)

            def square(g, j):
                if not exists(g):
                    return
                act.wait_ge(cen_done, g + 1)
                if due(g):
                    act.wait_ge(ssum_done if conv else var_done, g)
                act.activation(sq[:, :], cen[j][:, :], ACT.Square).then_inc(sq_done, 1)

            def rstd(g, j):
                if not exists(g):
                    return
                act.wait_ge(var_done, g + 1)
                if due(g):
                    act.wait_ge(xn_done, g)
                width = GI if conv else T
                eps = sh.eps6 if conv else sh.eps5
                act.activation(rs[:, :], st[:, 0:width], ACT.Ln, bias=eps[:, 0:1]).then_inc(ln_done, 1)
                act.wait_ge(ln_done, g + 1)
                act.activation(rs[:, :], rs[:, :], ACT.Exp, scale=-0.5).then_inc(rs_done, 1)

            def qk_out(g, j):
                if not exists(g) or not conv:
                    return
                act.wait_ge(q_mm, g + 1)
                if due(g):
                    act.wait_ge(s_mm, g)
                act.activation(qt[:, :], pjq[:, 0:T], ACT.Identity, bias=b_use[:, 0:1], scale=C ** -0.5).then_inc(q_done, 1)
                act.wait_ge(k_mm, g + 1)
                act.activation(kt[:, :], pjk[:, 0:T], ACT.Identity, bias=b_use[:, 1:2]).then_inc(k_done, 1)

            def expo(g, j):
                if not exists(g):
                    return
                act.wait_ge(sub_done, g + 1)
                if due(g):
                    act.wait_ge(t_mm, g)
                act.activation(pr[:, :], sc[:, :], ACT.Exp).then_inc(exp_done, 1)

            def turned(g):
                act.wait_ge(t_mm, g + 1)
                if due(g):
                    act.wait_ge(pv_mm, g)
                act.activation(pt[:, :], ptps[0:N, 0:PAIRS * R], ACT.Copy).then_inc(t_done, 1)

            def o_out(g):
                if not conv:
                    return
                act.wait_ge(pv_mm, g + 1)
                if due(g):
                    act.wait_ge(out_mm, g)
                act.activation(ot[:, :], ops_[:, 0:T], ACT.Copy).then_inc(o_done, 1)

            square(0, 0)
            rstd(0, 0)
            qk_out(0, 0)
            square(1, 1)
            expo(0, 0)
            rstd(1, 1)

            def body(g, j):
                square(g + 2, j)
                qk_out(g + 1, 1 - j)
                turned(g)
                expo(g + 1, 1 - j)
                o_out(g)
                rstd(g + 2, j)

            over_groups(act, body)


def gate_phase(nc, sh, kind, gates_dram):
    X, XN, ident, mean_w = sh.X, sh.XN, sh.ident, sh.mean_w
    wg, bg = (sh.wg2, sh.bg2) if kind == "g2" else (sh.wg3, sh.bg3)
    with ExitStack() as ctx:
        def sb(name, shape, dt=F32):
            return ctx.enter_context(nc.sbuf_tensor(f"{kind}_{name}", shape, dt))

        def ps(name, shape):
            return ctx.enter_context(nc.psum_tensor(f"{kind}_{name}", shape, F32))

        sem = ctx.enter_context(PhaseSemaphores(nc, kind))

        NT = T // TT
        mean_ps = [ps(f"mean{i}", [C, 512]) for i in range(2)]
        var_ps = [ps(f"var{i}", [C, 512]) for i in range(2)]
        log_ps = [ps(f"log{i}", [TT, 512]) for i in range(2)]
        gt_ps = [ps(f"gt{i}", [C, 512]) for i in range(2)]
        cen = [sb(f"cen{i}", [C, T]) for i in range(2)]
        sq = sb("sq", [C, T])
        rs = [sb(f"rs{i}", [C, T]) for i in range(2)]
        xn = [sb(f"xn{i}", [C, T]) for i in range(2)]
        lg = sb("lg", [TT, NT, EXPERTS])
        top = sb("top", [TT, NT, 8])
        idx = sb("idx", [TT, NT, 8], U32)
        idf = sb("idf", [TT, NT, 2])
        gap = [sb(f"gap{i}", [TT, NT]) for i in range(2)]
        ex = [sb(f"ex{i}", [TT, NT]) for i in range(2)]
        g1, g2, den = sb("g1", [TT, NT]), sb("g2", [TT, NT]), sb("den", [TT, NT])
        pick = [sb(f"pick{i}", [TT, NT, EXPERTS]) for i in range(2)]
        comb = [sb(f"comb{i}", [TT, NT, EXPERTS]) for i in range(2)]
        hi = [sb(f"hi{i}", [EXPERTS, T], F32R) for i in range(2)]
        lo = [sb(f"lo{i}", [EXPERTS, T]) for i in range(2)]

        mean_done, cen_done, sq_done, var_done = sem("mean"), sem("centred"), sem("squared"), sem("variance")
        ln_done, rs_done, xn_done, keep_done = sem("logvar"), sem("rstd"), sem("normed"), sem("kept")
        log_mm, exp_done, gt_mm, hi_done, gt_done = sem("logits"), sem("exped"), sem("turned"), sem("high"), sem("split")
        small = sem("small_steps")
        stored = [sem(f"stored{i}") for i in range(2)]
        STEPS = 11

        block = ctx.enter_context(nc.Block())

        @block.tensor
        def _(pe):
            def mean(g, j):
                if not exists(g):
                    return
                if due(g - 1):
                    pe.wait_ge(cen_done, g - 1)
                pe.matmul(mean_ps[j][:, 0:T], mean_w[:, :], X[:, cols(g)], start=True, stop=True).then_inc(mean_done, 1)

            def var(g, j):
                if not exists(g):
                    return
                pe.wait_ge(sq_done, g + 1)
                if due(g - 1):
                    pe.wait_ge(ln_done, g - 1)
                pe.matmul(var_ps[j][:, 0:T], mean_w[:, :], sq[:, :], start=True, stop=True).then_inc(var_done, 1)

            def logits(g, j):
                pe.wait_ge(xn_done, g + 1)
                if due((g - 1) * STEPS):
                    pe.wait_ge(small, (g - 1) * STEPS)
                for t in range(NT):
                    last = pe.matmul(log_ps[j][:, t * EXPERTS:(t + 1) * EXPERTS], xn[j][:, t * TT:(t + 1) * TT], wg[:, :],
                                     start=True, stop=True, skip_group_check=True)
                last.then_inc(log_mm, 1)

            def turn(g, j):
                if isinstance(g, int) and g < 0:
                    return
                pe.wait_ge(small, g * STEPS + STEPS)
                if due(g - 1):
                    pe.wait_ge(gt_done, g - 1)
                for t in range(NT):
                    last = pe.transpose(gt_ps[j][0:EXPERTS, t * TT:(t + 1) * TT], comb[j][:, t, :], ident[0:TT, 0:TT])
                last.then_inc(gt_mm, 1)

            mean(0, 0)
            mean(1, 1)
            var(0, 0)

            def body(g, j):
                mean(g + 2, j)
                logits(g, j)
                var(g + 1, 1 - j)
                turn(g - 1, 1 - j)

            over_groups(pe, body, head=4)
            turn(NG - 1, 1)

        @block.scalar
        def _(act):
            act.preload_act_table_set(EXP_SET)

            def square(g, j):
                if not exists(g):
                    return
                act.wait_ge(cen_done, g + 1)
                if due(g):
                    act.wait_ge(var_done, g)
                act.activation(sq[:, :], cen[j][:, :], ACT.Square).then_inc(sq_done, 1)

            def rstd(g, j):
                if not exists(g):
                    return
                act.wait_ge(var_done, g + 1)
                if due(g - 1):
                    act.wait_ge(xn_done, g - 1)
                act.activation(rs[j][:, :], var_ps[j][:, 0:T], ACT.Ln, bias=sh.eps5[:, 0:1]).then_inc(ln_done, 1)
                act.wait_ge(ln_done, g + 1)
                act.activation(rs[j][:, :], rs[j][:, :], ACT.Exp, scale=-0.5).then_inc(rs_done, 1)

            square(0, 0)
            rstd(0, 0)

            def body(g, j):
                square(g + 1, 1 - j)
                rstd(g + 1, 1 - j)
                act.wait_ge(xn_done, g + 1)
                act.activation(XN[:, cols(g)], xn[j][:, :], ACT.Copy).then_inc(keep_done, 1)
                act.wait_ge(small, g * STEPS + 4)
                act.activation(ex[j][:, :], gap[j][:, :], ACT.Exp).then_inc(exp_done, 1)

            over_groups(act, body)

        @block.vector
        def _(dve):
            def centre(g, j):
                if not exists(g):
                    return
                dve.wait_ge(mean_done, g + 1)
                if due(g - 1):
                    dve.wait_ge(sq_done, g - 1)
                if due(g - 1):
                    dve.wait_ge(xn_done, g - 1)
                dve.tensor_tensor(cen[j][:, :], X[:, cols(g)], mean_ps[j][:, 0:T], ALU.subtract).then_inc(cen_done, 1)

            def norm(g, j):
                if not exists(g):
                    return
                dve.wait_ge(rs_done, g + 1)
                if due(g - 1):
                    dve.wait_ge(log_mm, g - 1)
                if due(g - 1):
                    dve.wait_ge(keep_done, g - 1)
                dve.tensor_tensor(xn[j][:, :], cen[j][:, :], rs[j][:, :], ALU.mult).then_inc(xn_done, 1)

            def step(g, k, ins):
                ins.then_inc(small, 1)
                dve.wait_ge(small, g * STEPS + k)

            def choose(g, j):
                dve.wait_ge(log_mm, g + 1)
                step(g, 1, dve.tensor_tensor(lg[:, :, :], log_ps[j][:, 0:NT * EXPERTS].rearrange("q (t e) -> q t e", e=EXPERTS),
                                             bg[:, :][:, None, :].to_broadcast([TT, NT, EXPERTS]), ALU.add))
                centre(g + 2, j)
                for t in range(NT):
                    last = dve.max(top[:, t, :], lg[:, t, :])
                step(g, 2, last)
                split(g - 1, 1 - j)
                for t in range(NT):
                    last = dve.max_index(idx[:, t, :], top[:, t, :], lg[:, t, :])
                step(g, 3, last)
                step(g, 4, dve.tensor_tensor(gap[j][:, :], top[:, :, 1], top[:, :, 0], ALU.subtract))
                step(g, 5, dve.tensor_copy(idf[:, :, :], idx[:, :, 0:2]))
                iota = sh.iota8[:, :][:, None, :].to_broadcast([TT, NT, EXPERTS])
                dve.tensor_tensor(pick[0][:, :, :], iota, idf[:, :, 0:1].to_broadcast([TT, NT, EXPERTS]), ALU.is_equal)
                step(g, 6, dve.tensor_tensor(pick[1][:, :, :], iota, idf[:, :, 1:2].to_broadcast([TT, NT, EXPERTS]), ALU.is_equal))

            def weigh(g, j):
                def per_tile(a):
                    return a[:, :][:, :, None].to_broadcast([TT, NT, EXPERTS])

                dve.wait_ge(exp_done, g + 1)
                step(g, 7, dve.tensor_scalar(den[:, :], ex[j][:, :], 1.0, None, ALU.add))
                step(g, 8, dve.reciprocal(g1[:, :], den[:, :]))
                step(g, 9, dve.tensor_tensor(g2[:, :], g1[:, :], ex[j][:, :], ALU.mult))
                dve.tensor_tensor(pick[0][:, :, :], pick[0][:, :, :], per_tile(g1), ALU.mult)
                step(g, 10, dve.tensor_tensor(pick[1][:, :, :], pick[1][:, :, :], per_tile(g2), ALU.mult))
                if due(g - 1):
                    dve.wait_ge(gt_mm, g - 1)
                step(g, 11, dve.tensor_tensor(comb[j][:, :, :], pick[0][:, :, :], pick[1][:, :, :], ALU.add))

            def split(g, j):
                if isinstance(g, int) and g < 0:
                    return
                dve.wait_ge(gt_mm, g + 1)
                if due(16 * (g - j) if not isinstance(g, int) else 16 * 2 * (g // 2)):
                    dve.wait_ge(stored[j], 16 * (g - j) if not isinstance(g, int) else 16 * 2 * (g // 2))
                dve.tensor_copy(hi[j][:, :], gt_ps[j][0:EXPERTS, 0:T]).then_inc(hi_done, 1)
                dve.wait_ge(hi_done, g + 1)
                dve.tensor_tensor(lo[j][:, :], gt_ps[j][0:EXPERTS, 0:T], hi[j][:, :].bitcast(F32), ALU.subtract).then_inc(gt_done, 1)

            centre(0, 0)
            centre(1, 1)
            norm(0, 0)

            def body(g, j):
                norm(g + 1, 1 - j)
                choose(g, j)
                weigh(g, j)

            over_groups(dve, body, head=4)
            split(NG - 1, 1)

        @block.sync
        def _(sp):
            def store(g, j):
                sp.wait_ge(gt_done, g + 1)
                dst = gates_dram[g * 16:g * 16 + 8] if isinstance(g, int) else gates_dram[bass.ds(g * 16, 8)]
                sp.dma_start(dst, hi[j][:, :].bitcast(F32)).then_inc(stored[j], 16)
                dst = gates_dram[g * 16 + 8:g * 16 + 16] if isinstance(g, int) else gates_dram[bass.ds(g * 16 + 8, 8)]
                sp.dma_start(dst, lo[j][:, :]).then_inc(stored[j], 16)

            over_groups(sp, store)
            for j in range(2):
                sp.wait_ge(stored[j], 16 * NG)


def experts_phase(nc, sh, kind, gates_dram, w1, b1, w2, b2, func, out_dram):
    X, XN = sh.X, sh.XN
    F = w1.shape[1]
    NC = F // C
    PIECE = 512
    CP = PIECE // C
    NP = F // PIECE
    per = 4 if (F // EXPERTS) % C == 0 else 1
    LA = 3
    with ExitStack() as ctx:
        def sb(name, shape, dt=F32):
            return ctx.enter_context(nc.sbuf_tensor(f"{kind}_{name}", shape, dt))

        def ps(name, shape):
            return ctx.enter_context(nc.psum_tensor(f"{kind}_{name}", shape, F32))

        sem = ctx.enter_context(PhaseSemaphores(nc, kind))

        hps = [ps(f"hps{i}", [C, 512]) for i in range(4)]
        gps = [ps(f"gps{i}", [C, 512]) for i in range(2)]
        ops_ = [ps(f"ops{i}", [C, 512]) for i in range(2)]
        raw = [sb(f"raw{i}", [C, PIECE]) for i in range(2)]
        w1h, w1l = sb("w1h", [C, F], F32R), sb("w1l", [C, F], F32R)
        w2h, w2l = sb("w2h", [C, NC * C], F32R), sb("w2l", [C, NC * C], F32R)
        b1t = sb("b1t", [C, NC])
        sel = sb("sel", [16, (NC // per) * C], F32R)
        b2r = sb("b2r", [16, C])
        b2h, b2l = sb("b2h", [16, C], F32R), sb("b2l", [16, C], F32R)
        xh = [sb(f"xh{i}", [C, T], F32R) for i in range(2)]
        xl = [sb(f"xl{i}", [C, T], F32R) for i in range(2)]
        ct = [sb(f"ct{i}", [16, T], F32R) for i in range(2)]
        gs = [sb(f"gs{i}", [C, T]) for i in range(2)]
        h_all = sb("h", [C, 4 * T])
        act_h = [h_all[:, i * T:(i + 1) * T] for i in range(4)]
        selr = h_all[0:16, 0:(NC // per) * C]
        hh = [sb(f"hh{i}", [C, T], F32R) for i in range(4)]
        hl = [sb(f"hl{i}", [C, T], F32R) for i in range(4)]

        small_loaded, small_split = sem("small_loaded"), sem("small_split")
        raw_loaded = [sem(f"raw_loaded{i}") for i in range(2)]
        w_high, w_split = sem("w_high"), sem("w_split")
        ct_loaded = [sem(f"ct_loaded{i}") for i in range(2)]
        xh_done, x_split = sem("xh"), sem("x_split")
        g_mm, g_done, h_mm, h_done = sem("gate_mm"), sem("gate_out"), sem("hidden_mm"), sem("hidden_out")
        gated = [sem("gated_pool"), sem("gated_dve")]
        hh_done, h_split, o_mm, res_done, stored = sem("hh"), sem("h_split"), sem("out_mm"), sem("residual"), sem("stored")

        block = ctx.enter_context(nc.Block())

        def on_dve(k):
            return k % 4 == 3

        def pieces():
            return [(m, q) for q in range(NP) for m in range(2)]

        @block.sync
        def _(sp):
            sp.dma_start(b1t[:, :], b1).then_inc(small_loaded, 16)
            sp.dma_start(selr[:, :], sh.sel_dram[kind]).then_inc(small_loaded, 16)
            sp.dma_start(b2r[0:8, :], b2).then_inc(small_loaded, 16)
            sp.dma_start(b2r[8:16, :], b2).then_inc(small_loaded, 16)

            def load_piece(n):
                m, q = pieces()[n]
                if due(n - 1):
                    sp.wait_ge(w_split, n - 1)
                src = w1[:, q * PIECE:(q + 1) * PIECE] if m == 0 else w2[q * PIECE:(q + 1) * PIECE, :].rearrange("(k p) c -> p k c", p=C)
                dst = raw[n % 2][:, :] if m == 0 else raw[n % 2][:, :].rearrange("p (k c) -> p k c", c=C)
                sp.dma_start(dst, src).then_inc(raw_loaded[n % 2], 16)

            def load_gates(g, j):
                if not exists(g):
                    return
                if due((g - 1) * NC):
                    sp.wait_ge(o_mm, (g - 1) * NC)
                src = gates_dram[g * 16:g * 16 + 16] if isinstance(g, int) else gates_dram[bass.ds(g * 16, 16)]
                sp.dma_start(ct[j][:, :].bitcast(F32), src).then_inc(ct_loaded[j], 16)

            load_gates(0, 0)
            load_gates(1, 1)
            for n in range(2 * NP):
                load_piece(n)

            def body(g, j):
                load_gates(g + 2, j)

            over_groups(sp, body)
            if out_dram is not None:
                sp.wait_ge(stored, 16 * NG)

        @block.tensor
        def _(pe):
            def gate(g, j, k):
                if k % per or not exists(g):
                    return
                q = k // per
                n = g * (NC // per) + q
                if q == 0:
                    if due(16 * (g // 2 + 1) if isinstance(g, int) else (g - j) * 8 + 16):
                        pe.wait_ge(ct_loaded[j], 16 * (g // 2 + 1) if isinstance(g, int) else (g - j) * 8 + 16)
                    if isinstance(g, int) and g == 0:
                        pe.wait_ge(small_split, 4)
                if due(n - 1):
                    pe.wait_ge(g_done, n - 1)
                pe.matmul(gps[q % 2][:, 0:T], sel[:, q * C:(q + 1) * C], ct[j][:, :], start=True, stop=True).then_inc(g_mm, 1)

            def hidden(g, j, k):
                if not exists(g):
                    return
                n = g * NC + k
                if k == 0:
                    pe.wait_ge(x_split, g + 1)
                if isinstance(g, int) and g == 0:
                    if due(2 * (k // CP) + 1):
                        pe.wait_ge(w_split, 2 * (k // CP) + 1)
                if due(n - 3):
                    pe.wait_ge(h_done, n - 3)
                c = slice(k * C, (k + 1) * C)
                pe.matmul(hps[k % 4][:, 0:T], w1h[:, c], xh[j][:, :], start=True, stop=False)
                pe.matmul(hps[k % 4][:, 0:T], w1h[:, c], xl[j][:, :], start=False, stop=False)
                pe.matmul(hps[k % 4][:, 0:T], w1l[:, c], xh[j][:, :], start=False, stop=True).then_inc(h_mm, 1)

            def output(g, j, k):
                n = g * NC + k
                if k == 0:
                    if due(g - 1):
                        pe.wait_ge(res_done, g - 1)
                    pe.matmul(ops_[j][:, 0:T], b2h[:, :], ct[j][:, :], start=True, stop=False)
                    pe.matmul(ops_[j][:, 0:T], b2l[:, :], ct[j][:, :], start=False, stop=False)
                if isinstance(g, int) and g == 0:
                    if due(2 * (k // CP) + 2):
                        pe.wait_ge(w_split, 2 * (k // CP) + 2)
                pe.wait_ge(h_split, n + 1)
                c = slice(k * C, (k + 1) * C)
                pe.matmul(ops_[j][:, 0:T], w2h[:, c], hh[k % 4][:, :], start=False, stop=False)
                pe.matmul(ops_[j][:, 0:T], w2h[:, c], hl[k % 4][:, :], start=False, stop=False)
                pe.matmul(ops_[j][:, 0:T], w2l[:, c], hh[k % 4][:, :], start=False, stop=(k == NC - 1)).then_inc(o_mm, 1)

            def ahead(g, j, k):
                if k + LA < NC:
                    gate(g, j, k + LA)
                    hidden(g, j, k + LA)
                else:
                    gate(g + 1, 1 - j, k + LA - NC)
                    hidden(g + 1, 1 - j, k + LA - NC)

            for k in range(LA):
                gate(0, 0, k)
                hidden(0, 0, k)

            def body(g, j):
                for k in range(NC):
                    ahead(g, j, k)
                    output(g, j, k)

            over_groups(pe, body)

        @block.scalar
        def _(act):
            act.wait_ge(small_loaded, 64)
            act.wait_ge(small_split, 1)

            def store(g):
                if out_dram is None or (isinstance(g, int) and g < 0):
                    return
                act.wait_ge(res_done, g + 1)
                dst = out_dram[g * GI:(g + 1) * GI] if isinstance(g, int) else out_dram[bass.ds(g * GI, GI)]
                act.dma_start(dst.rearrange("b c n -> c b n"), X[:, cols(g)].rearrange("c (b n) -> c b n", n=N)).then_inc(stored, 16)

            def body(g, j):
                for k in range(NC):
                    n = g * NC + k
                    if k == NC // 2:
                        store(g - 1)
                    if k % per == 0:
                        q = g * (NC // per) + k // per
                        act.wait_ge(g_mm, q + 1)
                        if due(n - per):
                            act.wait_ge(hh_done, n - per)
                        act.activation(gs[(k // per) % 2][:, :], gps[(k // per) % 2][:, 0:T], ACT.Copy).then_inc(g_done, 1)
                    act.wait_ge(h_mm, n + 1)
                    if due(n - 3):
                        act.wait_ge(h_split, n - 3)
                    act.activation(act_h[k % 4][:, :], hps[k % 4][:, 0:T], func, bias=b1t[:, k:k + 1]).then_inc(h_done, 1)

            over_groups(act, body)
            store(NG - 1)

        @block.gpsimd
        def _(pool):
            def body(g, j):
                for k in range(NC):
                    if on_dve(k):
                        continue
                    n = g * NC + k
                    if due(g * (NC // per) + k // per + 1):
                        pool.wait_ge(g_done, g * (NC // per) + k // per + 1)
                    pool.wait_ge(h_done, n + 1)
                    pool.tensor_tensor(act_h[k % 4][:, :], act_h[k % 4][:, :], gs[(k // per) % 2][:, :], ALU.mult).then_inc(gated[0], 1)

            over_groups(pool, body)

        @block.vector
        def _(dve):
            def split_piece(n):
                m, q = pieces()[n]
                high, low = (w1h, w1l) if m == 0 else (w2h, w2l)
                c = slice(q * PIECE, (q + 1) * PIECE)
                dve.wait_ge(raw_loaded[n % 2], 16 * (n // 2 + 1))
                dve.tensor_copy(high[:, c], raw[n % 2][:, :]).then_inc(w_high, 1)
                dve.wait_ge(w_high, n + 1)
                dve.tensor_tensor(low[:, c], raw[n % 2][:, :], high[:, c].bitcast(F32), ALU.subtract).then_inc(w_split, 1)

            def split_x(g, j):
                if not exists(g):
                    return
                if due((g - 1) * NC):
                    dve.wait_ge(h_mm, (g - 1) * NC)
                dve.tensor_copy(xh[j][:, :], XN[:, cols(g)]).then_inc(xh_done, 1)
                dve.wait_ge(xh_done, g + 1)
                dve.tensor_tensor(xl[j][:, :], XN[:, cols(g)], xh[j][:, :].bitcast(F32), ALU.subtract).then_inc(x_split, 1)

            def residual(g, j):
                if isinstance(g, int) and g < 0:
                    return
                dve.wait_ge(o_mm, (g + 1) * NC)
                dve.tensor_tensor(X[:, cols(g)], ops_[j][:, 0:T], X[:, cols(g)], ALU.add).then_inc(res_done, 1)

            dve.wait_ge(small_loaded, 64)
            dve.tensor_copy(sel[:, :], selr[:, :]).then_inc(small_split, 1)
            dve.tensor_copy(b2h[:, :], b2r[:, :]).then_inc(small_split, 1)
            dve.wait_ge(small_split, 2)
            dve.tensor_tensor(b2l[:, :], b2r[:, :], b2h[:, :].bitcast(F32), ALU.subtract).then_inc(small_split, 2)
            split_x(0, 0)
            split_piece(0)
            split_piece(1)

            def body(g, j):
                first = isinstance(g, int) and g == 0
                for k in range(NC):
                    n = g * NC + k
                    if first and k % CP == 0 and k // CP + 1 < NP:
                        split_piece(2 * (k // CP) + 2)
                        split_piece(2 * (k // CP) + 3)
                    if on_dve(k):
                        dve.wait_ge(h_done, n + 1)
                        if due(g * (NC // per) + k // per + 1):
                            dve.wait_ge(g_done, g * (NC // per) + k // per + 1)
                        dve.tensor_tensor(act_h[k % 4][:, :], act_h[k % 4][:, :], gs[(k // per) % 2][:, :], ALU.mult).then_inc(gated[1], 1)
                        if due(g * (NC // 4) + k // 4 + 1):
                            dve.wait_ge(gated[1], g * (NC // 4) + k // 4 + 1)
                    else:
                        if due(g * (NC - NC // 4) + k - k // 4 + 1):
                            dve.wait_ge(gated[0], g * (NC - NC // 4) + k - k // 4 + 1)
                    if due(n - 3):
                        dve.wait_ge(o_mm, n - 3)
                    dve.tensor_copy(hh[k % 4][:, :], act_h[k % 4][:, :]).then_inc(hh_done, 1)
                    dve.wait_ge(hh_done, n + 1)
                    dve.tensor_tensor(hl[k % 4][:, :], act_h[k % 4][:, :], hh[k % 4][:, :].bitcast(F32), ALU.subtract).then_inc(h_split, 1)
                    if k == NC // 2:
                        split_x(g + 1, 1 - j)
                    if k == 1:
                        residual(g - 1, 1 - j)

            over_groups(dve, body)
            residual(NG - 1, 1)


def build(nc, a, out):
    sh = Shared()
    gates = nc.dram_tensor("gates", (NG * 16, T), F32, kind="Internal").ap()
    with ExitStack() as ctx:
        def sb(name, shape):
            return ctx.enter_context(nc.sbuf_tensor(name, shape, F32))

        sh.X = sb("X", [C, IMAGES * N])
        sh.ident, sh.mean_w, sh.group_w = sb("ident", [C, C]), sb("mean_w", [C, C]), sb("group_w", [C, C])
        sh.kmask, sh.vmask = sb("kmask", [C, HEADS]), sb("vmask", [S2, C])
        sh.iota8, sh.pos = sb("iota8", [TT, EXPERTS]), sb("pos", [C, N])
        sh.eps5, sh.eps6 = sb("eps5", [C, 1]), sb("eps6", [C, 1])
        sh.wg2, sh.wg3 = sb("wg2", [C, EXPERTS]), sb("wg3", [C, EXPERTS])
        sh.bg2, sh.bg3 = sb("bg2", [TT, EXPERTS]), sb("bg3", [TT, EXPERTS])
        sh.sel_dram = {"moe2": a["c_sel2"], "moe3": a["c_sel3"]}
        load_constants(nc, [
            (sh.ident[:, :], a["c_ident"]), (sh.mean_w[:, :], a["c_mean_w"]), (sh.group_w[:, :], a["c_group_w"]),
            (sh.kmask[:, :], a["c_kmask"]), (sh.vmask[:, :], a["c_vmask"]), (sh.iota8[:, :], a["c_iota8"]),
            (sh.pos[:, :], a["c_pos"]), (sh.eps5[:, :], a["c_eps5"]), (sh.eps6[:, :], a["c_eps6"]),
            (sh.wg2[:, :], a["L2_ffn_Wg"]), (sh.wg3[:, :], a["L3_ffn_Wr"]),
            (sh.bg2[:, :], a["L2_ffn_bg"].to_broadcast([TT, EXPERTS])),
            (sh.bg3[:, :], a["L3_ffn_br"].to_broadcast([TT, EXPERTS]))])
        heads_phase(nc, sh, a, "window", a["x"])
        if PHASES >= 2:
            single_phase(nc, sh, a, "conv")
        if PHASES >= 3:
            single_phase(nc, sh, a, "token")
        if PHASES >= 4:
            with nc.sbuf_tensor("XN2", [C, IMAGES * N], F32) as sh.XN:
                gate_phase(nc, sh, "g2", gates)
                experts_phase(nc, sh, "moe2", gates, a["L2_ffn_W1"], a["L2_ffn_b1"], a["L2_ffn_W2"], a["L2_ffn_b2"], ACT.Gelu, None)
        if PHASES >= 5:
            heads_phase(nc, sh, a, "scales", None)
        if PHASES >= 6:
            with nc.sbuf_tensor("XN3", [C, IMAGES * N], F32) as sh.XN:
                gate_phase(nc, sh, "g3", gates)
                experts_phase(nc, sh, "moe3", gates, a["L3_ffn_W1"], a["L3_ffn_b1"], a["L3_ffn_W2"], a["L3_ffn_b2"],
                              ACT.Gelu_apprx_tanh, out)
        else:
            with nc.semaphore("dbg") as dbg, nc.Block() as block:
                @block.sync
                def _(sp):
                    sp.dma_start(out.rearrange("b c n -> c b n"), sh.X[:, :].rearrange("c (b n) -> c b n", n=N)).then_inc(dbg, 16)
                    sp.wait_ge(dbg, 16)


PHASES = 6


def constants():
    import numpy as np
    f = np.float32
    c = np.arange(C)
    one = {"c_ident": np.eye(C, dtype=f), "c_mean_w": np.full((C, C), 1.0 / C, f)}
    one["c_group_w"] = np.where(c[:, None] // 4 == c[None, :] // 4, f(1.0 / (4 * N)), f(0)).astype(f)
    one["c_kmask"] = (c[:, None] // HD == np.arange(HEADS)[None, :]).astype(f)
    one["c_vmask"] = (np.arange(S2)[:, None] // N == c[None, :] // HD % 2).astype(f)
    one["c_iota8"] = np.tile(np.arange(EXPERTS, dtype=f), (TT, 1))
    inv = f(10000.0) ** (np.arange(0, C, 2, dtype=f) / f(C))
    ang = np.arange(N, dtype=f)[:, None] / inv
    one["c_pos"] = np.ascontiguousarray(np.concatenate([np.sin(ang), np.cos(ang)], -1).T.astype(f))
    one["c_eps5"], one["c_eps6"] = np.full((C, 1), 1e-5, f), np.full((C, 1), 1e-6, f)
    one["c_zeros"] = np.zeros((B1 - N, HEADS * N), f)
    for name, width, spread in (("c_sel2", 192, 1536), ("c_sel3", 128, 1024)):
        row = (np.arange(EXPERTS)[:, None] == np.arange(spread)[None, :] // width).astype(f)
        one[name] = np.concatenate([row, row])
    return one


def layout(inputs):
    import numpy as np
    a = {k: np.asarray(v) for k, v in inputs.items()}
    a["x"] = a["x"].reshape(IMAGES, C, N)
    side = 7
    rev = a.pop("L0_conv_rel_table")[::-1, ::-1, :]
    win = [rev[i:i + side, j:j + side].transpose(2, 0, 1) for i in reversed(range(side)) for j in reversed(range(side))]
    a["L0_conv_rel_bias"] = np.stack(win).reshape(N, HEADS * N)
    for n in ("wq", "wk", "wv", "wp"):
        a[f"L1_conv_{n}"] = a[f"L1_conv_{n}"].T
    for n, v in list(a.items()):
        if v.ndim == 1 and v.shape[0] == C:
            a[n] = v.reshape(C, 1)
    a["L2_ffn_bg"], a["L3_ffn_br"] = a["L2_ffn_bg"].reshape(1, EXPERTS), a["L3_ffn_br"].reshape(1, EXPERTS)
    a["L3_ffn_Wr"] = a["L3_ffn_Wr"].T
    for n in ("L2_ffn", "L3_ffn"):
        a[f"{n}_W1"] = a[f"{n}_W1"].transpose(1, 0, 2).reshape(C, -1)
        a[f"{n}_W2"] = a[f"{n}_W2"].reshape(-1, C)
        a[f"{n}_b1"] = a[f"{n}_b1"].reshape(-1, C).T
    return {k: np.ascontiguousarray(v) for k, v in a.items()}


def kernel(**inputs):
    import concourse.bacc as _bacc
    from concourse.bass_utils import run_bass_kernel_spmd as _run

    nc = _bacc.Bacc("TRN2", target_bir_lowering=False, num_devices=1)
    arrays = {f"in_{k}": v for k, v in {**layout(inputs), **constants()}.items()}
    args = {k[3:]: nc.dram_tensor(k, v.shape, F32, kind="ExternalInput").ap() for k, v in arrays.items()}
    out = nc.dram_tensor("out_y", (IMAGES, C, N), F32, kind="ExternalOutput").ap()
    build(nc, args, out)
    r = _run(nc, [arrays], core_ids=[0])
    return r.results[0]["out_y"].reshape(IMAGES, C, 7, 7)
```

```python
from contextlib import ExitStack

import concourse.bass as bass
from concourse import mybir

F32 = mybir.dt.float32
F32R = mybir.dt.float32r
U32 = mybir.dt.uint32
ALU = mybir.AluOpType
ACT = mybir.ActivationFunctionType
AX_X = mybir.AxisListType.X

C = 128
N = 49
IMAGES = 256
GI = 8
T = GI * N
NG = IMAGES // GI
PAIRS = GI // 2
HEADS = 8
HD = 16
HP = HEADS // 2
S2 = 2 * N
B1 = 64
R = B1 + N
EXPERTS = 8
TT = T // 4
EXP_SET = "natural_log_exp_and_others"


def due(count):
    assert isinstance(count, int) or count.min_val > 0, "a wait that could be for nothing"
    return not isinstance(count, int) or count > 0


def over_groups(eng, body, head=2, tail=2):
    for g in range(head):
        body(g, g % 2)
    with eng.Fori(head // 2, (NG - tail) // 2) as i:
        for j in range(2):
            body(i * 2 + j, j)
    for g in range(NG - tail, NG):
        body(g, g % 2)


def exists(g):
    return not isinstance(g, int) or g < NG


def cols(g):
    return bass.ds(g * T, T) if not isinstance(g, int) else slice(g * T, g * T + T)


def bcast(ap, shape):
    return ap.to_broadcast(shape)


class PhaseSemaphores:

    def __init__(self, nc, prefix):
        self.nc, self.prefix, self.held = nc, prefix, []

    def __enter__(self):
        return self

    def __call__(self, name):
        self.held.append(self.nc.alloc_semaphore(name=f"{self.prefix}_{name}"))
        return self.held[-1]

    def __exit__(self, *error):
        if error[0] is None:
            self.nc.clear_and_free_semaphores(self.held)
            self.nc.all_engine_barrier()


class Shared:
    pass


def load_constants(nc, loads):
    with PhaseSemaphores(nc, "constants") as sem, nc.Block() as block:
        loaded = sem("loaded")

        @block.sync
        def _(sp):
            for dst, src in loads:
                sp.dma_start(dst, src).then_inc(loaded, 16)
            sp.wait_ge(loaded, 16 * len(loads))


def heads_phase(nc, sh, a, kind, x_in):
    window = kind == "window"
    scales = [1] if window else [1, 2, 4]
    widths = [len(range(0, N, s)) for s in scales]
    offs = [HEADS * sum(widths[:i]) for i in range(len(scales))]
    SW = HEADS * sum(widths)
    NS = len(scales)
    X, ident, mean_w = sh.X, sh.ident, sh.mean_w
    with ExitStack() as ctx:
        def sb(name, shape, dt=F32):
            return ctx.enter_context(nc.sbuf_tensor(f"{kind}_{name}", shape, dt))

        sem = ctx.enter_context(PhaseSemaphores(nc, kind))

        pj = [ctx.enter_context(nc.psum_tensor(f"{kind}_pj{i}", [C, 512], F32)) for i in range(2)]
        vps = ctx.enter_context(nc.psum_tensor(f"{kind}_vps", [C, 4, C], F32))
        sps = [ctx.enter_context(nc.psum_tensor(f"{kind}_sps{i}", [C, 512], F32)) for i in range(2)]
        ptps = ctx.enter_context(nc.psum_tensor(f"{kind}_ptps", [C, 512], F32))
        ops_ = [ctx.enter_context(nc.psum_tensor(f"{kind}_ops{i}", [C, 512], F32)) for i in range(2)]

        w = sb("w", [C, 3 * C])
        wo = sb("wo", [C, C]) if window else None
        b_in = sb("b_in", [C, 8])
        b_use = sb("b_use", [C, 4])
        cen = [sb(f"cen{i}", [C, T]) for i in range(2)]
        sq = sb("sq", [C, T])
        rs = sb("rs", [C, T])
        xn = [sb(f"xn{i}", [C, T]) for i in range(2)]
        twice = sb("twice", [C, GI, 2, N])
        qt = [sb(f"qt{i}", [C, T]) for i in range(2)]
        kt = sb("kt", [C, T])
        kbd = [sb(f"kbd{i}", [C, GI, HEADS, N]) for i in range(2)]
        vbd = [sb(f"vbd{i}", [S2, GI, C]) for i in range(2)]
        sc = [sb(f"sc{i}", [R, SW]) for i in range(2)]
        pr = [sb(f"pr{i}", [R, SW]) for i in range(4)]
        mx = [sb(f"mx{i}", [R, NS * HEADS]) for i in range(2)]
        sm = [sb(f"sm{i}", [R, NS * HEADS]) for i in range(2)]
        rc = [sb(f"rc{i}", [R, NS * HEADS]) for i in range(2)]
        pt = [sb(f"pt{i}", [S2, HP * R]) for i in range(2)]
        ot = sb("ot", [C, T])
        relb = sb("relb", [R, HEADS * N]) if window else None

        if window:
            loads = [(w[:, :], a["L0_conv_w_qkv"]), (wo[:, :], a["L0_conv_w_out"]), (b_in[:, 3:4], a["L0_conv_b_out"]),
                     (b_in[:, 4:5], a["L0_conv_gamma"]), (b_in[:, 5:6], a["L0_conv_beta"]), (relb[0:N, :], a["L0_conv_rel_bias"]),
                     (relb[N:B1, :], a["c_zeros"]), (relb[B1:R, :], a["L0_conv_rel_bias"])]
        else:
            loads = [(w[:, 0:C], a["L3_attn_Wq"]), (w[:, C:2 * C], a["L3_attn_Wk"]), (w[:, 2 * C:3 * C], a["L3_attn_Wv"]),
                     (b_in[:, 0:1], a["L3_attn_bq"]), (b_in[:, 1:2], a["L3_attn_bk"]), (b_in[:, 2:3], a["L3_attn_bv"])]
        wloaded, wready, bmm = sem("weights_loaded"), sem("weights_ready"), sem("bias_products")
        x_loaded = [sem(f"x_loaded{i}") for i in range(2)]
        mean_done, cen_done, sq_done, var_done = sem("mean"), sem("centred"), sem("squared"), sem("variance")
        ln_done, rs_done, xn_done, pos_done = sem("logvar"), sem("rstd"), sem("normed"), sem("positioned")
        q_mm, k_mm, q_done, k_done, kbd_done = sem("q_mm"), sem("k_mm"), sem("q_out"), sem("k_out"), sem("kbd")
        v_mm, v_done, twice_done = sem("v_mm"), sem("v_out"), sem("twice")
        s_mm, add_done, max_done, sub_done, exp_done = sem("s_mm"), sem("biased"), sem("maxed"), sem("shifted"), sem("exped")
        sum_done, rec_done, prob_done, merged = sem("summed"), sem("recip"), sem("probs"), sem("merged")
        t_mm, t_done, pv_mm, o_done, out_mm, res_done = sem("t_mm"), sem("t_out"), sem("pv_mm"), sem("o_out"), sem("out_mm"), sem("residual")
        mid_done = sem("merged_mid")

        xn_ready = xn_done if window else pos_done
        final_probs = prob_done if window else merged

        block = ctx.enter_context(nc.Block())

        @block.sync
        def _(sp):
            for dst, src in loads:
                sp.dma_start(dst, src).then_inc(wloaded, 16)
            if window:
                def load(g, j):
                    if due(16 * ((g - j) // 2) if isinstance(g, int) else (g - j) * 8):
                        sp.wait_ge(x_loaded[j], 16 * ((g - j) // 2) if isinstance(g, int) else (g - j) * 8)
                    dst = X[:, cols(g)].rearrange("c (b n) -> c b n", n=N)
                    src = x_in[bass.ds(g * GI, GI)] if not isinstance(g, int) else x_in[g * GI:(g + 1) * GI]
                    sp.dma_start(dst, src.rearrange("b c n -> c b n")).then_inc(x_loaded[j], 16)

                over_groups(sp, load)
                for j in range(2):
                    sp.wait_ge(x_loaded[j], 16 * (NG // 2))

        def landed(eng, g, j):
            if window:
                if due(16 * (g // 2 + 1) if isinstance(g, int) else (g - j) * 8 + 16):
                    eng.wait_ge(x_loaded[j], 16 * (g // 2 + 1) if isinstance(g, int) else (g - j) * 8 + 16)

        @block.tensor
        def _(pe):
            pe.wait_ge(wloaded, 16 * len(loads))
            if window:
                for m in range(3):
                    last = pe.matmul(ops_[0][:, m:m + 1], w[:, m * C:(m + 1) * C], b_in[:, 5:6], start=(m == 0), stop=True,
                                     skip_group_check=True)
                last.then_inc(bmm, 1)
                pe.wait_ge(wready, 2)
                pe.matmul(ops_[0][:, 3:4], wo[:, :], b_use[:, 2:3], start=True, stop=True,
                          skip_group_check=True).then_inc(bmm, 1)
            pe.wait_ge(wready, 3)

            def mean(g, j):
                if not exists(g):
                    return
                landed(pe, g, j)
                if due(g):
                    pe.wait_ge(q_done, g)
                pe.matmul(pj[0][:, 0:T], mean_w[:, :], X[:, cols(g)], start=True, stop=True).then_inc(mean_done, 1)

            def var(g, j):
                if not exists(g):
                    return
                pe.wait_ge(sq_done, g + 1)
                pe.wait_ge(cen_done, g + 1)
                pe.matmul(pj[0][:, 0:T], mean_w[:, :], sq[:, :], start=True, stop=True).then_inc(var_done, 1)

            def qk(g, j):
                if not exists(g):
                    return
                pe.wait_ge(xn_ready, g + 1)
                pe.wait_ge(ln_done, g + 1)
                pe.matmul(pj[0][:, 0:T], w[:, 0:C], xn[j][:, :], start=True, stop=True).then_inc(q_mm, 1)
                if due((g - 2) if window else 0):
                    pe.wait_ge(res_done, (g - 2) if window else 0)
                if due(g):
                    pe.wait_ge(k_done, g)
                pe.matmul(pj[1][:, 0:T], w[:, C:2 * C], xn[j][:, :], start=True, stop=True).then_inc(k_mm, 1)

            def val(g, j, half):
                if not exists(g):
                    return
                pe.wait_ge(v_done, g * 2 + half)
                pe.wait_ge(twice_done, g + 1)
                for b in range(4):
                    last = pe.matmul(vps[0:S2, b, :], twice[:, 4 * half + b].rearrange("c r n -> c (r n)"), w[:, 2 * C:3 * C],
                                     start=True, stop=True, skip_group_check=True)
                last.then_inc(v_mm, 1)

            def scores(g, j, p):
                if not exists(g):
                    return
                n = g * PAIRS + p
                pe.wait_ge(q_done, g + 1)
                pe.wait_ge(kbd_done, n + 1)
                if due(n - 1):
                    pe.wait_ge((add_done if window else sub_done), n - 1)
                for im, m in ((0, B1), (1, N)):
                    a = (2 * p + im) * N
                    last = pe.matmul(sps[p % 2][B1 * im:B1 * im + m, 0:HEADS * N], qt[j][:, a:a + m],
                                     kbd[j][:, 2 * p + im].rearrange("c h n -> c (h n)"), start=True, stop=True)
                last.then_inc(s_mm, 1)

            def turn(n, p):
                if isinstance(n, int) and n < 0:
                    return
                pe.wait_ge(final_probs, n + 1)
                if due(n):
                    pe.wait_ge(t_done, n)
                for hp in range(HP):
                    last = pe.transpose(ptps[0:S2, hp * R:(hp + 1) * R], pr[p][:, hp * S2:(hp + 1) * S2], ident[0:R, 0:R])
                last.then_inc(t_mm, 1)

            def values(g, n, j, p):
                if isinstance(n, int) and n < 0:
                    return
                pe.wait_ge(t_done, n + 1)
                pe.wait_ge(v_done, g * 2 + 1 + p // 2)
                if p == 0:
                    if due(g - 1):
                        pe.wait_ge(o_done, g - 1)
                for im in range(2):
                    a = (2 * p + im) * N
                    for hp in range(HP):
                        last = pe.matmul(ops_[j][32 * hp:32 * hp + 32, a:a + N], vbd[j][:, 2 * p + im, 32 * hp:32 * hp + 32],
                                         pt[p % 2][:, hp * R + B1 * im:hp * R + B1 * im + N], start=True, stop=True,
                                         skip_group_check=True)
                last.then_inc(pv_mm, 1)

            def out(g):
                if not window or (isinstance(g, int) and g < 0):
                    return
                pe.wait_ge(o_done, g + 1)
                pe.wait_ge(k_done, g + 3 if exists(g + 2) else NG)
                if due(g):
                    pe.wait_ge(res_done, g)
                pe.matmul(pj[1][:, 0:T], wo[:, :], ot[:, :], start=True, stop=True).then_inc(out_mm, 1)

            mean(0, 0)
            var(0, 0)
            qk(0, 0)
            val(0, 0, 0)
            val(0, 0, 1)
            mean(1, 1)
            var(1, 1)
            scores(0, 0, 0)
            scores(0, 0, 1)

            def body(g, j):
                for p in range(PAIRS):
                    n = g * PAIRS + p
                    if p < 2:
                        scores(g, j, p + 2)
                    else:
                        scores(g + 1, 1 - j, p - 2)
                    if p < 2:
                        if not (isinstance(g, int) and g == 0):
                            values(g - 1, n - 2, 1 - j, p + 2)
                    else:
                        values(g, n - 2, j, p - 2)
                    if p == 0:
                        qk(g + 1, 1 - j)
                    if p == 1:
                        val(g + 1, 1 - j, 0)
                    if p == 2:
                        val(g + 1, 1 - j, 1)
                        mean(g + 2, j)
                        out(g - 1)
                    if p == 3:
                        var(g + 2, j)
                    turn(n - 1, (p - 1) % 4)

            over_groups(pe, body)
            last_n = NG * PAIRS
            values(NG - 1, last_n - 2, 1, 2)
            turn(last_n - 1, 3)
            values(NG - 1, last_n - 1, 1, 3)
            out(NG - 1)

        @block.vector
        def _(dve):
            dve.wait_ge(wloaded, 16 * len(loads))
            if window:
                dve.wait_ge(bmm, 1)
                dve.tensor_copy(b_use[:, 0:3], ops_[0][:, 0:3]).then_inc(wready, 1)
                dve.tensor_scalar(w[:, :], w[:, :], b_in[:, 4:5], None, ALU.mult).then_inc(wready, 1)
                dve.wait_ge(bmm, 2)
                dve.tensor_tensor(b_use[:, 3:4], ops_[0][:, 3:4], b_in[:, 3:4], ALU.add).then_inc(wready, 1)
                dve.tensor_scalar(b_use[:, 0:1], b_use[:, 0:1], HD ** -0.5, None, ALU.mult).then_inc(wready, 1)
            else:
                dve.tensor_copy(b_use[:, 1:3], b_in[:, 1:3]).then_inc(wready, 3)
                dve.tensor_scalar(b_use[:, 0:1], b_in[:, 0:1], HD ** -0.5, None, ALU.mult).then_inc(wready, 1)

            def centre(g, j):
                if not exists(g):
                    return
                dve.wait_ge(mean_done, g + 1)
                landed(dve, g, j)
                if due(g - 1):
                    dve.wait_ge(sq_done, g - 1)
                if due(g - 1):
                    dve.wait_ge(xn_done, g - 1)
                dve.tensor_tensor(cen[j][:, :], X[:, cols(g)], pj[0][:, 0:T], ALU.subtract).then_inc(cen_done, 1)

            def norm(g, j):
                if not exists(g):
                    return
                dve.wait_ge(rs_done, g + 1)
                if due(g * 2 - 2):
                    dve.wait_ge(v_mm, g * 2 - 2)
                if due(g - 1):
                    dve.wait_ge(twice_done, g - 1)
                if not window:
                    if due(g - 1):
                        dve.wait_ge(pos_done, g - 1)
                dve.tensor_tensor(xn[j][:, :], cen[j][:, :], rs[:, :], ALU.mult).then_inc(xn_done, 1)
                if not window:
                    dve.wait_ge(xn_done, g + 1)
                    v = xn[j][:, :].rearrange("c (b n) -> c b n", n=N)
                    dve.tensor_tensor(v, v, sh.pos[:, :][:, None, :].to_broadcast([C, GI, N]), ALU.add).then_inc(pos_done, 1)

            def val(g, j, half):
                if not exists(g):
                    return
                dve.wait_ge(v_mm, g * 2 + half + 1)
                if due(g * PAIRS - 2 * PAIRS + 2 * half + 2):
                    dve.wait_ge(pv_mm, g * PAIRS - 2 * PAIRS + 2 * half + 2)
                dve.tensor_tensor(vbd[j][:, 4 * half:4 * half + 4, :], vps[0:S2, :, :],
                                  sh.vmask[:, :][:, None, :].to_broadcast([S2, 4, C]), ALU.mult).then_inc(v_done, 1)

            def sview(ap, i):
                return ap[:, offs[i]:offs[i] + HEADS * widths[i]].rearrange("q (h k) -> q h k", h=HEADS)

            def picked(ap, i):
                return ap[0:R, 0:HEADS * N].rearrange("q (h k) -> q h k", h=HEADS)[:, :, 0:N:scales[i]]

            def shift(g, j, p):
                if not exists(g):
                    return
                n = g * PAIRS + p
                k = p % 2
                dve.wait_ge(s_mm, n + 1)
                if due(n - 1):
                    dve.wait_ge(exp_done, n - 1)
                if window:
                    dve.tensor_tensor(sc[k][:, :], sps[k][0:R, 0:HEADS * N], relb[:, :], ALU.add).then_inc(add_done, 1)
                    dve.wait_ge(add_done, n + 1)
                    if due(n - 1):
                        dve.wait_ge(sub_done, n - 1)
                    dve.tensor_reduce(mx[k][:, :], sview(sc[k], 0), AX_X, ALU.max).then_inc(max_done, 1)
                    dve.wait_ge(max_done, n + 1)
                    v = sview(sc[k], 0)
                    dve.tensor_tensor(v, v, mx[k][:, :][:, :, None].to_broadcast([R, HEADS, N]), ALU.subtract).then_inc(sub_done, 1)
                else:
                    if due(n - 1):
                        dve.wait_ge(sub_done, n - 1)
                    for i in range(NS):
                        last = dve.tensor_reduce(mx[k][:, i * HEADS:(i + 1) * HEADS], picked(sps[k], i), AX_X, ALU.max)
                    last.then_inc(max_done, 1)
                    dve.wait_ge(max_done, n + 1)
                    for i in range(NS):
                        last = dve.tensor_tensor(sview(sc[k], i), picked(sps[k], i),
                                                 mx[k][:, i * HEADS:(i + 1) * HEADS][:, :, None].to_broadcast([R, HEADS, widths[i]]),
                                                 ALU.subtract)
                    last.then_inc(sub_done, 1)

            def total(n, p):
                k = p % 2
                dve.wait_ge(exp_done, n + 1)
                if due(n - 1):
                    dve.wait_ge(rec_done, n - 1)
                for i in range(NS):
                    last = dve.tensor_reduce(sm[k][:, i * HEADS:(i + 1) * HEADS], sview(pr[p], i), AX_X, ALU.add)
                last.then_inc(sum_done, 1)
                dve.wait_ge(sum_done, n + 1)
                if due(n - 1):
                    dve.wait_ge(prob_done, n - 1)
                dve.reciprocal(rc[k][:, :], sm[k][:, :]).then_inc(rec_done, 1)

            def outputs(g, j):
                if isinstance(g, int) and g < 0:
                    return
                if window:
                    dve.wait_ge(out_mm, g + 1)
                    dve.scalar_tensor_tensor(out=X[:, cols(g)], in0=pj[1][:, 0:T], scalar=b_use[:, 3:4], in1=X[:, cols(g)],
                                             op0=ALU.add, op1=ALU.add).then_inc(res_done, 1)
                else:
                    dve.wait_ge(o_done, g + 1)
                    dve.tensor_tensor(X[:, cols(g)], X[:, cols(g)], ot[:, :], ALU.add).then_inc(res_done, 1)

            centre(0, 0)
            norm(0, 0)
            val(0, 0, 0)
            val(0, 0, 1)
            centre(1, 1)
            norm(1, 1)
            shift(0, 0, 0)

            def body(g, j):
                for p in range(PAIRS):
                    if p < 3:
                        shift(g, j, p + 1)
                    else:
                        shift(g + 1, 1 - j, 0)
                    total(g * PAIRS + p, p)
                    if p == 1:
                        val(g + 1, 1 - j, 0)
                    if p == 2:
                        val(g + 1, 1 - j, 1)
                        centre(g + 2, j)
                        outputs(g - 1, 1 - j)
                    if p == 3:
                        norm(g + 2, j)

            over_groups(dve, body)
            outputs(NG - 1, 1)
            dve.wait_ge(res_done, NG)

        @block.gpsimd
        def _(pool):
            def keys(g, j, p):
                if not exists(g):
                    return
                pool.wait_ge(k_done, g + 1)
                if due(g * PAIRS - 2 * PAIRS + p + 1):
                    pool.wait_ge(s_mm, g * PAIRS - 2 * PAIRS + p + 1)
                a = 2 * p * N
                pool.tensor_tensor(kbd[j][:, 2 * p:2 * p + 2],
                                   kt[:, a:a + S2].rearrange("c (b n) -> c b n", n=N)[:, :, None, :].to_broadcast([C, 2, HEADS, N]),
                                   sh.kmask[:, :][:, None, :, None].to_broadcast([C, 2, HEADS, N]), ALU.mult).then_inc(kbd_done, 1)

            def probs(n, p):
                pool.wait_ge(rec_done, n + 1)
                for i in range(NS):
                    v = pr[p][:, offs[i]:offs[i] + HEADS * widths[i]].rearrange("q (h k) -> q h k", h=HEADS)
                    last = pool.tensor_tensor(v, v, rc[p % 2][:, i * HEADS:(i + 1) * HEADS][:, :, None].to_broadcast([R, HEADS, widths[i]]),
                                              ALU.mult)
                last.then_inc(prob_done, 1)
                if not window:
                    full = pr[p][:, 0:HEADS * N].rearrange("q (h k) -> q h k", h=HEADS)
                    for i, (s_wait, s_sig) in ((1, (prob_done, mid_done)), (2, (mid_done, merged))):
                        pool.wait_ge(s_wait, n + 1)
                        v = pr[p][:, offs[i]:offs[i] + HEADS * widths[i]].rearrange("q (h k) -> q h k", h=HEADS)
                        d = full[:, :, 0:N:scales[i]]
                        pool.tensor_tensor(d, d, v, ALU.add).then_inc(s_sig, 1)

            for p in range(PAIRS):
                keys(0, 0, p)

            def body(g, j):
                for p in range(PAIRS):
                    probs(g * PAIRS + p, p)
                    keys(g + 1, 1 - j, p)

            over_groups(pool, body)

        @block.scalar
        def _(act):
            act.preload_act_table_set(EXP_SET)
            act.wait_ge(wready, 4)

            def square(g, j):
                if not exists(g):
                    return
                act.wait_ge(cen_done, g + 1)
                if due(g):
                    act.wait_ge(var_done, g)
                act.activation(sq[:, :], cen[j][:, :], ACT.Square).then_inc(sq_done, 1)

            def rstd(g, j):
                if not exists(g):
                    return
                act.wait_ge(var_done, g + 1)
                if due(g):
                    act.wait_ge(xn_done, g)
                act.activation(rs[:, :], pj[0][:, 0:T], ACT.Ln, bias=sh.eps5[:, 0:1]).then_inc(ln_done, 1)
                act.wait_ge(ln_done, g + 1)
                act.activation(rs[:, :], rs[:, :], ACT.Exp, scale=-0.5).then_inc(rs_done, 1)

            def q_out(g, j):
                if not exists(g):
                    return
                act.wait_ge(q_mm, g + 1)
                if due(g * PAIRS - PAIRS):
                    act.wait_ge(s_mm, g * PAIRS - PAIRS)
                act.activation(qt[j][:, :], pj[0][:, 0:T], ACT.Identity, bias=b_use[:, 0:1], scale=HD ** -0.5).then_inc(q_done, 1)
                act.wait_ge(k_mm, g + 1)
                if due(g * PAIRS):
                    act.wait_ge(kbd_done, g * PAIRS)
                act.activation(kt[:, :], pj[1][:, 0:T], ACT.Identity, bias=b_use[:, 1:2]).then_inc(k_done, 1)
                if due(g * 2):
                    act.wait_ge(v_mm, g * 2)
                act.activation(twice[:, :, :, :], xn[j][:, :].rearrange("c (b n) -> c b n", n=N)[:, :, None, :].to_broadcast([C, GI, 2, N]),
                               ACT.Copy).then_inc(twice_done, 1)

            def expo(g, j, p):
                if not exists(g):
                    return
                n = g * PAIRS + p
                act.wait_ge(sub_done, n + 1)
                if due(n - 3):
                    act.wait_ge(t_mm, n - 3)
                act.activation(pr[p][:, :], sc[p % 2][:, :], ACT.Exp).then_inc(exp_done, 1)

            def turned(n, p):
                if isinstance(n, int) and n < 0:
                    return
                act.wait_ge(t_mm, n + 1)
                if due(n - 1):
                    act.wait_ge(pv_mm, n - 1)
                act.activation(pt[p % 2][:, :], ptps[0:S2, 0:HP * R], ACT.Copy).then_inc(t_done, 1)

            def o_out(g, j):
                if isinstance(g, int) and g < 0:
                    return
                act.wait_ge(pv_mm, (g + 1) * PAIRS)
                if window:
                    if due(g):
                        act.wait_ge(out_mm, g)
                    act.activation(ot[:, :], ops_[j][:, 0:T], ACT.Copy).then_inc(o_done, 1)
                else:
                    if due(g):
                        act.wait_ge(res_done, g)
                    act.activation(ot[:, :], ops_[j][:, 0:T], ACT.Identity, bias=b_use[:, 2:3],
                                   scale=1.0 / NS).then_inc(o_done, 1)

            square(0, 0)
            rstd(0, 0)
            q_out(0, 0)
            square(1, 1)
            rstd(1, 1)
            expo(0, 0, 0)

            def body(g, j):
                for p in range(PAIRS):
                    n = g * PAIRS + p
                    if p == 0:
                        q_out(g + 1, 1 - j)
                    if p < 3:
                        expo(g, j, p + 1)
                    else:
                        expo(g + 1, 1 - j, 0)
                    turned(n - 1, (p - 1) % 4)
                    if p == 1:
                        o_out(g - 1, 1 - j)
                    if p == 2:
                        square(g + 2, j)
                    if p == 3:
                        rstd(g + 2, j)

            over_groups(act, body)
            turned(NG * PAIRS - 1, 3)
            o_out(NG - 1, 1)


def over_steps(eng, body, lead, lag=1):
    for s in range(-lead, 4):
        body(Step(s, s))
    with eng.Fori(1, (NG - lead) // 4) as i:
        for j in range(4):
            body(Step(i * 4 + j, j))
    for s in range((NG - lead) // 4 * 4, NG + lag):
        body(Step(s, s))


class Step:

    def __init__(self, g, remainder):
        self.g, self.r = g, remainder % 4

    def ahead(self, k):
        return Step(self.g + k, self.r + k)

    def exists(self):
        return not isinstance(self.g, int) or 0 <= self.g < NG


def single_phase(nc, sh, a, kind):
    conv = kind == "conv"
    X, ident = sh.X, sh.ident
    LEAD = 4
    with ExitStack() as ctx:
        def sb(name, shape, dt=F32):
            return ctx.enter_context(nc.sbuf_tensor(f"{kind}_{name}", shape, dt))

        def ps(name, shape):
            return ctx.enter_context(nc.psum_tensor(f"{kind}_{name}", shape, F32))

        sem = ctx.enter_context(PhaseSemaphores(nc, kind))

        if conv:
            st, pjq, pjk = ps("st", [C, 512]), ps("pjq", [C, 512]), ps("pjk", [C, 512])
        else:
            cps = [ps(f"cen{i}", [C, 512]) for i in range(2)]
            st = ps("st", [C, 512])
        vps = ps("vps", [C, 4, C])
        sps, ptps, ops_ = ps("sps", [C, 512]), ps("ptps", [C, 512]), ps("ops", [C, 2, 512])
        if conv:
            w = sb("w", [C, 4 * C])
            b_in = sb("b_in", [C, 6])
            b_use = sb("b_use", [C, 4])
            csum, ssum = sb("csum", [C, GI]), sb("ssum", [C, GI])
            cen = [sb(f"cen{i}", [C, T]) for i in range(2)]
            qt, kt, ot = sb("qt", [C, T]), sb("kt", [C, T]), sb("ot", [C, T])
            loads = [(w[:, i * C:(i + 1) * C], a[f"L1_conv_{n}"]) for i, n in enumerate(("wq", "wk", "wv", "wp"))]
            loads += [(b_in[:, i:i + 1], a[f"L1_conv_{n}"]) for i, n in enumerate(("bq", "bk", "bv", "bp", "gn_scale", "gn_bias"))]
        sq = sb("sq", [C, T])
        rs = sb("rs", [C, GI if conv else T])
        xn = [sb(f"xn{i}", [C, GI, B1]) for i in range(2)]
        vt = [sb(f"vt{i}", [R, 4, C]) for i in range(4)]
        sc = sb("sc", [R, PAIRS, N])
        pr = [sb(f"pr{i}", [R, PAIRS, B1]) for i in range(2)]
        mx, sm = sb("mx", [R, PAIRS]), sb("sm", [R, PAIRS])
        rc = [sb(f"rc{i}", [R, PAIRS]) for i in range(2)]
        pt = [sb(f"pt{i}", [C, 2 * R]) for i in range(2)]

        wloaded, wready, bmm, zeroed = sem("weights_loaded"), sem("weights_ready"), sem("bias_products"), sem("zeroed")
        csum_done, mean_done, cen_done, sq_done, ssum_done = sem("csum"), sem("mean"), sem("centred"), sem("squared"), sem("ssum")
        var_done, ln_done, rs_done, xn_done = sem("variance"), sem("logvar"), sem("rstd"), sem("normed")
        q_mm, k_mm, q_done, k_done, v_mm, v_done = sem("q_mm"), sem("k_mm"), sem("q_out"), sem("k_out"), sem("v_mm"), sem("v_out")
        s_mm, max_done, sub_done, exp_done = sem("s_mm"), sem("maxed"), sem("shifted"), sem("exped")
        sum_done, rec_done, prob_done = sem("summed"), sem("recip"), sem("probs")
        t_mm, t_done, pv_mm, o_done, out_mm, res_done = sem("t_mm"), sem("t_out"), sem("pv_mm"), sem("o_out"), sem("out_mm"), sem("residual")

        block = ctx.enter_context(nc.Block())

        def images(ap):
            return ap.rearrange("c (b n) -> c b n", n=N)

        def mrn(ap):
            return ap.rearrange("c (m r n) -> c r m n", r=2, n=N)

        if conv:
            @block.sync
            def _(sp):
                for dst, src in loads:
                    sp.dma_start(dst, src).then_inc(wloaded, 16)

        @block.tensor
        def _(pe):
            if conv:
                pe.wait_ge(wloaded, 16 * len(loads))
                for m in range(3):
                    last = pe.matmul(sps[:, m:m + 1], w[:, m * C:(m + 1) * C], b_in[:, 5:6], start=(m == 0), stop=True,
                                     skip_group_check=True)
                last.then_inc(bmm, 1)
                pe.wait_ge(wready, 2)
                pe.matmul(sps[:, 3:4], w[:, 3 * C:4 * C], b_use[:, 2:3], start=True, stop=True,
                          skip_group_check=True).then_inc(bmm, 1)
                pe.wait_ge(wready, 3)
            pe.wait_ge(zeroed, 4)

            def mean(at):
                g = at.g
                if not at.exists():
                    return
                if conv:
                    if due(g - 1):
                        pe.wait_ge(ln_done, g - 1)
                    pe.wait_ge(csum_done, g + 1)
                    pe.matmul(st[:, 0:GI], sh.group_w[:, :], csum[:, :], start=True, stop=True).then_inc(mean_done, 1)
                else:
                    if due(g - 1):
                        pe.wait_ge(xn_done, g - 1)
                    pe.matmul(cps[at.r % 2][:, 0:T], sh.centre_w[:, :], X[:, cols(g)], start=True, stop=True).then_inc(mean_done, 1)

            def var(at):
                g = at.g
                if not at.exists():
                    return
                if conv:
                    pe.wait_ge(cen_done, g + 2 if at.ahead(1).exists() else NG)
                    pe.wait_ge(ssum_done, g + 1)
                    pe.matmul(st[:, 0:GI], sh.group_w[:, :], ssum[:, :], start=True, stop=True).then_inc(var_done, 1)
                else:
                    pe.wait_ge(sq_done, g + 1)
                    if due(g):
                        pe.wait_ge(ln_done, g)
                    pe.matmul(st[:, 0:T], sh.mean_w[:, :], sq[:, :], start=True, stop=True).then_inc(var_done, 1)

            def queries(at):
                g = at.g
                if not at.exists() or not conv:
                    return
                x = xn[at.r % 2][:, :, 0:N]
                pe.wait_ge(xn_done, g + 1)
                if due(g - 3):
                    pe.wait_ge(res_done, g - 3)
                if due(g):
                    pe.wait_ge(q_done, g)
                pe.matmul(pjq[:, 0:T], w[:, 0:C], x, start=True, stop=True).then_inc(q_mm, 1)
                if due(g):
                    pe.wait_ge(k_done, g)
                pe.matmul(pjk[:, 0:T], w[:, C:2 * C], x, start=True, stop=True).then_inc(k_mm, 1)

            def tokens(at):
                g = at.g
                if not at.exists():
                    return
                x = xn[at.r % 2]
                pe.wait_ge(xn_done, g + 1)
                if due(g):
                    pe.wait_ge(v_done, g)
                for mq in range(4):
                    if conv:
                        for r, m in ((0, B1), (1, N)):
                            last = pe.matmul(vps[B1 * r:B1 * r + m, mq, :], x[:, 2 * mq + r, 0:m], w[:, 2 * C:3 * C],
                                             start=True, stop=True, skip_group_check=True)
                    else:
                        last = pe.transpose(vps[:, mq, :], x[:, 2 * mq:2 * mq + 2, :].rearrange("c b n -> c (b n)"), ident[:, :])
                last.then_inc(v_mm, 1)

            def scores(at):
                g = at.g
                if not at.exists():
                    return
                if conv:
                    pe.wait_ge(k_done, g + 1)
                else:
                    pe.wait_ge(xn_done, g + 1)
                if due(g):
                    pe.wait_ge(sub_done, g)
                for p in range(PAIRS):
                    for m, rows in ((0, B1), (1, N)):
                        b = 4 * m + p
                        if conv:
                            q, k = qt[:, b * N:b * N + rows], kt[:, b * N:b * N + N]
                        else:
                            q, k = xn[at.r % 2][:, b, 0:rows], xn[at.r % 2][:, b, 0:N]
                        last = pe.matmul(sps[B1 * m:B1 * m + rows, p * N:(p + 1) * N], q, k, start=True, stop=True,
                                         skip_group_check=True)
                last.then_inc(s_mm, 1)

            def turn(at):
                g = at.g
                if not at.exists():
                    return
                pe.wait_ge(prob_done, g + 1)
                if due(g):
                    pe.wait_ge(t_done, g)
                for q in range(2):
                    last = pe.transpose(ptps[:, q * R:(q + 1) * R], pr[at.r % 2][:, 2 * q:2 * q + 2, :].rearrange("t p k -> t (p k)"),
                                        ident[0:R, 0:R])
                last.then_inc(t_mm, 1)

            def values(at):
                g = at.g
                if not at.exists():
                    return
                pe.wait_ge(t_done, g + 1)
                pe.wait_ge(v_done, g + 1)
                if due(g):
                    pe.wait_ge(o_done if conv else res_done, g)
                for m in range(2):
                    for q in range(2):
                        for r in range(2):
                            rows = slice(B1 * r, B1 * r + N)
                            last = pe.matmul(ops_[:, r, (2 * m + q) * N:(2 * m + q + 1) * N], vt[at.r][rows, 2 * m + q, :],
                                             pt[at.r % 2][rows, q * R + B1 * m:q * R + B1 * m + N],
                                             start=True, stop=True, skip_group_check=True)
                last.then_inc(pv_mm, 1)

            def out(at):
                g = at.g
                if not at.exists() or not conv:
                    return
                pe.wait_ge(o_done, g + 1)
                pe.wait_ge(q_done, g + 4 if at.ahead(3).exists() else NG)
                if due(g):
                    pe.wait_ge(res_done, g)
                pe.matmul(pjq[:, 0:T], w[:, 3 * C:4 * C], ot[:, :], start=True, stop=True).then_inc(out_mm, 1)

            def body(s):
                scores(s.ahead(1))
                values(s.ahead(-1))
                turn(s)
                mean(s.ahead(4))
                queries(s.ahead(2))
                tokens(s.ahead(2))
                var(s.ahead(3))
                out(s.ahead(-1))

            over_steps(pe, body, LEAD)

        @block.vector
        def _(dve):
            for i in range(2):
                dve.memset(xn[i][:, :, :], 0.0).then_inc(zeroed, 1)
                dve.memset(pr[i][:, :, :], 0.0).then_inc(zeroed, 1)
            dve.wait_ge(zeroed, 4)
            if conv:
                dve.wait_ge(wloaded, 16 * len(loads))
                dve.wait_ge(bmm, 1)
                dve.tensor_tensor(b_use[:, 0:3], sps[:, 0:3], b_in[:, 0:3], ALU.add).then_inc(wready, 1)
                dve.tensor_scalar(w[:, 0:3 * C], w[:, 0:3 * C], b_in[:, 4:5], None, ALU.mult).then_inc(wready, 1)
                dve.wait_ge(bmm, 2)
                dve.tensor_tensor(b_use[:, 3:4], sps[:, 3:4], b_in[:, 3:4], ALU.add).then_inc(wready, 1)
                dve.tensor_scalar(b_use[:, 0:1], b_use[:, 0:1], C ** -0.5, None, ALU.mult).then_inc(wready, 1)

            def sums(at):
                g = at.g
                if not at.exists() or not conv:
                    return
                if due(g):
                    dve.wait_ge(mean_done, g)
                dve.tensor_reduce(csum[:, :], images(X[:, cols(g)]), AX_X, ALU.add).then_inc(csum_done, 1)

            def centre(at):
                g = at.g
                if not at.exists() or not conv:
                    return
                dve.wait_ge(mean_done, g + 1)
                if due(g - 1):
                    dve.wait_ge(sq_done, g - 1)
                    dve.wait_ge(xn_done, g - 1)
                dve.tensor_tensor(images(cen[at.r % 2][:, :]), images(X[:, cols(g)]), st[:, 0:GI][:, :, None].to_broadcast([C, GI, N]),
                                  ALU.subtract).then_inc(cen_done, 1)

            def squares(at):
                g = at.g
                if not at.exists() or not conv:
                    return
                dve.wait_ge(sq_done, g + 1)
                if due(g):
                    dve.wait_ge(var_done, g)
                dve.tensor_reduce(ssum[:, :], images(sq[:, :]), AX_X, ALU.add).then_inc(ssum_done, 1)

            def norm(at):
                g, x = at.g, xn[at.r % 2][:, :, 0:N]
                if not at.exists():
                    return
                dve.wait_ge(rs_done, g + 1)
                if due(g - 1):
                    dve.wait_ge(v_mm, g - 1)
                    dve.wait_ge(k_mm if conv else s_mm, g - 1)
                if conv:
                    dve.tensor_tensor(x, images(cen[at.r % 2][:, :]), rs[:, :][:, :, None].to_broadcast([C, GI, N]),
                                      ALU.mult).then_inc(xn_done, 1)
                else:
                    dve.tensor_tensor(x, images(cps[at.r % 2][:, 0:T]), images(rs[:, :]), ALU.mult).then_inc(xn_done, 1)

            def v_out(at):
                g = at.g
                if not at.exists():
                    return
                dve.wait_ge(v_mm, g + 1)
                if due(g - 3):
                    dve.wait_ge(pv_mm, g - 3)
                dve.tensor_copy(vt[at.r][:, :, :], vps[0:R, :, :]).then_inc(v_done, 1)

            def shift(at):
                g = at.g
                if not at.exists():
                    return
                s3 = sps[0:R, 0:PAIRS * N].rearrange("t (p k) -> t p k", k=N)
                dve.wait_ge(s_mm, g + 1)
                if due(g):
                    dve.wait_ge(sub_done, g)
                dve.tensor_reduce(mx[:, :], s3, AX_X, ALU.max).then_inc(max_done, 1)
                dve.wait_ge(max_done, g + 1)
                if due(g):
                    dve.wait_ge(exp_done, g)
                dve.tensor_tensor(sc[:, :, :], s3, mx[:, :][:, :, None].to_broadcast([R, PAIRS, N]), ALU.subtract).then_inc(sub_done, 1)

            def total(at):
                g = at.g
                if not at.exists():
                    return
                dve.wait_ge(exp_done, g + 1)
                if due(g):
                    dve.wait_ge(rec_done, g)
                dve.tensor_reduce(sm[:, :], pr[at.r % 2][:, :, 0:N], AX_X, ALU.add).then_inc(sum_done, 1)
                dve.wait_ge(sum_done, g + 1)
                if due(g - 1):
                    dve.wait_ge(prob_done, g - 1)
                dve.reciprocal(rc[at.r % 2][:, :], sm[:, :]).then_inc(rec_done, 1)

            def residual(at):
                g = at.g
                if not at.exists():
                    return
                dve.wait_ge(out_mm if conv else pv_mm, g + 1)
                if conv:
                    dve.scalar_tensor_tensor(out=X[:, cols(g)], in0=pjq[:, 0:T], scalar=b_use[:, 3:4], in1=X[:, cols(g)],
                                             op0=ALU.add, op1=ALU.add).then_inc(res_done, 1)
                else:
                    dve.tensor_tensor(mrn(X[:, cols(g)]), ops_[:, :, 0:4 * N].rearrange("c r (m n) -> c r m n", n=N),
                                      mrn(X[:, cols(g)]), ALU.add).then_inc(res_done, 1)

            def body(s):
                sums(s.ahead(4))
                shift(s.ahead(1))
                squares(s.ahead(3))
                centre(s.ahead(4))
                if not conv:
                    residual(s.ahead(-1))
                v_out(s.ahead(2))
                total(s.ahead(1))
                norm(s.ahead(3))
                if conv:
                    residual(s.ahead(-1))

            over_steps(dve, body, LEAD)
            dve.wait_ge(res_done, NG)

        @block.gpsimd
        def _(pool):
            def body(s):
                at = s.ahead(1)
                if not at.exists():
                    return
                p = pr[at.r % 2][:, :, 0:N]
                pool.wait_ge(rec_done, at.g + 1)
                pool.tensor_tensor(p, p, rc[at.r % 2][:, :][:, :, None].to_broadcast([R, PAIRS, N]), ALU.mult).then_inc(prob_done, 1)

            over_steps(pool, body, LEAD)

        @block.scalar
        def _(act):
            act.preload_act_table_set(EXP_SET)
            act.wait_ge(zeroed, 4)
            if conv:
                act.wait_ge(wready, 4)

            def square(at):
                g = at.g
                if not at.exists():
                    return
                act.wait_ge(cen_done if conv else mean_done, g + 1)
                if due(g):
                    act.wait_ge(ssum_done if conv else var_done, g)
                src = cen[at.r % 2][:, :] if conv else cps[at.r % 2][:, 0:T]
                act.activation(sq[:, :], src, ACT.Square).then_inc(sq_done, 1)

            def rstd(at):
                g = at.g
                if not at.exists():
                    return
                width, eps = (GI, sh.eps6) if conv else (T, sh.eps5)
                act.wait_ge(var_done, g + 1)
                if due(g):
                    act.wait_ge(xn_done, g)
                act.activation(rs[:, :], st[:, 0:width], ACT.Ln, bias=eps[:, 0:1]).then_inc(ln_done, 1)
                act.wait_ge(ln_done, g + 1)
                act.activation(rs[:, :], rs[:, :], ACT.Exp, scale=-0.5).then_inc(rs_done, 1)

            def qk_out(at):
                g = at.g
                if not at.exists() or not conv:
                    return
                act.wait_ge(q_mm, g + 1)
                if due(g):
                    act.wait_ge(s_mm, g)
                act.activation(qt[:, :], pjq[:, 0:T], ACT.Identity, bias=b_use[:, 0:1], scale=C ** -0.5).then_inc(q_done, 1)
                act.wait_ge(k_mm, g + 1)
                act.activation(kt[:, :], pjk[:, 0:T], ACT.Identity, bias=b_use[:, 1:2]).then_inc(k_done, 1)

            def expo(at):
                g = at.g
                if not at.exists():
                    return
                act.wait_ge(sub_done, g + 1)
                if due(g - 1):
                    act.wait_ge(t_mm, g - 1)
                act.activation(pr[at.r % 2][:, :, 0:N], sc[:, :, :], ACT.Exp).then_inc(exp_done, 1)

            def turned(at):
                g = at.g
                if not at.exists():
                    return
                act.wait_ge(t_mm, g + 1)
                if due(g - 1):
                    act.wait_ge(pv_mm, g - 1)
                act.activation(pt[at.r % 2][:, :], ptps[:, 0:2 * R], ACT.Copy).then_inc(t_done, 1)

            def o_out(at):
                g = at.g
                if not at.exists() or not conv:
                    return
                act.wait_ge(pv_mm, g + 1)
                if due(g):
                    act.wait_ge(out_mm, g)
                act.activation(mrn(ot[:, :]), ops_[:, :, 0:4 * N].rearrange("c r (m n) -> c r m n", n=N), ACT.Copy).then_inc(o_done, 1)

            def body(s):
                o_out(s.ahead(-1))
                expo(s.ahead(1))
                turned(s)
                square(s.ahead(4))
                qk_out(s.ahead(2))
                rstd(s.ahead(3))

            over_steps(act, body, LEAD)


def gate_phase(nc, sh, kind, gates_dram):
    X, XN, ident, mean_w = sh.X, sh.XN, sh.ident, sh.mean_w
    wg, bg = (sh.wg2, sh.bg2) if kind == "g2" else (sh.wg3, sh.bg3)
    with ExitStack() as ctx:
        def sb(name, shape, dt=F32):
            return ctx.enter_context(nc.sbuf_tensor(f"{kind}_{name}", shape, dt))

        def ps(name, shape):
            return ctx.enter_context(nc.psum_tensor(f"{kind}_{name}", shape, F32))

        sem = ctx.enter_context(PhaseSemaphores(nc, kind))

        NT = T // TT
        mean_ps = [ps(f"mean{i}", [C, 512]) for i in range(2)]
        var_ps = [ps(f"var{i}", [C, 512]) for i in range(2)]
        log_ps = [ps(f"log{i}", [TT, 512]) for i in range(2)]
        gt_ps = [ps(f"gt{i}", [C, 512]) for i in range(2)]
        cen = [sb(f"cen{i}", [C, T]) for i in range(2)]
        sq = sb("sq", [C, T])
        rs = [sb(f"rs{i}", [C, T]) for i in range(2)]
        xn = [sb(f"xn{i}", [C, T]) for i in range(2)]
        lg = sb("lg", [TT, NT, EXPERTS])
        top = sb("top", [TT, NT, 8])
        idx = sb("idx", [TT, NT, 8], U32)
        idf = sb("idf", [TT, NT, 2])
        gap = [sb(f"gap{i}", [TT, NT]) for i in range(2)]
        ex = [sb(f"ex{i}", [TT, NT]) for i in range(2)]
        g1, g2, den = sb("g1", [TT, NT]), sb("g2", [TT, NT]), sb("den", [TT, NT])
        pick = [sb(f"pick{i}", [TT, NT, EXPERTS]) for i in range(2)]
        comb = [sb(f"comb{i}", [TT, NT, EXPERTS]) for i in range(2)]
        hi = [sb(f"hi{i}", [EXPERTS, T], F32R) for i in range(2)]
        lo = [sb(f"lo{i}", [EXPERTS, T]) for i in range(2)]

        mean_done, cen_done, sq_done, var_done = sem("mean"), sem("centred"), sem("squared"), sem("variance")
        ln_done, rs_done, xn_done, keep_done = sem("logvar"), sem("rstd"), sem("normed"), sem("kept")
        log_mm, exp_done, gt_mm, hi_done, gt_done = sem("logits"), sem("exped"), sem("turned"), sem("high"), sem("split")
        small = sem("small_steps")
        stored = [sem(f"stored{i}") for i in range(2)]
        STEPS = 11

        block = ctx.enter_context(nc.Block())

        @block.tensor
        def _(pe):
            def mean(g, j):
                if not exists(g):
                    return
                if due(g - 1):
                    pe.wait_ge(cen_done, g - 1)
                pe.matmul(mean_ps[j][:, 0:T], mean_w[:, :], X[:, cols(g)], start=True, stop=True).then_inc(mean_done, 1)

            def var(g, j):
                if not exists(g):
                    return
                pe.wait_ge(sq_done, g + 1)
                if due(g - 1):
                    pe.wait_ge(ln_done, g - 1)
                pe.matmul(var_ps[j][:, 0:T], mean_w[:, :], sq[:, :], start=True, stop=True).then_inc(var_done, 1)

            def logits(g, j):
                pe.wait_ge(xn_done, g + 1)
                if due((g - 1) * STEPS):
                    pe.wait_ge(small, (g - 1) * STEPS)
                for t in range(NT):
                    last = pe.matmul(log_ps[j][:, t * EXPERTS:(t + 1) * EXPERTS], xn[j][:, t * TT:(t + 1) * TT], wg[:, :],
                                     start=True, stop=True, skip_group_check=True)
                last.then_inc(log_mm, 1)

            def turn(g, j):
                if isinstance(g, int) and g < 0:
                    return
                pe.wait_ge(small, g * STEPS + STEPS)
                if due(g - 1):
                    pe.wait_ge(gt_done, g - 1)
                for t in range(NT):
                    last = pe.transpose(gt_ps[j][0:EXPERTS, t * TT:(t + 1) * TT], comb[j][:, t, :], ident[0:TT, 0:TT])
                last.then_inc(gt_mm, 1)

            mean(0, 0)
            mean(1, 1)
            var(0, 0)

            def body(g, j):
                mean(g + 2, j)
                logits(g, j)
                var(g + 1, 1 - j)
                turn(g - 1, 1 - j)

            over_groups(pe, body, head=4)
            turn(NG - 1, 1)

        @block.scalar
        def _(act):
            act.preload_act_table_set(EXP_SET)

            def square(g, j):
                if not exists(g):
                    return
                act.wait_ge(cen_done, g + 1)
                if due(g):
                    act.wait_ge(var_done, g)
                act.activation(sq[:, :], cen[j][:, :], ACT.Square).then_inc(sq_done, 1)

            def rstd(g, j):
                if not exists(g):
                    return
                act.wait_ge(var_done, g + 1)
                if due(g - 1):
                    act.wait_ge(xn_done, g - 1)
                act.activation(rs[j][:, :], var_ps[j][:, 0:T], ACT.Ln, bias=sh.eps5[:, 0:1]).then_inc(ln_done, 1)
                act.wait_ge(ln_done, g + 1)
                act.activation(rs[j][:, :], rs[j][:, :], ACT.Exp, scale=-0.5).then_inc(rs_done, 1)

            square(0, 0)
            rstd(0, 0)

            def body(g, j):
                square(g + 1, 1 - j)
                rstd(g + 1, 1 - j)
                act.wait_ge(xn_done, g + 1)
                act.activation(XN[:, cols(g)], xn[j][:, :], ACT.Copy).then_inc(keep_done, 1)
                act.wait_ge(small, g * STEPS + 4)
                act.activation(ex[j][:, :], gap[j][:, :], ACT.Exp).then_inc(exp_done, 1)

            over_groups(act, body)

        @block.vector
        def _(dve):
            def centre(g, j):
                if not exists(g):
                    return
                dve.wait_ge(mean_done, g + 1)
                if due(g - 1):
                    dve.wait_ge(sq_done, g - 1)
                if due(g - 1):
                    dve.wait_ge(xn_done, g - 1)
                dve.tensor_tensor(cen[j][:, :], X[:, cols(g)], mean_ps[j][:, 0:T], ALU.subtract).then_inc(cen_done, 1)

            def norm(g, j):
                if not exists(g):
                    return
                dve.wait_ge(rs_done, g + 1)
                if due(g - 1):
                    dve.wait_ge(log_mm, g - 1)
                if due(g - 1):
                    dve.wait_ge(keep_done, g - 1)
                dve.tensor_tensor(xn[j][:, :], cen[j][:, :], rs[j][:, :], ALU.mult).then_inc(xn_done, 1)

            def step(g, k, ins):
                ins.then_inc(small, 1)
                dve.wait_ge(small, g * STEPS + k)

            def choose(g, j):
                dve.wait_ge(log_mm, g + 1)
                step(g, 1, dve.tensor_tensor(lg[:, :, :], log_ps[j][:, 0:NT * EXPERTS].rearrange("q (t e) -> q t e", e=EXPERTS),
                                             bg[:, :][:, None, :].to_broadcast([TT, NT, EXPERTS]), ALU.add))
                centre(g + 2, j)
                for t in range(NT):
                    last = dve.max(top[:, t, :], lg[:, t, :])
                step(g, 2, last)
                split(g - 1, 1 - j)
                for t in range(NT):
                    last = dve.max_index(idx[:, t, :], top[:, t, :], lg[:, t, :])
                step(g, 3, last)
                step(g, 4, dve.tensor_tensor(gap[j][:, :], top[:, :, 1], top[:, :, 0], ALU.subtract))
                step(g, 5, dve.tensor_copy(idf[:, :, :], idx[:, :, 0:2]))
                iota = sh.iota8[:, :][:, None, :].to_broadcast([TT, NT, EXPERTS])
                dve.tensor_tensor(pick[0][:, :, :], iota, idf[:, :, 0:1].to_broadcast([TT, NT, EXPERTS]), ALU.is_equal)
                step(g, 6, dve.tensor_tensor(pick[1][:, :, :], iota, idf[:, :, 1:2].to_broadcast([TT, NT, EXPERTS]), ALU.is_equal))

            def weigh(g, j):
                def per_tile(a):
                    return a[:, :][:, :, None].to_broadcast([TT, NT, EXPERTS])

                dve.wait_ge(exp_done, g + 1)
                step(g, 7, dve.tensor_scalar(den[:, :], ex[j][:, :], 1.0, None, ALU.add))
                step(g, 8, dve.reciprocal(g1[:, :], den[:, :]))
                step(g, 9, dve.tensor_tensor(g2[:, :], g1[:, :], ex[j][:, :], ALU.mult))
                dve.tensor_tensor(pick[0][:, :, :], pick[0][:, :, :], per_tile(g1), ALU.mult)
                step(g, 10, dve.tensor_tensor(pick[1][:, :, :], pick[1][:, :, :], per_tile(g2), ALU.mult))
                if due(g - 1):
                    dve.wait_ge(gt_mm, g - 1)
                step(g, 11, dve.tensor_tensor(comb[j][:, :, :], pick[0][:, :, :], pick[1][:, :, :], ALU.add))

            def split(g, j):
                if isinstance(g, int) and g < 0:
                    return
                dve.wait_ge(gt_mm, g + 1)
                if due(16 * (g - j) if not isinstance(g, int) else 16 * 2 * (g // 2)):
                    dve.wait_ge(stored[j], 16 * (g - j) if not isinstance(g, int) else 16 * 2 * (g // 2))
                dve.tensor_copy(hi[j][:, :], gt_ps[j][0:EXPERTS, 0:T]).then_inc(hi_done, 1)
                dve.wait_ge(hi_done, g + 1)
                dve.tensor_tensor(lo[j][:, :], gt_ps[j][0:EXPERTS, 0:T], hi[j][:, :].bitcast(F32), ALU.subtract).then_inc(gt_done, 1)

            centre(0, 0)
            centre(1, 1)
            norm(0, 0)

            def body(g, j):
                norm(g + 1, 1 - j)
                choose(g, j)
                weigh(g, j)

            over_groups(dve, body, head=4)
            split(NG - 1, 1)

        @block.sync
        def _(sp):
            def store(g, j):
                sp.wait_ge(gt_done, g + 1)
                dst = gates_dram[g * 16:g * 16 + 8] if isinstance(g, int) else gates_dram[bass.ds(g * 16, 8)]
                sp.dma_start(dst, hi[j][:, :].bitcast(F32)).then_inc(stored[j], 16)
                dst = gates_dram[g * 16 + 8:g * 16 + 16] if isinstance(g, int) else gates_dram[bass.ds(g * 16 + 8, 8)]
                sp.dma_start(dst, lo[j][:, :]).then_inc(stored[j], 16)

            over_groups(sp, store)
            for j in range(2):
                sp.wait_ge(stored[j], 16 * NG)


def experts_phase(nc, sh, kind, gates_dram, w1, b1, w2, b2, func, out_dram):
    X, XN = sh.X, sh.XN
    F = w1.shape[1]
    NC = F // C
    PIECE = 512
    CP = PIECE // C
    NP = F // PIECE
    per = 4 if (F // EXPERTS) % C == 0 else 1
    LA = 3
    with ExitStack() as ctx:
        def sb(name, shape, dt=F32):
            return ctx.enter_context(nc.sbuf_tensor(f"{kind}_{name}", shape, dt))

        def ps(name, shape):
            return ctx.enter_context(nc.psum_tensor(f"{kind}_{name}", shape, F32))

        sem = ctx.enter_context(PhaseSemaphores(nc, kind))

        hps = [ps(f"hps{i}", [C, 512]) for i in range(4)]
        gps = [ps(f"gps{i}", [C, 512]) for i in range(2)]
        ops_ = [ps(f"ops{i}", [C, 512]) for i in range(2)]
        raw = [sb(f"raw{i}", [C, PIECE]) for i in range(2)]
        w1h, w1l = sb("w1h", [C, F], F32R), sb("w1l", [C, F], F32R)
        w2h, w2l = sb("w2h", [C, NC * C], F32R), sb("w2l", [C, NC * C], F32R)
        b1t = sb("b1t", [C, NC])
        sel = sb("sel", [16, (NC // per) * C], F32R)
        b2r = sb("b2r", [16, C])
        b2h, b2l = sb("b2h", [16, C], F32R), sb("b2l", [16, C], F32R)
        xh = [sb(f"xh{i}", [C, T], F32R) for i in range(2)]
        xl = [sb(f"xl{i}", [C, T], F32R) for i in range(2)]
        ct = [sb(f"ct{i}", [16, T], F32R) for i in range(2)]
        gs = [sb(f"gs{i}", [C, T]) for i in range(2)]
        h_all = sb("h", [C, 4 * T])
        act_h = [h_all[:, i * T:(i + 1) * T] for i in range(4)]
        selr = h_all[0:16, 0:(NC // per) * C]
        hh = [sb(f"hh{i}", [C, T], F32R) for i in range(4)]
        hl = [sb(f"hl{i}", [C, T], F32R) for i in range(4)]

        small_loaded, small_split = sem("small_loaded"), sem("small_split")
        raw_loaded = [sem(f"raw_loaded{i}") for i in range(2)]
        w_high, w_split = sem("w_high"), sem("w_split")
        ct_loaded = [sem(f"ct_loaded{i}") for i in range(2)]
        xh_done, x_split = sem("xh"), sem("x_split")
        g_mm, g_done, h_mm, h_done = sem("gate_mm"), sem("gate_out"), sem("hidden_mm"), sem("hidden_out")
        gated = [sem("gated_pool"), sem("gated_dve")]
        hh_done, h_split, o_mm, res_done, stored = sem("hh"), sem("h_split"), sem("out_mm"), sem("residual"), sem("stored")

        block = ctx.enter_context(nc.Block())

        def on_dve(k):
            return k % 4 == 3

        def pieces():
            return [(m, q) for q in range(NP) for m in range(2)]

        @block.sync
        def _(sp):
            sp.dma_start(b1t[:, :], b1).then_inc(small_loaded, 16)
            sp.dma_start(selr[:, :], sh.sel_dram[kind]).then_inc(small_loaded, 16)
            sp.dma_start(b2r[0:8, :], b2).then_inc(small_loaded, 16)
            sp.dma_start(b2r[8:16, :], b2).then_inc(small_loaded, 16)

            def load_piece(n):
                m, q = pieces()[n]
                if due(n - 1):
                    sp.wait_ge(w_split, n - 1)
                src = w1[:, q * PIECE:(q + 1) * PIECE] if m == 0 else w2[q * PIECE:(q + 1) * PIECE, :].rearrange("(k p) c -> p k c", p=C)
                dst = raw[n % 2][:, :] if m == 0 else raw[n % 2][:, :].rearrange("p (k c) -> p k c", c=C)
                sp.dma_start(dst, src).then_inc(raw_loaded[n % 2], 16)

            def load_gates(g, j):
                if not exists(g):
                    return
                if due((g - 1) * NC):
                    sp.wait_ge(o_mm, (g - 1) * NC)
                src = gates_dram[g * 16:g * 16 + 16] if isinstance(g, int) else gates_dram[bass.ds(g * 16, 16)]
                sp.dma_start(ct[j][:, :].bitcast(F32), src).then_inc(ct_loaded[j], 16)

            load_gates(0, 0)
            load_gates(1, 1)
            for n in range(2 * NP):
                load_piece(n)

            def body(g, j):
                load_gates(g + 2, j)

            over_groups(sp, body)
            if out_dram is not None:
                sp.wait_ge(stored, 16 * NG)

        @block.tensor
        def _(pe):
            def gate(g, j, k):
                if k % per or not exists(g):
                    return
                q = k // per
                n = g * (NC // per) + q
                if q == 0:
                    if due(16 * (g // 2 + 1) if isinstance(g, int) else (g - j) * 8 + 16):
                        pe.wait_ge(ct_loaded[j], 16 * (g // 2 + 1) if isinstance(g, int) else (g - j) * 8 + 16)
                    if isinstance(g, int) and g == 0:
                        pe.wait_ge(small_split, 4)
                if due(n - 1):
                    pe.wait_ge(g_done, n - 1)
                pe.matmul(gps[q % 2][:, 0:T], sel[:, q * C:(q + 1) * C], ct[j][:, :], start=True, stop=True).then_inc(g_mm, 1)

            def hidden(g, j, k):
                if not exists(g):
                    return
                n = g * NC + k
                if k == 0:
                    pe.wait_ge(x_split, g + 1)
                if isinstance(g, int) and g == 0:
                    if due(2 * (k // CP) + 1):
                        pe.wait_ge(w_split, 2 * (k // CP) + 1)
                if due(n - 3):
                    pe.wait_ge(h_done, n - 3)
                c = slice(k * C, (k + 1) * C)
                pe.matmul(hps[k % 4][:, 0:T], w1h[:, c], xh[j][:, :], start=True, stop=False)
                pe.matmul(hps[k % 4][:, 0:T], w1h[:, c], xl[j][:, :], start=False, stop=False)
                pe.matmul(hps[k % 4][:, 0:T], w1l[:, c], xh[j][:, :], start=False, stop=True).then_inc(h_mm, 1)

            def output(g, j, k):
                n = g * NC + k
                if k == 0:
                    if due(g - 1):
                        pe.wait_ge(res_done, g - 1)
                    pe.matmul(ops_[j][:, 0:T], b2h[:, :], ct[j][:, :], start=True, stop=False)
                    pe.matmul(ops_[j][:, 0:T], b2l[:, :], ct[j][:, :], start=False, stop=False)
                if isinstance(g, int) and g == 0:
                    if due(2 * (k // CP) + 2):
                        pe.wait_ge(w_split, 2 * (k // CP) + 2)
                pe.wait_ge(h_split, n + 1)
                c = slice(k * C, (k + 1) * C)
                pe.matmul(ops_[j][:, 0:T], w2h[:, c], hh[k % 4][:, :], start=False, stop=False)
                pe.matmul(ops_[j][:, 0:T], w2h[:, c], hl[k % 4][:, :], start=False, stop=False)
                pe.matmul(ops_[j][:, 0:T], w2l[:, c], hh[k % 4][:, :], start=False, stop=(k == NC - 1)).then_inc(o_mm, 1)

            def ahead(g, j, k):
                if k + LA < NC:
                    gate(g, j, k + LA)
                    hidden(g, j, k + LA)
                else:
                    gate(g + 1, 1 - j, k + LA - NC)
                    hidden(g + 1, 1 - j, k + LA - NC)

            for k in range(LA):
                gate(0, 0, k)
                hidden(0, 0, k)

            def body(g, j):
                for k in range(NC):
                    ahead(g, j, k)
                    output(g, j, k)

            over_groups(pe, body)

        @block.scalar
        def _(act):
            act.wait_ge(small_loaded, 64)
            act.wait_ge(small_split, 1)

            def store(g):
                if out_dram is None or (isinstance(g, int) and g < 0):
                    return
                act.wait_ge(res_done, g + 1)
                dst = out_dram[g * GI:(g + 1) * GI] if isinstance(g, int) else out_dram[bass.ds(g * GI, GI)]
                act.dma_start(dst.rearrange("b c n -> c b n"), X[:, cols(g)].rearrange("c (b n) -> c b n", n=N)).then_inc(stored, 16)

            def body(g, j):
                for k in range(NC):
                    n = g * NC + k
                    if k == NC // 2:
                        store(g - 1)
                    if k % per == 0:
                        q = g * (NC // per) + k // per
                        act.wait_ge(g_mm, q + 1)
                        if due(n - per):
                            act.wait_ge(hh_done, n - per)
                        act.activation(gs[(k // per) % 2][:, :], gps[(k // per) % 2][:, 0:T], ACT.Copy).then_inc(g_done, 1)
                    act.wait_ge(h_mm, n + 1)
                    if due(n - 3):
                        act.wait_ge(h_split, n - 3)
                    act.activation(act_h[k % 4][:, :], hps[k % 4][:, 0:T], func, bias=b1t[:, k:k + 1]).then_inc(h_done, 1)

            over_groups(act, body)
            store(NG - 1)

        @block.gpsimd
        def _(pool):
            def body(g, j):
                for k in range(NC):
                    if on_dve(k):
                        continue
                    n = g * NC + k
                    if due(g * (NC // per) + k // per + 1):
                        pool.wait_ge(g_done, g * (NC // per) + k // per + 1)
                    pool.wait_ge(h_done, n + 1)
                    pool.tensor_tensor(act_h[k % 4][:, :], act_h[k % 4][:, :], gs[(k // per) % 2][:, :], ALU.mult).then_inc(gated[0], 1)

            over_groups(pool, body)

        @block.vector
        def _(dve):
            def split_piece(n):
                m, q = pieces()[n]
                high, low = (w1h, w1l) if m == 0 else (w2h, w2l)
                c = slice(q * PIECE, (q + 1) * PIECE)
                dve.wait_ge(raw_loaded[n % 2], 16 * (n // 2 + 1))
                dve.tensor_copy(high[:, c], raw[n % 2][:, :]).then_inc(w_high, 1)
                dve.wait_ge(w_high, n + 1)
                dve.tensor_tensor(low[:, c], raw[n % 2][:, :], high[:, c].bitcast(F32), ALU.subtract).then_inc(w_split, 1)

            def split_x(g, j):
                if not exists(g):
                    return
                if due((g - 1) * NC):
                    dve.wait_ge(h_mm, (g - 1) * NC)
                dve.tensor_copy(xh[j][:, :], XN[:, cols(g)]).then_inc(xh_done, 1)
                dve.wait_ge(xh_done, g + 1)
                dve.tensor_tensor(xl[j][:, :], XN[:, cols(g)], xh[j][:, :].bitcast(F32), ALU.subtract).then_inc(x_split, 1)

            def residual(g, j):
                if isinstance(g, int) and g < 0:
                    return
                dve.wait_ge(o_mm, (g + 1) * NC)
                dve.tensor_tensor(X[:, cols(g)], ops_[j][:, 0:T], X[:, cols(g)], ALU.add).then_inc(res_done, 1)

            dve.wait_ge(small_loaded, 64)
            dve.tensor_copy(sel[:, :], selr[:, :]).then_inc(small_split, 1)
            dve.tensor_copy(b2h[:, :], b2r[:, :]).then_inc(small_split, 1)
            dve.wait_ge(small_split, 2)
            dve.tensor_tensor(b2l[:, :], b2r[:, :], b2h[:, :].bitcast(F32), ALU.subtract).then_inc(small_split, 2)
            split_x(0, 0)
            split_piece(0)
            split_piece(1)

            def body(g, j):
                first = isinstance(g, int) and g == 0
                for k in range(NC):
                    n = g * NC + k
                    if first and k % CP == 0 and k // CP + 1 < NP:
                        split_piece(2 * (k // CP) + 2)
                        split_piece(2 * (k // CP) + 3)
                    if on_dve(k):
                        dve.wait_ge(h_done, n + 1)
                        if due(g * (NC // per) + k // per + 1):
                            dve.wait_ge(g_done, g * (NC // per) + k // per + 1)
                        dve.tensor_tensor(act_h[k % 4][:, :], act_h[k % 4][:, :], gs[(k // per) % 2][:, :], ALU.mult).then_inc(gated[1], 1)
                        if due(g * (NC // 4) + k // 4 + 1):
                            dve.wait_ge(gated[1], g * (NC // 4) + k // 4 + 1)
                    else:
                        if due(g * (NC - NC // 4) + k - k // 4 + 1):
                            dve.wait_ge(gated[0], g * (NC - NC // 4) + k - k // 4 + 1)
                    if due(n - 3):
                        dve.wait_ge(o_mm, n - 3)
                    dve.tensor_copy(hh[k % 4][:, :], act_h[k % 4][:, :]).then_inc(hh_done, 1)
                    dve.wait_ge(hh_done, n + 1)
                    dve.tensor_tensor(hl[k % 4][:, :], act_h[k % 4][:, :], hh[k % 4][:, :].bitcast(F32), ALU.subtract).then_inc(h_split, 1)
                    if k == NC // 2:
                        split_x(g + 1, 1 - j)
                    if k == 1:
                        residual(g - 1, 1 - j)

            over_groups(dve, body)
            residual(NG - 1, 1)


def build(nc, a, out):
    sh = Shared()
    gates = nc.dram_tensor("gates", (NG * 16, T), F32, kind="Internal").ap()
    with ExitStack() as ctx:
        def sb(name, shape):
            return ctx.enter_context(nc.sbuf_tensor(name, shape, F32))

        sh.X = sb("X", [C, IMAGES * N])
        sh.ident, sh.group_w = sb("ident", [C, C]), sb("group_w", [C, C])
        sh.mean_w, sh.centre_w = sb("mean_w", [C, C]), sb("centre_w", [C, C])
        sh.kmask, sh.vmask = sb("kmask", [C, HEADS]), sb("vmask", [S2, C])
        sh.iota8, sh.pos = sb("iota8", [TT, EXPERTS]), sb("pos", [C, N])
        sh.eps5, sh.eps6 = sb("eps5", [C, 1]), sb("eps6", [C, 1])
        sh.wg2, sh.wg3 = sb("wg2", [C, EXPERTS]), sb("wg3", [C, EXPERTS])
        sh.bg2, sh.bg3 = sb("bg2", [TT, EXPERTS]), sb("bg3", [TT, EXPERTS])
        sh.sel_dram = {"moe2": a["c_sel2"], "moe3": a["c_sel3"]}
        load_constants(nc, [
            (sh.ident[:, :], a["c_ident"]), (sh.mean_w[:, :], a["c_mean_w"]), (sh.centre_w[:, :], a["c_centre_w"]), (sh.group_w[:, :], a["c_group_w"]),
            (sh.kmask[:, :], a["c_kmask"]), (sh.vmask[:, :], a["c_vmask"]), (sh.iota8[:, :], a["c_iota8"]),
            (sh.pos[:, :], a["c_pos"]), (sh.eps5[:, :], a["c_eps5"]), (sh.eps6[:, :], a["c_eps6"]),
            (sh.wg2[:, :], a["L2_ffn_Wg"]), (sh.wg3[:, :], a["L3_ffn_Wr"]),
            (sh.bg2[:, :], a["L2_ffn_bg"].to_broadcast([TT, EXPERTS])),
            (sh.bg3[:, :], a["L3_ffn_br"].to_broadcast([TT, EXPERTS]))])
        heads_phase(nc, sh, a, "window", a["x"])
        if PHASES >= 2:
            single_phase(nc, sh, a, "conv")
        if PHASES >= 3:
            single_phase(nc, sh, a, "token")
        if PHASES >= 4:
            with nc.sbuf_tensor("XN2", [C, IMAGES * N], F32) as sh.XN:
                gate_phase(nc, sh, "g2", gates)
                experts_phase(nc, sh, "moe2", gates, a["L2_ffn_W1"], a["L2_ffn_b1"], a["L2_ffn_W2"], a["L2_ffn_b2"], ACT.Gelu, None)
        if PHASES >= 5:
            heads_phase(nc, sh, a, "scales", None)
        if PHASES >= 6:
            with nc.sbuf_tensor("XN3", [C, IMAGES * N], F32) as sh.XN:
                gate_phase(nc, sh, "g3", gates)
                experts_phase(nc, sh, "moe3", gates, a["L3_ffn_W1"], a["L3_ffn_b1"], a["L3_ffn_W2"], a["L3_ffn_b2"],
                              ACT.Gelu_apprx_tanh, out)
        else:
            with nc.semaphore("dbg") as dbg, nc.Block() as block:
                @block.sync
                def _(sp):
                    sp.dma_start(out.rearrange("b c n -> c b n"), sh.X[:, :].rearrange("c (b n) -> c b n", n=N)).then_inc(dbg, 16)
                    sp.wait_ge(dbg, 16)


PHASES = 6


def constants():
    import numpy as np
    f = np.float32
    c = np.arange(C)
    one = {"c_ident": np.eye(C, dtype=f), "c_mean_w": np.full((C, C), 1.0 / C, f)}
    one["c_centre_w"] = one["c_ident"] - one["c_mean_w"]
    one["c_group_w"] = np.where(c[:, None] // 4 == c[None, :] // 4, f(1.0 / (4 * N)), f(0)).astype(f)
    one["c_kmask"] = (c[:, None] // HD == np.arange(HEADS)[None, :]).astype(f)
    one["c_vmask"] = (np.arange(S2)[:, None] // N == c[None, :] // HD % 2).astype(f)
    one["c_iota8"] = np.tile(np.arange(EXPERTS, dtype=f), (TT, 1))
    inv = f(10000.0) ** (np.arange(0, C, 2, dtype=f) / f(C))
    ang = np.arange(N, dtype=f)[:, None] / inv
    one["c_pos"] = np.ascontiguousarray(np.concatenate([np.sin(ang), np.cos(ang)], -1).T.astype(f))
    one["c_eps5"], one["c_eps6"] = np.full((C, 1), 1e-5, f), np.full((C, 1), 1e-6, f)
    one["c_zeros"] = np.zeros((B1 - N, HEADS * N), f)
    for name, width, spread in (("c_sel2", 192, 1536), ("c_sel3", 128, 1024)):
        row = (np.arange(EXPERTS)[:, None] == np.arange(spread)[None, :] // width).astype(f)
        one[name] = np.concatenate([row, row])
    return one


def layout(inputs):
    import numpy as np
    a = {k: np.asarray(v) for k, v in inputs.items()}
    a["x"] = a["x"].reshape(IMAGES, C, N)
    side = 7
    rev = a.pop("L0_conv_rel_table")[::-1, ::-1, :]
    win = [rev[i:i + side, j:j + side].transpose(2, 0, 1) for i in reversed(range(side)) for j in reversed(range(side))]
    a["L0_conv_rel_bias"] = np.stack(win).reshape(N, HEADS * N)
    for n in ("wq", "wk", "wv", "wp"):
        a[f"L1_conv_{n}"] = a[f"L1_conv_{n}"].T
    for n, v in list(a.items()):
        if v.ndim == 1 and v.shape[0] == C:
            a[n] = v.reshape(C, 1)
    a["L2_ffn_bg"], a["L3_ffn_br"] = a["L2_ffn_bg"].reshape(1, EXPERTS), a["L3_ffn_br"].reshape(1, EXPERTS)
    a["L3_ffn_Wr"] = a["L3_ffn_Wr"].T
    for n in ("L2_ffn", "L3_ffn"):
        a[f"{n}_W1"] = a[f"{n}_W1"].transpose(1, 0, 2).reshape(C, -1)
        a[f"{n}_W2"] = a[f"{n}_W2"].reshape(-1, C)
        a[f"{n}_b1"] = a[f"{n}_b1"].reshape(-1, C).T
    return {k: np.ascontiguousarray(v) for k, v in a.items()}


def kernel(**inputs):
    import concourse.bacc as _bacc
    from concourse.bass_utils import run_bass_kernel_spmd as _run

    nc = _bacc.Bacc("TRN2", target_bir_lowering=False, num_devices=1)
    arrays = {f"in_{k}": v for k, v in {**layout(inputs), **constants()}.items()}
    args = {k[3:]: nc.dram_tensor(k, v.shape, F32, kind="ExternalInput").ap() for k, v in arrays.items()}
    out = nc.dram_tensor("out_y", (IMAGES, C, N), F32, kind="ExternalOutput").ap()
    build(nc, args, out)
    r = _run(nc, [arrays], core_ids=[0])
    return r.results[0]["out_y"].reshape(IMAGES, C, 7, 7)
```

```python
from contextlib import ExitStack

import concourse.bass as bass
from concourse import mybir

F32 = mybir.dt.float32
F32R = mybir.dt.float32r
U32 = mybir.dt.uint32
ALU = mybir.AluOpType
ACT = mybir.ActivationFunctionType
AX_X = mybir.AxisListType.X

C = 128
N = 49
IMAGES = 256
GI = 8
T = GI * N
NG = IMAGES // GI
PAIRS = GI // 2
HEADS = 8
HD = 16
HP = HEADS // 2
S2 = 2 * N
B1 = 64
R = B1 + N
EXPERTS = 8
TT = T // 4
EXP_SET = "natural_log_exp_and_others"


def due(count):
    assert isinstance(count, int) or count.min_val > 0, "a wait that could be for nothing"
    return not isinstance(count, int) or count > 0


def over_groups(eng, body, head=2, tail=2):
    for g in range(head):
        body(g, g % 2)
    with eng.Fori(head // 2, (NG - tail) // 2) as i:
        for j in range(2):
            body(i * 2 + j, j)
    for g in range(NG - tail, NG):
        body(g, g % 2)


def exists(g):
    return not isinstance(g, int) or g < NG


def cols(g):
    return bass.ds(g * T, T) if not isinstance(g, int) else slice(g * T, g * T + T)


def bcast(ap, shape):
    return ap.to_broadcast(shape)


class PhaseSemaphores:

    def __init__(self, nc, prefix):
        self.nc, self.prefix, self.held = nc, prefix, []

    def __enter__(self):
        return self

    def __call__(self, name):
        self.held.append(self.nc.alloc_semaphore(name=f"{self.prefix}_{name}"))
        return self.held[-1]

    def __exit__(self, *error):
        if error[0] is None:
            self.nc.clear_and_free_semaphores(self.held)
            self.nc.all_engine_barrier()


class Shared:
    pass


def load_constants(nc, loads):
    with PhaseSemaphores(nc, "constants") as sem, nc.Block() as block:
        loaded = sem("loaded")

        @block.sync
        def _(sp):
            for dst, src in loads:
                sp.dma_start(dst, src).then_inc(loaded, 16)
            sp.wait_ge(loaded, 16 * len(loads))


def heads_weights(nc, ctx, a, kind):
    def sb(name, shape):
        return ctx.enter_context(nc.sbuf_tensor(f"{kind}_{name}", shape, F32))

    w, b_in = sb("w", [C, 3 * C]), sb("b_in", [C, 6])
    if kind == "window":
        wo, relb = sb("wo", [C, C]), sb("relb", [R, HEADS * N])
        return (w, b_in, wo, relb), [
            (w[:, :], a["L0_conv_w_qkv"]), (wo[:, :], a["L0_conv_w_out"]), (b_in[:, 3:4], a["L0_conv_b_out"]),
            (b_in[:, 4:5], a["L0_conv_gamma"]), (b_in[:, 5:6], a["L0_conv_beta"]), (relb[0:N, :], a["L0_conv_rel_bias"]),
            (relb[N:B1, :], a["c_zeros"]), (relb[B1:R, :], a["L0_conv_rel_bias"])]
    return (w, b_in, None, None), [
        (w[:, 0:C], a["L3_attn_Wq"]), (w[:, C:2 * C], a["L3_attn_Wk"]), (w[:, 2 * C:3 * C], a["L3_attn_Wv"]),
        (b_in[:, 0:1], a["L3_attn_bq"]), (b_in[:, 1:2], a["L3_attn_bk"]), (b_in[:, 2:3], a["L3_attn_bv"])]


def conv_weights(nc, ctx, a):
    w = ctx.enter_context(nc.sbuf_tensor("conv_w", [C, 4 * C], F32))
    b_in = ctx.enter_context(nc.sbuf_tensor("conv_b_in", [C, 6], F32))
    loads = [(w[:, i * C:(i + 1) * C], a[f"L1_conv_{n}"]) for i, n in enumerate(("wq", "wk", "wv", "wp"))]
    loads += [(b_in[:, i:i + 1], a[f"L1_conv_{n}"]) for i, n in enumerate(("bq", "bk", "bv", "bp", "gn_scale", "gn_bias"))]
    return (w, b_in), loads


def heads_phase(nc, sh, kind, weights, x_in, later=()):
    window = kind == "window"
    scales = [1] if window else [1, 2, 4]
    widths = [len(range(0, N, s)) for s in scales]
    offs = [HEADS * sum(widths[:i]) for i in range(len(scales))]
    SW = HEADS * sum(widths)
    NS = len(scales)
    LEAD = 2
    X, ident = sh.X, sh.ident
    with ExitStack() as ctx:
        def sb(name, shape, dt=F32):
            return ctx.enter_context(nc.sbuf_tensor(f"{kind}_{name}", shape, dt))

        def ps(name, shape):
            return ctx.enter_context(nc.psum_tensor(f"{kind}_{name}", shape, F32))

        sem = ctx.enter_context(PhaseSemaphores(nc, kind))

        cps = ps("cen", [C, 512])
        vq, ko = ps("vq", [C, 512]), ps("ko", [C, 512])
        vps = ps("vps", [C, GI, HP * HD])
        sps = ps("sps", [C, 2, 512])
        ptps = ps("ptps", [C, 512])
        ops_ = ps("ops", [C, 512])

        w, b_in, wo, relb = weights
        b_use = sb("b_use", [C, 8])
        sq, rs = sb("sq", [C, T]), sb("rs", [C, T])
        xn = [sb(f"xn{i}", [C, T]) for i in range(2)]
        qt = [sb(f"qt{i}", [C, T]) for i in range(2)]
        kbd = [sb(f"kbd{i}", [C, GI, HP, N]) for i in range(2)]
        vbd = [sb(f"vbd{i}", [C, GI, C]) for i in range(2)]
        sc = [sb(f"sc{i}", [R, SW]) for i in range(2)]
        pr = [sb(f"pr{i}", [R, HEADS, B1]) for i in range(4)]
        px = [sb(f"px{i}", [R, SW - HEADS * N]) for i in range(2)] if not window else None
        mx = [sb(f"mx{i}", [R, NS * HEADS]) for i in range(2)]
        sm = [sb(f"sm{i}", [R, NS * HEADS]) for i in range(2)]
        rc = [sb(f"rc{i}", [R, NS * HEADS]) for i in range(2)]
        pt = [sb(f"pt{i}", [C, HP * R]) for i in range(2)]
        ot = sb("ot", [C, T])

        wready, bmm, zeroed = sem("weights_ready"), sem("bias_products"), sem("zeroed")
        preloaded = sem("preloaded")
        x_loaded = [sem(f"x_loaded{i}") for i in range(2)]
        mean_done, sq_done, var_done, ln_done, rs_done = sem("centred"), sem("squared"), sem("variance"), sem("logvar"), sem("rstd")
        xn_done, pos_done = sem("normed"), sem("positioned")
        q_mm, k_mm, q_done, k_done = sem("q_mm"), sem("k_mm"), sem("q_out"), sem("k_out")
        v_mm, v_done = sem("v_mm"), sem("v_out")
        s_mm, add_done, max_done, sub_done, exp_done = sem("s_mm"), sem("biased"), sem("maxed"), sem("shifted"), sem("exped")
        sum_done, rec_done, prob_done, mid_done, merged = sem("summed"), sem("recip"), sem("probs"), sem("merged_mid"), sem("merged")
        t_mm, t_done, pv_mm, o_done, out_mm, res_done = sem("t_mm"), sem("t_out"), sem("pv_mm"), sem("o_out"), sem("out_mm"), sem("residual")

        xn_ready = xn_done if window else pos_done
        final_probs = prob_done if window else merged
        ZEROED = 6

        block = ctx.enter_context(nc.Block())

        def pair(s, p, ahead):
            at = s.ahead((p + ahead) // PAIRS)
            return at, (p + ahead) % PAIRS, at.g * PAIRS + (p + ahead) % PAIRS

        def v_places(at, r):
            rows = slice(B1 * r, B1 * r + N)
            return (vbd[at.r % 2][rows].rearrange("k b (h r d) -> k b r h d", r=2, d=HD)[:, :, r],
                    vps[rows].rearrange("k b (h d) -> k b h d", d=HD))

        if window:
            @block.sync
            def _(sp):
                def load(g, j):
                    if due(16 * ((g - j) // 2) if isinstance(g, int) else (g - j) * 8):
                        sp.wait_ge(x_loaded[j], 16 * ((g - j) // 2) if isinstance(g, int) else (g - j) * 8)
                    dst = X[:, cols(g)].rearrange("c (b n) -> c b n", n=N)
                    src = x_in[bass.ds(g * GI, GI)] if not isinstance(g, int) else x_in[g * GI:(g + 1) * GI]
                    sp.dma_start(dst, src.rearrange("b c n -> c b n")).then_inc(x_loaded[j], 16)

                over_groups(sp, load)
                for dst, src in later:
                    sp.dma_start(dst, src).then_inc(preloaded, 16)
                for j in range(2):
                    sp.wait_ge(x_loaded[j], 16 * (NG // 2))
                sp.wait_ge(preloaded, 16 * len(later))

        @block.tensor
        def _(pe):
            if window:
                for m in range(3):
                    last = pe.matmul(ops_[:, m:m + 1], w[:, m * C:(m + 1) * C], b_in[:, 5:6], start=(m == 0), stop=True,
                                     skip_group_check=True)
                last.then_inc(bmm, 1)
                pe.wait_ge(wready, 2)
                pe.matmul(ops_[:, 3:4], wo[:, :], b_use[:, 2:3], start=True, stop=True,
                          skip_group_check=True).then_inc(bmm, 1)
            pe.wait_ge(wready, 8)
            pe.wait_ge(zeroed, ZEROED)

            def mean(at):
                g, j = at.g, at.r % 2
                if not at.exists():
                    return
                if window:
                    if due(16 * (g // 2 + 1) if isinstance(g, int) else (g - j) * 8 + 16):
                        pe.wait_ge(x_loaded[j], 16 * (g // 2 + 1) if isinstance(g, int) else (g - j) * 8 + 16)
                if due(g):
                    pe.wait_ge(xn_done, g)
                pe.matmul(cps[:, 0:T], sh.centre_w[:, :], X[:, cols(g)], start=True, stop=True).then_inc(mean_done, 1)

            def var(at):
                g = at.g
                if not at.exists():
                    return
                pe.wait_ge(sq_done, g + 1)
                if due(g):
                    pe.wait_ge(q_done, g)
                pe.matmul(vq[:, 0:T], sh.mean_w[:, :], sq[:, :], start=True, stop=True).then_inc(var_done, 1)

            def queries(at):
                g = at.g
                if not at.exists():
                    return
                pe.wait_ge(xn_ready, g + 1)
                pe.wait_ge(ln_done, g + 1)
                pe.matmul(vq[:, 0:T], w[:, 0:C], xn[at.r % 2][:, :], start=True, stop=True).then_inc(q_mm, 1)

            def keys(at):
                g = at.g
                if not at.exists():
                    return
                pe.wait_ge(xn_ready, g + 1)
                if due(g):
                    pe.wait_ge(k_done, g)
                if window:
                    if due(g - 2):
                        pe.wait_ge(res_done, g - 2)
                pe.matmul(ko[:, 0:T], w[:, C:2 * C], xn[at.r % 2][:, :], start=True, stop=True).then_inc(k_mm, 1)

            def tokens(at):
                g = at.g
                if not at.exists():
                    return
                if due(2 * g):
                    pe.wait_ge(v_done, 2 * g)
                wv = w[:, 2 * C:3 * C].rearrange("c (h r d) -> c r h d", r=2, d=HD)
                for b in range(GI):
                    for r in range(2):
                        last = pe.matmul(vps[B1 * r:B1 * r + N, b, :], xn[at.r % 2][:, b * N:(b + 1) * N], wv[:, r],
                                         start=True, stop=True, skip_group_check=True)
                last.then_inc(v_mm, 1)

            def scores_ready(at, n):
                if not at.exists():
                    return
                pe.wait_ge(q_done, at.g + 1)
                pe.wait_ge(k_done, at.g + 1)
                if due(n):
                    pe.wait_ge(add_done if window else sub_done, n)

            def scores(at, p, n):
                if not at.exists():
                    return
                j = at.r % 2
                for hf in range(2):
                    for im, m in ((0, B1), (1, N)):
                        b = 2 * p + im
                        rows = slice(B1 * hf, B1 * hf + B1)
                        last = pe.matmul(sps[B1 * im:B1 * im + m, hf, 0:HP * N], qt[j][rows, b * N:b * N + m],
                                         kbd[j][rows, b].rearrange("c h n -> c (h n)"), start=True, stop=True, skip_group_check=True)
                last.then_inc(s_mm, 1)

            def turn(at, p, n):
                if not at.exists():
                    return
                pe.wait_ge(final_probs, n + 1)
                if due(n):
                    pe.wait_ge(t_done, n)
                for hp in range(HP):
                    last = pe.transpose(ptps[:, hp * R:(hp + 1) * R], pr[p][:, 2 * hp:2 * hp + 2, :].rearrange("q h k -> q (h k)"),
                                        ident[0:R, 0:R])
                last.then_inc(t_mm, 1)

            def values(at, p, n, next_at, next_n):
                if not at.exists():
                    scores_ready(next_at, next_n)
                    return
                g, j = at.g, at.r % 2
                pe.wait_ge(t_done, n + 1)
                pe.wait_ge(v_done, 2 * g + 2)
                if p == 0:
                    if due(g):
                        pe.wait_ge(o_done, g)
                for im in range(2):
                    for hp in range(HP):
                        b = 2 * p + im
                        if im == 1 and hp == HP - 1:
                            scores_ready(next_at, next_n)
                        last = pe.matmul(ops_[32 * hp:32 * hp + 32, b * N:(b + 1) * N], vbd[j][:, b, 32 * hp:32 * hp + 32],
                                         pt[p % 2][:, hp * R + B1 * im:hp * R + B1 * im + N], start=True, stop=True,
                                         skip_group_check=True)
                last.then_inc(pv_mm, 1)

            def out(at):
                if not window or not at.exists():
                    return
                pe.wait_ge(o_done, at.g + 1)
                pe.wait_ge(k_done, at.g + 3 if at.ahead(2).exists() else NG)
                if due(at.g):
                    pe.wait_ge(res_done, at.g)
                pe.matmul(ko[:, 0:T], wo[:, :], ot[:, :], start=True, stop=True).then_inc(out_mm, 1)

            def window_body(s):
                for p in range(PAIRS):
                    if p == 3:
                        queries(s.ahead(2))
                    turn(*pair(s, p, -1))
                    if p == 0:
                        mean(s.ahead(2))
                        keys(s.ahead(1))
                    if p == 1:
                        tokens(s.ahead(1))
                        var(s.ahead(2))
                    if p == 2:
                        out(s.ahead(-1))
                    next_at, next_p, next_n = pair(s, p, 3)
                    values(*pair(s, p, -2), next_at, next_n)
                    scores(next_at, next_p, next_n)

            def scales_body(s):
                for p in range(PAIRS):
                    if p == 0:
                        mean(s.ahead(2))
                        keys(s.ahead(1))
                    turn(*pair(s, p, -1))
                    if p == 1:
                        var(s.ahead(2))
                    if p == 3:
                        queries(s.ahead(2))
                    next_at, next_p, next_n = pair(s, p, 3)
                    values(*pair(s, p, -2), next_at, next_n)
                    scores(next_at, next_p, next_n)
                    if p == 1:
                        tokens(s.ahead(1))

            over_steps(pe, window_body if window else scales_body, LEAD, turn=2)

        @block.vector
        def _(dve):
            if window:
                dve.wait_ge(bmm, 1)
                dve.tensor_copy(b_use[:, 0:3], ops_[:, 0:3]).then_inc(wready, 1)
                dve.tensor_scalar(w[:, :], w[:, :], b_in[:, 4:5], None, ALU.mult).then_inc(wready, 1)
                dve.wait_ge(bmm, 2)
                dve.tensor_tensor(b_use[:, 3:4], ops_[:, 3:4], b_in[:, 3:4], ALU.add).then_inc(wready, 1)
                dve.tensor_scalar(b_use[:, 0:1], b_use[:, 0:1], HD ** -0.5, None, ALU.mult).then_inc(wready, 1)
            else:
                dve.tensor_copy(b_use[:, 1:3], b_in[:, 1:3]).then_inc(wready, 3)
                dve.wait_ge(wready, 3)
                dve.tensor_scalar(b_use[:, 0:1], b_in[:, 0:1], HD ** -0.5, None, ALU.mult).then_inc(wready, 1)
            for r in range(HP):
                dve.tensor_tensor(b_use[:, 4 + r:5 + r], b_use[:, 1:2], sh.kmask[:, r:r + 1], ALU.mult).then_inc(wready, 1)

            dve.wait_ge(zeroed, ZEROED)

            def norm(at):
                g, j = at.g, at.r % 2
                if not at.exists():
                    return
                dve.wait_ge(rs_done, g + 1)
                if due(g - 1):
                    dve.wait_ge(v_mm, g - 1)
                dve.tensor_tensor(xn[j][:, :], cps[:, 0:T], rs[:, :], ALU.mult).then_inc(xn_done, 1)

            def sview(ap, i):
                return ap[:, offs[i]:offs[i] + HEADS * widths[i]].rearrange("q (h k) -> q h k", h=HEADS)

            def halves(ap, i):
                return sview(ap, i).rearrange("q (f h) k -> q f h k", f=2)

            def picked(i):
                return sps[0:R, :, 0:HP * N].rearrange("q f (h k) -> q f h k", k=N)[:, :, :, 0:N:scales[i]]

            def maxima(k, i):
                return mx[k][:, i * HEADS:(i + 1) * HEADS].rearrange("q (f h) -> q f h", f=2)

            def v_out(at, r):
                if not window or not at.exists():
                    return
                dve.wait_ge(v_mm, at.g + 1)
                if due((at.g - 1) * PAIRS):
                    dve.wait_ge(pv_mm, (at.g - 1) * PAIRS)
                dst, src = v_places(at, r)
                dve.tensor_copy(dst, src).then_inc(v_done, 1)

            def shift(at, p, n):
                if not at.exists():
                    return
                k = p % 2
                dve.wait_ge(s_mm, n + 1)
                if due(n - 1):
                    dve.wait_ge(exp_done, n - 1)
                if due(n - 1):
                    dve.wait_ge(sub_done, n - 1)
                if window:
                    dve.tensor_tensor(halves(sc[k], 0), picked(0), halves(relb, 0), ALU.add).then_inc(add_done, 1)
                    dve.wait_ge(add_done, n + 1)
                    dve.tensor_reduce(mx[k][:, :], sview(sc[k], 0), AX_X, ALU.max).then_inc(max_done, 1)
                else:
                    for i in range(NS):
                        last = dve.tensor_reduce(maxima(k, i), picked(i), AX_X, ALU.max)
                    last.then_inc(max_done, 1)
                    dve.wait_ge(max_done, n + 1)
                    for i in range(NS):
                        last = dve.tensor_tensor(halves(sc[k], i), picked(i), maxima(k, i)[:, :, :, None].to_broadcast([R, 2, HP, widths[i]]),
                                                 ALU.subtract)
                    last.then_inc(sub_done, 1)

            def total(at, p, n):
                if not at.exists():
                    return
                k = p % 2
                dve.wait_ge(exp_done, n + 1)
                if due(n - 1):
                    dve.wait_ge(rec_done, n - 1)
                for i in range(NS):
                    v = pr[p][:, :, 0:N] if i == 0 else px[k][:, offs[i] - offs[1]:offs[i] - offs[1] + HEADS * widths[i]].rearrange(
                        "q (h k) -> q h k", h=HEADS)
                    last = dve.tensor_reduce(sm[k][:, i * HEADS:(i + 1) * HEADS], v, AX_X, ALU.add)
                last.then_inc(sum_done, 1)
                dve.wait_ge(sum_done, n + 1)
                if due(n - 1):
                    dve.wait_ge(prob_done, n - 1)
                dve.reciprocal(rc[k][:, :], sm[k][:, :]).then_inc(rec_done, 1)

            def residual(at):
                if not window or not at.exists():
                    return
                g = at.g
                dve.wait_ge(out_mm, g + 1)
                dve.scalar_tensor_tensor(out=X[:, cols(g)], in0=ko[:, 0:T], scalar=b_use[:, 3:4], in1=X[:, cols(g)],
                                         op0=ALU.add, op1=ALU.add).then_inc(res_done, 1)

            def window_body(s):
                for p in range(PAIRS):
                    total(*pair(s, p, 0))
                    shift(*pair(s, p, 2))
                    if p == 1:
                        v_out(s.ahead(1), 0)
                    if p == 2:
                        norm(s.ahead(2))
                    if p == 3:
                        v_out(s.ahead(1), 1)
                        residual(s.ahead(-1))

            def scales_body(s):
                for p in range(PAIRS):
                    total(*pair(s, p, 0))
                    shift(*pair(s, p, 2))
                    if p == 2:
                        norm(s.ahead(2))

            over_steps(dve, window_body if window else scales_body, LEAD, turn=2)
            dve.wait_ge(res_done, NG)

        @block.gpsimd
        def _(pool):
            for t in (pr[0][:, :, :], vbd[0][:, :, :], pr[1][:, :, :], pr[2][:, :, :], pr[3][:, :, :], vbd[1][:, :, :]):
                pool.memset(t, 0.0).then_inc(zeroed, 1)
            pool.wait_ge(zeroed, ZEROED)

            def shift(at, p, n):
                if not window or not at.exists():
                    return
                v = sc[p % 2][:, :].rearrange("q (h k) -> q h k", h=HEADS)
                pool.wait_ge(max_done, n + 1)
                pool.tensor_tensor(v, v, mx[p % 2][:, :][:, :, None].to_broadcast([R, HEADS, N]), ALU.subtract).then_inc(sub_done, 1)

            def probs(at, p, n):
                if not at.exists():
                    return
                k = p % 2
                full = pr[p][:, :, 0:N]
                parts = [full] + [px[k][:, offs[i] - offs[1]:offs[i] - offs[1] + HEADS * widths[i]].rearrange("q (h k) -> q h k", h=HEADS)
                                  for i in range(1, NS)]
                pool.wait_ge(rec_done, n + 1)
                for i, v in enumerate(parts):
                    last = pool.tensor_tensor(v, v, rc[k][:, i * HEADS:(i + 1) * HEADS][:, :, None].to_broadcast([R, HEADS, widths[i]]),
                                              ALU.mult)
                last.then_inc(prob_done, 1)
                if not window:
                    d = full[:, :, 0:N:scales[1]]
                    pool.wait_ge(prob_done, n + 1)
                    pool.tensor_tensor(d, d, parts[1], ALU.add).then_inc(mid_done, 1)
                    d = full[:, :, 0:N:scales[2]]
                    pool.wait_ge(mid_done, n + 1)
                    pool.tensor_tensor(d, d, parts[2], ALU.add).then_inc(merged, 1)

            def position(at):
                if window or not at.exists():
                    return
                v = xn[at.r % 2][:, :].rearrange("c (b n) -> c b n", n=N)
                pool.wait_ge(xn_done, at.g + 1)
                pool.tensor_tensor(v, v, sh.pos[:, :][:, None, :].to_broadcast([C, GI, N]), ALU.add).then_inc(pos_done, 1)

            def residual(at):
                if window or not at.exists():
                    return
                pool.wait_ge(o_done, at.g + 1)
                pool.tensor_tensor(X[:, cols(at.g)], X[:, cols(at.g)], ot[:, :], ALU.add).then_inc(res_done, 1)

            def window_body(s):
                for p in range(PAIRS):
                    shift(*pair(s, p, 1))
                    probs(*pair(s, p, 0))

            def scales_body(s):
                for p in range(PAIRS):
                    shift(*pair(s, p, 1))
                    probs(*pair(s, p, 0))
                    if p == 2:
                        position(s.ahead(2))
                    if p == 3:
                        residual(s.ahead(-1))

            over_steps(pool, window_body if window else scales_body, LEAD, turn=2)

        @block.scalar
        def _(act):
            act.preload_act_table_set(EXP_SET)
            act.wait_ge(wready, 8)
            act.wait_ge(zeroed, ZEROED)

            def square(at):
                g = at.g
                if not at.exists():
                    return
                act.wait_ge(mean_done, g + 1)
                if due(g):
                    act.wait_ge(var_done, g)
                act.activation(sq[:, :], cps[:, 0:T], ACT.Square).then_inc(sq_done, 1)

            def rstd(at):
                g = at.g
                if not at.exists():
                    return
                act.wait_ge(var_done, g + 1)
                if due(g):
                    act.wait_ge(xn_done, g)
                act.activation(rs[:, :], vq[:, 0:T], ACT.Ln, bias=sh.eps5[:, 0:1]).then_inc(ln_done, 1)
                act.wait_ge(ln_done, g + 1)
                act.activation(rs[:, :], rs[:, :], ACT.Exp, scale=-0.5).then_inc(rs_done, 1)

            def q_out(at):
                g, j = at.g, at.r % 2
                if not at.exists():
                    return
                act.wait_ge(q_mm, g + 1)
                if due(g * PAIRS - PAIRS):
                    act.wait_ge(s_mm, g * PAIRS - PAIRS)
                act.activation(qt[j][:, :], vq[:, 0:T], ACT.Identity, bias=b_use[:, 0:1], scale=HD ** -0.5).then_inc(q_done, 1)

            def k_out(at, half):
                g, j = at.g, at.r % 2
                if not at.exists():
                    return
                act.wait_ge(k_mm, g + 1)
                for r in range(2 * half, 2 * half + 2):
                    last = act.activation(kbd[j][:, :, r, :], ko[:, 0:T].rearrange("c (b n) -> c b n", n=N), ACT.Identity,
                                          bias=b_use[:, 4 + r:5 + r], scale=sh.kmask[:, r:r + 1])
                if half:
                    last.then_inc(k_done, 1)

            def expo(at, p, n):
                if not at.exists():
                    return
                act.wait_ge(sub_done, n + 1)
                if due(n - 3):
                    act.wait_ge(t_mm, n - 3)
                last = act.activation(pr[p][:, :, 0:N], sc[p % 2][:, 0:HEADS * N].rearrange("q (h k) -> q h k", h=HEADS), ACT.Exp)
                if not window:
                    if due(n - 1):
                        act.wait_ge(merged, n - 1)
                    last = act.activation(px[p % 2][:, :], sc[p % 2][:, HEADS * N:SW], ACT.Exp)
                last.then_inc(exp_done, 1)

            def turned(at, p, n):
                if not at.exists():
                    return
                act.wait_ge(t_mm, n + 1)
                if due(n - 1):
                    act.wait_ge(pv_mm, n - 1)
                act.activation(pt[p % 2][:, :], ptps[:, 0:HP * R], ACT.Copy).then_inc(t_done, 1)

            def o_out(at):
                if not at.exists():
                    return
                g, j = at.g, at.r % 2
                act.wait_ge(pv_mm, (g + 1) * PAIRS)
                if due(g):
                    act.wait_ge(out_mm if window else res_done, g)
                if window:
                    act.activation(ot[:, :], ops_[:, 0:T], ACT.Copy).then_inc(o_done, 1)
                else:
                    act.activation(ot[:, :], ops_[:, 0:T], ACT.Identity, bias=b_use[:, 2:3], scale=1.0 / NS).then_inc(o_done, 1)

            def v_out(at, r):
                if window or not at.exists():
                    return
                act.wait_ge(v_mm, at.g + 1)
                if due((at.g - 1) * PAIRS):
                    act.wait_ge(pv_mm, (at.g - 1) * PAIRS)
                dst, src = v_places(at, r)
                act.activation(dst, src, ACT.Copy).then_inc(v_done, 1)

            def window_body(s):
                for p in range(PAIRS):
                    if p == 2:
                        o_out(s.ahead(-1))
                    turned(*pair(s, p, -1))
                    if p == 0:
                        square(s.ahead(2))
                    if p == 1:
                        k_out(s.ahead(1), 1)
                    expo(*pair(s, p, 1))
                    if p == 0:
                        k_out(s.ahead(1), 0)
                    if p == 1:
                        rstd(s.ahead(2))
                    if p == 3:
                        q_out(s.ahead(2))

            def scales_body(s):
                for p in range(PAIRS):
                    if p == 0:
                        square(s.ahead(2))
                    expo(*pair(s, p, 1))
                    if p == 0:
                        k_out(s.ahead(1), 0)
                    if p == 1:
                        k_out(s.ahead(1), 1)
                    if p == 2:
                        o_out(s.ahead(-1))
                    turned(*pair(s, p, -1))
                    if p == 1:
                        rstd(s.ahead(2))
                    if p == 2:
                        v_out(s.ahead(1), 0)
                    if p == 3:
                        q_out(s.ahead(2))
                        v_out(s.ahead(1), 1)

            over_steps(act, window_body if window else scales_body, LEAD, turn=2)


def over_steps(eng, body, lead, lag=1, turn=4):
    stop = (NG - lead) // 4 * 4
    for s in range(-lead, 4):
        body(Step(s, s))
    with eng.Fori(4 // turn, stop // turn) as i:
        for j in range(turn):
            body(Step(i * turn + j, j))
    for s in range(stop, NG + lag):
        body(Step(s, s))


class Step:

    def __init__(self, g, remainder):
        self.g, self.r = g, remainder % 4

    def ahead(self, k):
        return Step(self.g + k, self.r + k)

    def exists(self):
        return not isinstance(self.g, int) or 0 <= self.g < NG


def single_phase(nc, sh, kind, weights=None):
    conv = kind == "conv"
    X, ident = sh.X, sh.ident
    LEAD = 4
    with ExitStack() as ctx:
        def sb(name, shape, dt=F32):
            return ctx.enter_context(nc.sbuf_tensor(f"{kind}_{name}", shape, dt))

        def ps(name, shape):
            return ctx.enter_context(nc.psum_tensor(f"{kind}_{name}", shape, F32))

        sem = ctx.enter_context(PhaseSemaphores(nc, kind))

        if conv:
            st, pjq, pjk = ps("st", [C, 512]), ps("pjq", [C, 512]), ps("pjk", [C, 512])
        else:
            cps = [ps(f"cen{i}", [C, 512]) for i in range(2)]
            st = ps("st", [C, 512])
        vps = ps("vps", [C, 4, C])
        sps, ptps, ops_ = ps("sps", [C, 512]), ps("ptps", [C, 512]), ps("ops", [C, 512])
        if conv:
            w, b_in = weights
            b_use = sb("b_use", [C, 4])
            csum, ssum = sb("csum", [C, GI]), sb("ssum", [C, GI])
            cen = [sb(f"cen{i}", [C, T]) for i in range(2)]
            qt, kt, ot = sb("qt", [C, T]), sb("kt", [C, T]), sb("ot", [C, T])
        sq = sb("sq", [C, T])
        rs = sb("rs", [C, GI if conv else T])
        xn = [sb(f"xn{i}", [C, GI, B1]) for i in range(2)]
        vt = [sb(f"vt{i}", [R, 4, C]) for i in range(4)]
        sc = sb("sc", [R, PAIRS, N])
        pr = [sb(f"pr{i}", [R, PAIRS, B1]) for i in range(2)]
        mx, sm = sb("mx", [R, PAIRS]), sb("sm", [R, PAIRS])
        rc = [sb(f"rc{i}", [R, PAIRS]) for i in range(2)]
        pt = [sb(f"pt{i}", [C, 2, 2, 2, N]) for i in range(2)]

        wready, bmm, zeroed = sem("weights_ready"), sem("bias_products"), sem("zeroed")
        csum_done, mean_done, cen_done, sq_done, ssum_done = sem("csum"), sem("mean"), sem("centred"), sem("squared"), sem("ssum")
        var_done, ln_done, rs_done, xn_done = sem("variance"), sem("logvar"), sem("rstd"), sem("normed")
        q_mm, k_mm, q_done, k_done, v_mm, v_done = sem("q_mm"), sem("k_mm"), sem("q_out"), sem("k_out"), sem("v_mm"), sem("v_out")
        s_mm, max_done, sub_done, exp_done = sem("s_mm"), sem("maxed"), sem("shifted"), sem("exped")
        sum_done, rec_done, prob_done = sem("summed"), sem("recip"), sem("probs")
        t_mm, t_done, pv_mm, o_done, out_mm, res_done = sem("t_mm"), sem("t_out"), sem("pv_mm"), sem("o_out"), sem("out_mm"), sem("residual")

        block = ctx.enter_context(nc.Block())

        def images(ap):
            return ap.rearrange("c (b n) -> c b n", n=N)

        @block.tensor
        def _(pe):
            if conv:
                for m in range(3):
                    last = pe.matmul(sps[:, m:m + 1], w[:, m * C:(m + 1) * C], b_in[:, 5:6], start=(m == 0), stop=True,
                                     skip_group_check=True)
                last.then_inc(bmm, 1)
                pe.wait_ge(wready, 2)
                pe.matmul(sps[:, 3:4], w[:, 3 * C:4 * C], b_use[:, 2:3], start=True, stop=True,
                          skip_group_check=True).then_inc(bmm, 1)
                pe.wait_ge(wready, 3)
            pe.wait_ge(zeroed, 6)

            def mean(at):
                g = at.g
                if not at.exists():
                    return
                if conv:
                    if due(g - 1):
                        pe.wait_ge(ln_done, g - 1)
                    pe.wait_ge(csum_done, g + 1)
                    pe.matmul(st[:, 0:GI], sh.group_w[:, :], csum[:, :], start=True, stop=True).then_inc(mean_done, 1)
                else:
                    if due(g - 1):
                        pe.wait_ge(xn_done, g - 1)
                    pe.matmul(cps[at.r % 2][:, 0:T], sh.centre_w[:, :], X[:, cols(g)], start=True, stop=True).then_inc(mean_done, 1)

            def var(at):
                g = at.g
                if not at.exists():
                    return
                if conv:
                    pe.wait_ge(cen_done, g + 2 if at.ahead(1).exists() else NG)
                    pe.wait_ge(ssum_done, g + 1)
                    pe.matmul(st[:, 0:GI], sh.group_w[:, :], ssum[:, :], start=True, stop=True).then_inc(var_done, 1)
                else:
                    pe.wait_ge(sq_done, g + 1)
                    if due(g):
                        pe.wait_ge(ln_done, g)
                    pe.matmul(st[:, 0:T], sh.mean_w[:, :], sq[:, :], start=True, stop=True).then_inc(var_done, 1)

            def queries(at):
                g = at.g
                if not at.exists() or not conv:
                    return
                x = xn[at.r % 2][:, :, 0:N]
                pe.wait_ge(xn_done, g + 1)
                if due(g - 3):
                    pe.wait_ge(res_done, g - 3)
                if due(g):
                    pe.wait_ge(q_done, g)
                pe.matmul(pjq[:, 0:T], w[:, 0:C], x, start=True, stop=True).then_inc(q_mm, 1)
                if due(g):
                    pe.wait_ge(k_done, g)
                pe.matmul(pjk[:, 0:T], w[:, C:2 * C], x, start=True, stop=True).then_inc(k_mm, 1)

            def tokens(at):
                g = at.g
                if not at.exists():
                    return
                x = xn[at.r % 2]
                pe.wait_ge(xn_done, g + 1)
                if due(g):
                    pe.wait_ge(v_done, g)
                for mq in range(4):
                    if conv:
                        for r, m in ((0, B1), (1, N)):
                            last = pe.matmul(vps[B1 * r:B1 * r + m, mq, :], x[:, 2 * mq + r, 0:m], w[:, 2 * C:3 * C],
                                             start=True, stop=True, skip_group_check=True)
                    else:
                        last = pe.transpose(vps[:, mq, :], x[:, 2 * mq:2 * mq + 2, :].rearrange("c b n -> c (b n)"), ident[:, :])
                last.then_inc(v_mm, 1)

            def scores(at):
                g = at.g
                if not at.exists():
                    return
                if conv:
                    pe.wait_ge(k_done, g + 1)
                else:
                    pe.wait_ge(xn_done, g + 1)
                if due(g):
                    pe.wait_ge(sub_done, g)
                for p in range(PAIRS):
                    for m, rows in ((0, B1), (1, N)):
                        b = 4 * m + p
                        if conv:
                            q, k = qt[:, b * N:b * N + rows], kt[:, b * N:b * N + N]
                        else:
                            q, k = xn[at.r % 2][:, b, 0:rows], xn[at.r % 2][:, b, 0:N]
                        last = pe.matmul(sps[B1 * m:B1 * m + rows, p * N:(p + 1) * N], q, k, start=True, stop=True,
                                         skip_group_check=True)
                last.then_inc(s_mm, 1)

            def turn(at):
                g = at.g
                if not at.exists():
                    return
                pe.wait_ge(prob_done, g + 1)
                if due(g):
                    pe.wait_ge(t_done, g)
                for q in range(2):
                    last = pe.transpose(ptps[:, q * R:(q + 1) * R], pr[at.r % 2][:, 2 * q:2 * q + 2, :].rearrange("t p k -> t (p k)"),
                                        ident[0:R, 0:R])
                last.then_inc(t_mm, 1)

            def values(at):
                g = at.g
                if not at.exists():
                    return
                pe.wait_ge(t_done, g + 1)
                pe.wait_ge(v_done, g + 1)
                if due(g):
                    pe.wait_ge(o_done if conv else res_done, g)
                for m in range(2):
                    for q in range(2):
                        mq = 2 * m + q
                        last = pe.matmul(ops_[:, mq * S2:(mq + 1) * S2], vt[at.r][:, mq, :],
                                         pt[at.r % 2][0:R, m, q].rearrange("k r n -> k (r n)"),
                                         start=True, stop=True, skip_group_check=True)
                last.then_inc(pv_mm, 1)

            def out(at):
                g = at.g
                if not at.exists() or not conv:
                    return
                pe.wait_ge(o_done, g + 1)
                pe.wait_ge(q_done, g + 4 if at.ahead(3).exists() else NG)
                if due(g):
                    pe.wait_ge(res_done, g)
                pe.matmul(pjq[:, 0:T], w[:, 3 * C:4 * C], ot[:, :], start=True, stop=True).then_inc(out_mm, 1)

            def body(s):
                scores(s.ahead(1))
                values(s.ahead(-1))
                turn(s)
                mean(s.ahead(4))
                queries(s.ahead(2))
                var(s.ahead(3))
                tokens(s.ahead(2))
                out(s.ahead(-1))

            over_steps(pe, body, LEAD)

        @block.vector
        def _(dve):
            for i in range(2):
                dve.memset(xn[i][:, :, :], 0.0).then_inc(zeroed, 1)
                dve.memset(pr[i][:, :, :], 0.0).then_inc(zeroed, 1)
                dve.memset(pt[i][:, :, :, :, :], 0.0).then_inc(zeroed, 1)
            dve.wait_ge(zeroed, 6)
            if conv:
                dve.wait_ge(bmm, 1)
                dve.tensor_tensor(b_use[:, 0:3], sps[:, 0:3], b_in[:, 0:3], ALU.add).then_inc(wready, 1)
                dve.tensor_scalar(w[:, 0:3 * C], w[:, 0:3 * C], b_in[:, 4:5], None, ALU.mult).then_inc(wready, 1)
                dve.wait_ge(bmm, 2)
                dve.tensor_tensor(b_use[:, 3:4], sps[:, 3:4], b_in[:, 3:4], ALU.add).then_inc(wready, 1)
                dve.tensor_scalar(b_use[:, 0:1], b_use[:, 0:1], C ** -0.5, None, ALU.mult).then_inc(wready, 1)

            def sums(at):
                g = at.g
                if not at.exists() or not conv:
                    return
                if due(g):
                    dve.wait_ge(mean_done, g)
                dve.tensor_reduce(csum[:, :], images(X[:, cols(g)]), AX_X, ALU.add).then_inc(csum_done, 1)

            def centre(at):
                g = at.g
                if not at.exists() or not conv:
                    return
                dve.wait_ge(mean_done, g + 1)
                if due(g - 1):
                    dve.wait_ge(sq_done, g - 1)
                    dve.wait_ge(xn_done, g - 1)
                dve.tensor_tensor(images(cen[at.r % 2][:, :]), images(X[:, cols(g)]), st[:, 0:GI][:, :, None].to_broadcast([C, GI, N]),
                                  ALU.subtract).then_inc(cen_done, 1)

            def squares(at):
                g = at.g
                if not at.exists() or not conv:
                    return
                dve.wait_ge(sq_done, g + 1)
                if due(g):
                    dve.wait_ge(var_done, g)
                dve.tensor_reduce(ssum[:, :], images(sq[:, :]), AX_X, ALU.add).then_inc(ssum_done, 1)

            def norm(at):
                g, x = at.g, xn[at.r % 2][:, :, 0:N]
                if not at.exists():
                    return
                dve.wait_ge(rs_done, g + 1)
                if due(g - 1):
                    dve.wait_ge(v_mm, g - 1)
                    dve.wait_ge(k_mm if conv else s_mm, g - 1)
                if conv:
                    dve.tensor_tensor(x, images(cen[at.r % 2][:, :]), rs[:, :][:, :, None].to_broadcast([C, GI, N]),
                                      ALU.mult).then_inc(xn_done, 1)
                else:
                    dve.tensor_tensor(x, images(cps[at.r % 2][:, 0:T]), images(rs[:, :]), ALU.mult).then_inc(xn_done, 1)

            def v_out(at):
                g = at.g
                if not at.exists():
                    return
                dve.wait_ge(v_mm, g + 1)
                if due(g - 3):
                    dve.wait_ge(pv_mm, g - 3)
                dve.tensor_copy(vt[at.r][:, :, :], vps[0:R, :, :]).then_inc(v_done, 1)

            def shift(at):
                g = at.g
                if not at.exists():
                    return
                s3 = sps[0:R, 0:PAIRS * N].rearrange("t (p k) -> t p k", k=N)
                dve.wait_ge(s_mm, g + 1)
                if due(g):
                    dve.wait_ge(sub_done, g)
                dve.tensor_reduce(mx[:, :], s3, AX_X, ALU.max).then_inc(max_done, 1)
                dve.wait_ge(max_done, g + 1)
                if due(g):
                    dve.wait_ge(exp_done, g)
                dve.tensor_tensor(sc[:, :, :], s3, mx[:, :][:, :, None].to_broadcast([R, PAIRS, N]), ALU.subtract).then_inc(sub_done, 1)

            def total(at):
                g = at.g
                if not at.exists():
                    return
                dve.wait_ge(exp_done, g + 1)
                if due(g):
                    dve.wait_ge(rec_done, g)
                dve.tensor_reduce(sm[:, :], pr[at.r % 2][:, :, 0:N], AX_X, ALU.add).then_inc(sum_done, 1)
                dve.wait_ge(sum_done, g + 1)
                if due(g - 1):
                    dve.wait_ge(prob_done, g - 1)
                dve.reciprocal(rc[at.r % 2][:, :], sm[:, :]).then_inc(rec_done, 1)

            def residual(at):
                g = at.g
                if not at.exists():
                    return
                dve.wait_ge(out_mm if conv else pv_mm, g + 1)
                if conv:
                    dve.scalar_tensor_tensor(out=X[:, cols(g)], in0=pjq[:, 0:T], scalar=b_use[:, 3:4], in1=X[:, cols(g)],
                                             op0=ALU.add, op1=ALU.add).then_inc(res_done, 1)
                else:
                    dve.tensor_tensor(X[:, cols(g)], ops_[:, 0:T], X[:, cols(g)], ALU.add).then_inc(res_done, 1)

            def body(s):
                sums(s.ahead(4))
                shift(s.ahead(1))
                squares(s.ahead(3))
                centre(s.ahead(4))
                if not conv:
                    residual(s.ahead(-1))
                total(s.ahead(1))
                v_out(s.ahead(2))
                norm(s.ahead(3))
                if conv:
                    residual(s.ahead(-1))

            over_steps(dve, body, LEAD)
            dve.wait_ge(res_done, NG)

        @block.gpsimd
        def _(pool):
            def body(s):
                at = s.ahead(1)
                if not at.exists():
                    return
                p = pr[at.r % 2][:, :, 0:N]
                pool.wait_ge(rec_done, at.g + 1)
                pool.tensor_tensor(p, p, rc[at.r % 2][:, :][:, :, None].to_broadcast([R, PAIRS, N]), ALU.mult).then_inc(prob_done, 1)

            over_steps(pool, body, LEAD)

        @block.scalar
        def _(act):
            act.preload_act_table_set(EXP_SET)
            act.wait_ge(zeroed, 6)
            if conv:
                act.wait_ge(wready, 4)

            def square(at):
                g = at.g
                if not at.exists():
                    return
                act.wait_ge(cen_done if conv else mean_done, g + 1)
                if due(g):
                    act.wait_ge(ssum_done if conv else var_done, g)
                src = cen[at.r % 2][:, :] if conv else cps[at.r % 2][:, 0:T]
                act.activation(sq[:, :], src, ACT.Square).then_inc(sq_done, 1)

            def rstd(at):
                g = at.g
                if not at.exists():
                    return
                width, eps = (GI, sh.eps6) if conv else (T, sh.eps5)
                act.wait_ge(var_done, g + 1)
                if due(g):
                    act.wait_ge(xn_done, g)
                act.activation(rs[:, :], st[:, 0:width], ACT.Ln, bias=eps[:, 0:1]).then_inc(ln_done, 1)
                act.wait_ge(ln_done, g + 1)
                act.activation(rs[:, :], rs[:, :], ACT.Exp, scale=-0.5).then_inc(rs_done, 1)

            def q_out(at):
                g = at.g
                if not at.exists() or not conv:
                    return
                act.wait_ge(q_mm, g + 1)
                if due(g):
                    act.wait_ge(s_mm, g)
                act.activation(qt[:, :], pjq[:, 0:T], ACT.Identity, bias=b_use[:, 0:1], scale=C ** -0.5).then_inc(q_done, 1)

            def k_out(at):
                g = at.g
                if not at.exists() or not conv:
                    return
                act.wait_ge(k_mm, g + 1)
                if due(g):
                    act.wait_ge(s_mm, g)
                act.activation(kt[:, :], pjk[:, 0:T], ACT.Identity, bias=b_use[:, 1:2]).then_inc(k_done, 1)

            def expo(at):
                g = at.g
                if not at.exists():
                    return
                act.wait_ge(sub_done, g + 1)
                if due(g - 1):
                    act.wait_ge(t_mm, g - 1)
                act.activation(pr[at.r % 2][:, :, 0:N], sc[:, :, :], ACT.Exp).then_inc(exp_done, 1)

            def turned(at):
                g = at.g
                if not at.exists():
                    return
                act.wait_ge(t_mm, g + 1)
                if due(g - 1):
                    act.wait_ge(pv_mm, g - 1)
                for r in range(2):
                    rows = slice(B1 * r, B1 * r + N)
                    for m in range(2):
                        last = act.activation(pt[at.r % 2][rows, m, :, r, :],
                                              ptps[rows, 0:2 * R].rearrange("k (q n) -> k q n", q=2)[:, :, B1 * m:B1 * m + N], ACT.Copy)
                last.then_inc(t_done, 1)

            def o_out(at):
                g = at.g
                if not at.exists() or not conv:
                    return
                act.wait_ge(pv_mm, g + 1)
                if due(g):
                    act.wait_ge(out_mm, g)
                act.activation(ot[:, :], ops_[:, 0:T], ACT.Copy).then_inc(o_done, 1)

            def body(s):
                o_out(s.ahead(-1))
                expo(s.ahead(1))
                turned(s)
                square(s.ahead(4))
                q_out(s.ahead(2))
                rstd(s.ahead(3))
                k_out(s.ahead(2))

            over_steps(act, body, LEAD)


def gate_phase(nc, sh, kind, gates_dram, loads):
    X, XN, ident = sh.X, sh.XN, sh.ident
    wg, bg = (sh.wg2, sh.bg2) if kind == "g2" else (sh.wg3, sh.bg3)
    NT = T // TT
    TILES = NG * NT
    BLOCKS = TILES * EXPERTS // C
    LEAD = 3
    with ExitStack() as ctx:
        def sb(name, shape, dt=F32):
            return ctx.enter_context(nc.sbuf_tensor(f"{kind}_{name}", shape, dt))

        def ps(name, shape):
            return ctx.enter_context(nc.psum_tensor(f"{kind}_{name}", shape, F32))

        sem = ctx.enter_context(PhaseSemaphores(nc, kind))

        cps = [ps(f"cen{i}", [C, 512]) for i in range(4)]
        st = ps("st", [C, 512])
        log_ps = [ps(f"log{i}", [TT, 512]) for i in range(2)]
        sq = sb("sq", [C, T])
        rs = [sb(f"rs{i}", [C, T]) for i in range(2)]
        xn = [sb(f"xn{i}", [C, T]) for i in range(2)]
        lg = [sb(f"lg{i}", [TT, NT, EXPERTS]) for i in range(2)]
        top = [sb(f"top{i}", [TT, NT, 8]) for i in range(2)]
        idx = [sb(f"idx{i}", [TT, NT, 8], U32) for i in range(2)]
        idf = sb("idf", [TT, TILES, 2])
        gap, ex, den = sb("gap", [TT, TILES]), sb("ex", [TT, TILES]), sb("den", [TT, TILES])
        g1, g2 = sb("g1", [TT, TILES]), sb("g2", [TT, TILES])
        pick = [sb(f"pick{i}", [TT, TILES, EXPERTS]) for i in range(2)]
        hi, lo = sb("hi", [C, BLOCKS * TT], F32R), sb("lo", [C, BLOCKS * TT])

        mean_done, sq_done, var_done, ln_done, rs_done = sem("centred"), sem("squared"), sem("variance"), sem("logvar"), sem("rstd")
        xn_done, keep_done, log_mm, lg_done = sem("normed"), sem("kept"), sem("logits"), sem("biased")
        top_done, idx_done = sem("top"), sem("index")
        gap_done, exp_done, idf_done, den_done, g1_done, g2_done = sem("gap"), sem("exped"), sem("indexf"), sem("den"), sem("g1"), sem("g2")
        preloaded = sem("preloaded")
        pick_done, comb_done, gt_mm, hi_done, lo_done, stored = sem("picks"), sem("combined"), sem("turned"), sem("high"), sem("low"), sem("stored")

        block = ctx.enter_context(nc.Block())

        def tiles(g):
            return slice(g * NT, g * NT + NT) if isinstance(g, int) else bass.ds(g * NT, NT)

        @block.tensor
        def _(pe):
            def mean(at):
                g = at.g
                if not at.exists():
                    return
                if due(g - 3):
                    pe.wait_ge(xn_done, g - 3)
                pe.matmul(cps[at.r][:, 0:T], sh.centre_w[:, :], X[:, cols(g)], start=True, stop=True).then_inc(mean_done, 1)

            def var(at):
                g = at.g
                if not at.exists():
                    return
                pe.wait_ge(sq_done, g + 1)
                if due(g):
                    pe.wait_ge(ln_done, g)
                pe.matmul(st[:, 0:T], sh.mean_w[:, :], sq[:, :], start=True, stop=True).then_inc(var_done, 1)

            def logits(at):
                g = at.g
                if not at.exists():
                    return
                pe.wait_ge(xn_done, g + 1)
                if due(g - 1):
                    pe.wait_ge(lg_done, g - 1)
                for t in range(NT):
                    last = pe.matmul(log_ps[at.r % 2][:, t * EXPERTS:(t + 1) * EXPERTS], xn[at.r % 2][:, t * TT:(t + 1) * TT], wg[:, :],
                                     start=True, stop=True, skip_group_check=True)
                last.then_inc(log_mm, 1)

            def body(s):
                mean(s.ahead(3))
                var(s.ahead(2))
                logits(s)

            over_steps(pe, body, LEAD)
            pe.wait_ge(xn_done, NG)
            pe.wait_ge(comb_done, 1)
            half = BLOCKS // 2
            for q in range(BLOCKS):
                pe.transpose(cps[q // half][:, q % half * TT:(q % half + 1) * TT],
                             pick[0][:, q * (C // EXPERTS):(q + 1) * (C // EXPERTS), :].rearrange("q t e -> q (t e)"),
                             ident[0:TT, 0:TT]).then_inc(gt_mm, 1)

        @block.scalar
        def _(act):
            act.preload_act_table_set(EXP_SET)

            def square(at):
                g = at.g
                if not at.exists():
                    return
                act.wait_ge(mean_done, g + 1)
                if due(g):
                    act.wait_ge(var_done, g)
                act.activation(sq[:, :], cps[at.r][:, 0:T], ACT.Square).then_inc(sq_done, 1)

            def rstd(at):
                g = at.g
                if not at.exists():
                    return
                act.wait_ge(var_done, g + 1)
                if due(g - 1):
                    act.wait_ge(xn_done, g - 1)
                r = rs[at.r % 2][:, :]
                act.activation(r, st[:, 0:T], ACT.Ln, bias=sh.eps5[:, 0:1]).then_inc(ln_done, 1)
                act.wait_ge(ln_done, g + 1)
                act.activation(r, r, ACT.Exp, scale=-0.5).then_inc(rs_done, 1)

            def body(s):
                square(s.ahead(3))
                rstd(s.ahead(2))

            over_steps(act, body, LEAD)
            act.wait_ge(gap_done, NG)
            act.activation(ex[:, :], gap[:, :], ACT.Exp).then_inc(exp_done, 1)

        @block.vector
        def _(dve):
            def body(s):
                old, new, g = s.ahead(-1), s.ahead(1), s.g
                if old.exists() and due(g):
                    dve.wait_ge(top_done, g)
                    if due(g - 2):
                        dve.wait_ge(idf_done, g - 2)
                    dve.tensor_tensor(gap[:, tiles(g - 1)], top[old.r % 2][:, :, 1], top[old.r % 2][:, :, 0], ALU.subtract).then_inc(gap_done, 1)
                    for t in range(NT):
                        last = dve.max_index(idx[old.r % 2][:, t, :], top[old.r % 2][:, t, :], lg[old.r % 2][:, t, :])
                    last.then_inc(idx_done, 1)
                if new.exists():
                    dve.wait_ge(rs_done, g + 2)
                    if due(g):
                        dve.wait_ge(log_mm, g)
                        dve.wait_ge(keep_done, g)
                    dve.tensor_tensor(xn[new.r % 2][:, :], cps[new.r][:, 0:T], rs[new.r % 2][:, :], ALU.mult).then_inc(xn_done, 1)
                if s.exists():
                    dve.wait_ge(log_mm, g + 1)
                    dve.tensor_tensor(lg[s.r % 2][:, :, :], log_ps[s.r % 2][:, 0:NT * EXPERTS].rearrange("q (t e) -> q t e", e=EXPERTS),
                                      bg[:, :][:, None, :].to_broadcast([TT, NT, EXPERTS]), ALU.add).then_inc(lg_done, 1)
                if new.exists():
                    dve.wait_ge(xn_done, g + 2)
                    dve.tensor_copy(XN[:, cols(new.g)], xn[new.r % 2][:, :]).then_inc(keep_done, 1)
                if old.exists() and due(g):
                    dve.wait_ge(idx_done, g)
                    if s.exists():
                        dve.wait_ge(lg_done, g + 1)
                    if due(g - 1):
                        dve.wait_ge(gap_done, g - 1)
                    dve.tensor_copy(idf[:, tiles(g - 1), :], idx[old.r % 2][:, :, 0:2]).then_inc(idf_done, 1)
                elif s.exists():
                    dve.wait_ge(lg_done, g + 1)
                if s.exists():
                    for t in range(NT):
                        last = dve.max(top[s.r % 2][:, t, :], lg[s.r % 2][:, t, :])
                    last.then_inc(top_done, 1)

            over_steps(dve, body, LEAD)

            iota = sh.iota8[:, :][:, None, :].to_broadcast([TT, TILES, EXPERTS])
            dve.wait_ge(idf_done, NG)
            for i in range(2):
                dve.tensor_tensor(pick[i][:, :, :], iota, idf[:, :, i:i + 1].to_broadcast([TT, TILES, EXPERTS]),
                                  ALU.is_equal).then_inc(pick_done, 1)
            dve.wait_ge(exp_done, 1)
            dve.tensor_scalar(den[:, :], ex[:, :], 1.0, None, ALU.add).then_inc(den_done, 1)
            dve.wait_ge(den_done, 1)
            dve.reciprocal(g1[:, :], den[:, :]).then_inc(g1_done, 1)
            dve.wait_ge(g1_done, 1)
            dve.tensor_tensor(g2[:, :], g1[:, :], ex[:, :], ALU.mult).then_inc(g2_done, 1)
            dve.wait_ge(g2_done, 1)
            dve.wait_ge(pick_done, 2)
            for i, gate in enumerate((g1, g2)):
                dve.tensor_tensor(pick[i][:, :, :], pick[i][:, :, :], gate[:, :][:, :, None].to_broadcast([TT, TILES, EXPERTS]),
                                  ALU.mult).then_inc(pick_done, 1)
            dve.wait_ge(pick_done, 4)
            dve.tensor_tensor(pick[0][:, :, :], pick[0][:, :, :], pick[1][:, :, :], ALU.add).then_inc(comb_done, 1)
            half = BLOCKS // 2
            for q in range(2):
                part_of = slice(q * half * TT, (q + 1) * half * TT)
                dve.wait_ge(gt_mm, (q + 1) * half)
                dve.tensor_copy(hi[:, part_of], cps[q][:, 0:half * TT]).then_inc(hi_done, 1)
                dve.wait_ge(hi_done, q + 1)
                dve.tensor_tensor(lo[:, part_of], cps[q][:, 0:half * TT], hi[:, part_of].bitcast(F32), ALU.subtract).then_inc(lo_done, 1)

        @block.sync
        def _(sp):
            for to, what in loads:
                sp.dma_start(to, what).then_inc(preloaded, 16)
            dst = gates_dram.rearrange("h (q p) c -> h p q c", p=C)
            sp.wait_ge(lo_done, 2)
            for i, src in enumerate((hi[:, :].bitcast(F32), lo[:, :])):
                sp.dma_start(dst[i], src.rearrange("p (q c) -> p q c", c=TT)).then_inc(stored, 16)
            sp.wait_ge(stored, 32)
            sp.wait_ge(preloaded, 16 * len(loads))


PIECE = 512


def pieces(count):
    order = [(0, 0)]
    for q in range(1, count):
        order += [(0, q), (1, q - 1)]
    return order + [(1, count - 1)]


def weight_piece(w1, w2, n):
    m, q = pieces(w1.shape[1] // PIECE)[n]
    if m == 0:
        return w1[:, q * PIECE:(q + 1) * PIECE].rearrange("p (k c) -> p k c", c=C)
    return w2[q * PIECE:(q + 1) * PIECE, :].rearrange("(k p) c -> p k c", p=C)


def hidden_buffers(chunks):
    return 6 if chunks % 6 == 0 else 4


def experts_weights(nc, ctx, sh, kind, w1, b1, w2, b2):
    def sb(name, shape):
        return ctx.enter_context(nc.sbuf_tensor(f"{kind}_{name}", shape, F32))

    raw = [sb(f"raw{i}", [C, PIECE]) for i in range(2)]
    b1t, b2r, h = sb("b1t", [C, w1.shape[1] // C]), sb("b2r", [16, C]), sb("h", [C, hidden_buffers(w1.shape[1] // C) * T])
    selr = h[0:16, 0:sh.sel_dram[kind].shape[1]]
    loads = [(raw[n][:, :].rearrange("p (k c) -> p k c", c=C), weight_piece(w1, w2, n)) for n in range(2)]
    loads += [(b1t[:, :], b1), (b2r[0:8, :], b2), (b2r[8:16, :], b2), (selr, sh.sel_dram[kind])]
    return (raw, b1t, b2r, h, selr), loads


def experts_phase(nc, sh, kind, gates_dram, weights, w1, w2, func, out_dram):
    X, XN = sh.X, sh.XN
    F = w1.shape[1]
    NC = F // C
    CP = PIECE // C
    NP = F // PIECE
    per = 4 if (F // EXPERTS) % C == 0 else 1
    LA = 4
    NGS = 4 if per == 1 else 2
    NB = hidden_buffers(NC)
    with ExitStack() as ctx:
        def sb(name, shape, dt=F32):
            return ctx.enter_context(nc.sbuf_tensor(f"{kind}_{name}", shape, dt))

        def ps(name, shape):
            return ctx.enter_context(nc.psum_tensor(f"{kind}_{name}", shape, F32))

        sem = ctx.enter_context(PhaseSemaphores(nc, kind))

        hps = [ps(f"hps{i}", [C, 512]) for i in range(4)]
        gps = [ps(f"gps{i}", [C, 512]) for i in range(2)]
        ops_ = [ps(f"ops{i}", [C, 512]) for i in range(2)]
        raw, b1t, b2r, h_all, selr = weights
        w1h, w1l = sb("w1h", [C, F], F32R), sb("w1l", [C, F], F32R)
        w2h, w2l = sb("w2h", [C, NC * C], F32R), sb("w2l", [C, NC * C], F32R)
        sel = sb("sel", [16, (NC // per) * C], F32R)
        b2h, b2l = sb("b2h", [16, C], F32R), sb("b2l", [16, C], F32R)
        xh = [sb(f"xh{i}", [C, T], F32R) for i in range(2)]
        xl = [sb(f"xl{i}", [C, T], F32R) for i in range(2)]
        ct = [sb(f"ct{i}", [16, T], F32R) for i in range(2)]
        gs = [sb(f"gs{i}", [C, T]) for i in range(NGS)]
        act_h = [h_all[:, i * T:(i + 1) * T] for i in range(NB)]
        hh = [sb(f"hh{i}", [C, T], F32R) for i in range(NB)]
        hl = [sb(f"hl{i}", [C, T], F32R) for i in range(NB)]

        small_split = sem("small_split")
        raw_loaded = [sem(f"raw_loaded{i}") for i in range(2)]
        w_high, w_split = sem("w_high"), sem("w_split")
        ct_loaded = [sem(f"ct_loaded{i}") for i in range(2)]
        xh_done, x_split = sem("xh"), sem("x_split")
        g_mm, g_done, h_mm, h_done = sem("gate_mm"), sem("gate_out"), sem("hidden_mm"), sem("hidden_out")
        gated = [sem("gated_pool"), sem("gated_dve")]
        hh_done, h_split, o_mm, res_done, stored = sem("hh"), sem("h_split"), sem("out_mm"), sem("residual"), sem("stored")

        block = ctx.enter_context(nc.Block())

        def on_dve(g, k):
            return k % 4 == 3 and not (isinstance(g, int) and g == 0)

        order = pieces(NP)

        @block.sync
        def _(sp):
            def load_piece(n):
                sp.wait_ge(w_split, n - 1)
                sp.dma_start(raw[n % 2][:, :].rearrange("p (k c) -> p k c", c=C), weight_piece(w1, w2, n)).then_inc(raw_loaded[n % 2], 16)

            def load_gates(g, j):
                if not exists(g):
                    return
                if due((g - 1) * NC):
                    sp.wait_ge(o_mm, (g - 1) * NC)
                NT = T // TT
                for i in range(2):
                    src = gates_dram[i, g * NT * EXPERTS:(g + 1) * NT * EXPERTS] if isinstance(g, int) else gates_dram[i, bass.ds(g * NT * EXPERTS, NT * EXPERTS)]
                    sp.dma_start(ct[j][i * EXPERTS:(i + 1) * EXPERTS, :].bitcast(F32).rearrange("e (t c) -> e t c", c=TT),
                                 src.rearrange("(t e) c -> e t c", e=EXPERTS)).then_inc(ct_loaded[j], 16)

            load_gates(0, 0)
            load_gates(1, 1)
            for n in range(2, 2 * NP):
                load_piece(n)

            def body(g, j):
                load_gates(g + 2, j)

            over_groups(sp, body)
            if out_dram is not None:
                sp.wait_ge(stored, 16 * NG)

        @block.tensor
        def _(pe):
            def gate(g, j, k):
                if k % per or not exists(g):
                    return
                q = k // per
                n = g * (NC // per) + q
                if q == 0:
                    if due(32 * (g // 2 + 1) if isinstance(g, int) else (g - j) * 16 + 32):
                        pe.wait_ge(ct_loaded[j], 32 * (g // 2 + 1) if isinstance(g, int) else (g - j) * 16 + 32)
                    if isinstance(g, int) and g == 0:
                        pe.wait_ge(small_split, 4)
                if due(n - 1):
                    pe.wait_ge(g_done, n - 1)
                pe.matmul(gps[q % 2][:, 0:T], sel[:, q * C:(q + 1) * C], ct[j][:, :], start=True, stop=True).then_inc(g_mm, 1)

            def hidden(g, j, k):
                if not exists(g):
                    return
                n = g * NC + k
                if k == 0:
                    pe.wait_ge(x_split, g + 1)
                if isinstance(g, int) and g == 0:
                    pe.wait_ge(w_split, order.index((0, k // CP)) + 1)
                if due(n - 3):
                    pe.wait_ge(h_done, n - 3)
                c = slice(k * C, (k + 1) * C)
                pe.matmul(hps[k % 4][:, 0:T], w1h[:, c], xh[j][:, :], start=True, stop=False)
                pe.matmul(hps[k % 4][:, 0:T], w1h[:, c], xl[j][:, :], start=False, stop=False)
                pe.matmul(hps[k % 4][:, 0:T], w1l[:, c], xh[j][:, :], start=False, stop=True).then_inc(h_mm, 1)

            def output(g, j, k):
                n = g * NC + k
                if k == 0:
                    if due(g - 1):
                        pe.wait_ge(res_done, g - 1)
                    pe.matmul(ops_[j][:, 0:T], b2h[:, :], ct[j][:, :], start=True, stop=False)
                    pe.matmul(ops_[j][:, 0:T], b2l[:, :], ct[j][:, :], start=False, stop=False)
                if isinstance(g, int) and g == 0:
                    pe.wait_ge(w_split, order.index((1, k // CP)) + 1)
                pe.wait_ge(h_split, n + 1)
                c = slice(k * C, (k + 1) * C)
                pe.matmul(ops_[j][:, 0:T], w2h[:, c], hh[k % NB][:, :], start=False, stop=False)
                pe.matmul(ops_[j][:, 0:T], w2h[:, c], hl[k % NB][:, :], start=False, stop=False)
                pe.matmul(ops_[j][:, 0:T], w2l[:, c], hh[k % NB][:, :], start=False, stop=(k == NC - 1)).then_inc(o_mm, 1)

            def ahead(g, j, k):
                if k + LA < NC:
                    gate(g, j, k + LA)
                    hidden(g, j, k + LA)
                else:
                    gate(g + 1, 1 - j, k + LA - NC)
                    hidden(g + 1, 1 - j, k + LA - NC)

            for k in range(LA):
                gate(0, 0, k)
                hidden(0, 0, k)

            def body(g, j):
                for k in range(NC):
                    ahead(g, j, k)
                    output(g, j, k)

            over_groups(pe, body)

        @block.scalar
        def _(act):
            def store(g):
                if out_dram is None or (isinstance(g, int) and g < 0):
                    return
                act.wait_ge(res_done, g + 1)
                dst = out_dram[g * GI:(g + 1) * GI] if isinstance(g, int) else out_dram[bass.ds(g * GI, GI)]
                act.dma_start(dst.rearrange("b c n -> c b n"), X[:, cols(g)].rearrange("c (b n) -> c b n", n=N)).then_inc(stored, 16)

            def high_x(g, j):
                if not exists(g):
                    return
                if due((g - 1) * NC):
                    act.wait_ge(h_mm, (g - 1) * NC)
                act.activation(xh[j][:, :], XN[:, cols(g)], ACT.Copy).then_inc(xh_done, 1)

            def high_piece(n):
                m, q = order[n]
                if n >= 2:
                    act.wait_ge(raw_loaded[n % 2], 16 * (n // 2))
                act.activation((w1h if m == 0 else w2h)[:, q * PIECE:(q + 1) * PIECE], raw[n % 2][:, :], ACT.Copy).then_inc(w_high, 1)

            high_x(0, 0)
            high_piece(0)
            high_piece(1)
            high_piece(2)
            act.wait_ge(small_split, 1)

            def body(g, j):
                for k in range(NC):
                    n = g * NC + k
                    if isinstance(g, int) and g == 0 and k % 2 == 1 and 3 + k // 2 < 2 * NP:
                        high_piece(3 + k // 2)
                    if k == NC // 2:
                        store(g - 1)
                    if k == NC // 2 - 1:
                        high_x(g + 1, 1 - j)
                    if k % per == 0:
                        q = g * (NC // per) + k // per
                        act.wait_ge(g_mm, q + 1)
                        if due(n - per * (NGS - 1)):
                            act.wait_ge(hh_done, n - per * (NGS - 1))
                        act.activation(gs[(k // per) % NGS][:, :], gps[(k // per) % 2][:, 0:T], ACT.Copy).then_inc(g_done, 1)
                    act.wait_ge(h_mm, n + 1)
                    if due(n - NB + 1):
                        act.wait_ge(h_split, n - NB + 1)
                    act.activation(act_h[k % NB][:, :], hps[k % 4][:, 0:T], func, bias=b1t[:, k:k + 1]).then_inc(h_done, 1)

            over_groups(act, body)
            store(NG - 1)

        @block.gpsimd
        def _(pool):
            def body(g, j):
                for k in range(NC):
                    if on_dve(g, k):
                        continue
                    n = g * NC + k
                    if due(g * (NC // per) + k // per + 1):
                        pool.wait_ge(g_done, g * (NC // per) + k // per + 1)
                    pool.wait_ge(h_done, n + 1)
                    pool.tensor_tensor(act_h[k % NB][:, :], act_h[k % NB][:, :], gs[(k // per) % NGS][:, :], ALU.mult).then_inc(gated[0], 1)

            over_groups(pool, body)

        @block.vector
        def _(dve):
            def low_piece(n):
                m, q = order[n]
                high, low = (w1h, w1l) if m == 0 else (w2h, w2l)
                c = slice(q * PIECE, (q + 1) * PIECE)
                dve.wait_ge(w_high, n + 1)
                dve.tensor_tensor(low[:, c], raw[n % 2][:, :], high[:, c].bitcast(F32), ALU.subtract).then_inc(w_split, 1)

            def split_x(g, j):
                if not exists(g):
                    return
                dve.wait_ge(xh_done, g + 1)
                dve.tensor_tensor(xl[j][:, :], XN[:, cols(g)], xh[j][:, :].bitcast(F32), ALU.subtract).then_inc(x_split, 1)

            def residual(g, j):
                if isinstance(g, int) and g < 0:
                    return
                dve.wait_ge(o_mm, (g + 1) * NC)
                dve.tensor_tensor(X[:, cols(g)], ops_[j][:, 0:T], X[:, cols(g)], ALU.add).then_inc(res_done, 1)

            dve.tensor_copy(sel[:, :], selr).then_inc(small_split, 1)
            dve.tensor_copy(b2h[:, :], b2r[:, :]).then_inc(small_split, 1)
            dve.wait_ge(small_split, 2)
            dve.tensor_tensor(b2l[:, :], b2r[:, :], b2h[:, :].bitcast(F32), ALU.subtract).then_inc(small_split, 2)
            split_x(0, 0)
            low_piece(0)
            low_piece(1)
            low_piece(2)

            def body(g, j):
                first = isinstance(g, int) and g == 0
                for k in range(NC):
                    n = g * NC + k
                    if first and k % 2 == 1 and 3 + k // 2 < 2 * NP:
                        low_piece(3 + k // 2)
                    if on_dve(g, k):
                        dve.wait_ge(h_done, n + 1)
                        if due(g * (NC // per) + k // per + 1):
                            dve.wait_ge(g_done, g * (NC // per) + k // per + 1)
                        dve.tensor_tensor(act_h[k % NB][:, :], act_h[k % NB][:, :], gs[(k // per) % NGS][:, :], ALU.mult).then_inc(gated[1], 1)
                        if due((g - 1) * (NC // 4) + k // 4 + 1):
                            dve.wait_ge(gated[1], (g - 1) * (NC // 4) + k // 4 + 1)
                    elif first:
                        dve.wait_ge(gated[0], k + 1)
                    else:
                        if due(NC // 4 + g * (NC - NC // 4) + k - k // 4 + 1):
                            dve.wait_ge(gated[0], NC // 4 + g * (NC - NC // 4) + k - k // 4 + 1)
                    if due(n - NB + 1):
                        dve.wait_ge(o_mm, n - NB + 1)
                    dve.tensor_copy(hh[k % NB][:, :], act_h[k % NB][:, :]).then_inc(hh_done, 1)
                    dve.wait_ge(hh_done, n + 1)
                    dve.tensor_tensor(hl[k % NB][:, :], act_h[k % NB][:, :], hh[k % NB][:, :].bitcast(F32), ALU.subtract).then_inc(h_split, 1)
                    if k == NC // 2:
                        split_x(g + 1, 1 - j)
                    if k == 1:
                        residual(g - 1, 1 - j)

            over_groups(dve, body)
            residual(NG - 1, 1)


def build(nc, a, out):
    sh = Shared()
    gates = nc.dram_tensor("gates", (2, NG * (T // TT) * EXPERTS, TT), F32, kind="Internal").ap()
    with ExitStack() as ctx:
        def sb(name, shape):
            return ctx.enter_context(nc.sbuf_tensor(name, shape, F32))

        sh.X = sb("X", [C, IMAGES * N])
        sh.ident, sh.group_w = sb("ident", [C, C]), sb("group_w", [C, C])
        sh.mean_w, sh.centre_w = sb("mean_w", [C, C]), sb("centre_w", [C, C])
        sh.kmask = sb("kmask", [C, HP])
        sh.iota8, sh.pos = sb("iota8", [TT, EXPERTS]), sb("pos", [C, N])
        sh.eps5, sh.eps6 = sb("eps5", [C, 1]), sb("eps6", [C, 1])
        sh.wg2, sh.wg3 = sb("wg2", [C, EXPERTS]), sb("wg3", [C, EXPERTS])
        sh.bg2, sh.bg3 = sb("bg2", [TT, EXPERTS]), sb("bg3", [TT, EXPERTS])
        sh.sel_dram = {"moe2": a["c_sel2"], "moe3": a["c_sel3"]}
        with ExitStack() as early:
            window, window_loads = heads_weights(nc, early, a, "window")
            conv, conv_loads = conv_weights(nc, early, a)
            load_constants(nc, window_loads + [
                (sh.centre_w[:, :], a["c_centre_w"]), (sh.mean_w[:, :], a["c_mean_w"]), (sh.ident[:, :], a["c_ident"]),
                (sh.kmask[:, :], a["c_kmask"]), (sh.eps5[:, :], a["c_eps5"])])
            heads_phase(nc, sh, "window", window, a["x"], conv_loads + [
                (sh.group_w[:, :], a["c_group_w"]), (sh.iota8[:, :], a["c_iota8"]), (sh.pos[:, :], a["c_pos"]),
                (sh.eps6[:, :], a["c_eps6"]), (sh.wg2[:, :], a["L2_ffn_Wg"]), (sh.wg3[:, :], a["L3_ffn_Wr"]),
                (sh.bg2[:, :], a["L2_ffn_bg"].to_broadcast([TT, EXPERTS])),
                (sh.bg3[:, :], a["L3_ffn_br"].to_broadcast([TT, EXPERTS]))])
            single_phase(nc, sh, "conv", conv)
        single_phase(nc, sh, "token")
        with ExitStack() as middle:
            scales, scales_loads = heads_weights(nc, middle, a, "scales")
            with ExitStack() as moe:
                sh.XN = moe.enter_context(nc.sbuf_tensor("XN2", [C, IMAGES * N], F32))
                first, loads = experts_weights(nc, moe, sh, "moe2", a["L2_ffn_W1"], a["L2_ffn_b1"], a["L2_ffn_W2"], a["L2_ffn_b2"])
                gate_phase(nc, sh, "g2", gates, loads + scales_loads)
                experts_phase(nc, sh, "moe2", gates, first, a["L2_ffn_W1"], a["L2_ffn_W2"], ACT.Gelu, None)
            heads_phase(nc, sh, "scales", scales, None)
        with ExitStack() as moe:
            sh.XN = moe.enter_context(nc.sbuf_tensor("XN3", [C, IMAGES * N], F32))
            first, loads = experts_weights(nc, moe, sh, "moe3", a["L3_ffn_W1"], a["L3_ffn_b1"], a["L3_ffn_W2"], a["L3_ffn_b2"])
            gate_phase(nc, sh, "g3", gates, loads)
            experts_phase(nc, sh, "moe3", gates, first, a["L3_ffn_W1"], a["L3_ffn_W2"], ACT.Gelu_apprx_tanh, out)


def constants():
    import numpy as np
    f = np.float32
    c = np.arange(C)
    one = {"c_ident": np.eye(C, dtype=f), "c_mean_w": np.full((C, C), 1.0 / C, f)}
    one["c_centre_w"] = one["c_ident"] - one["c_mean_w"]
    one["c_group_w"] = np.where(c[:, None] // 4 == c[None, :] // 4, f(1.0 / (4 * N)), f(0)).astype(f)
    one["c_kmask"] = (c[:, None] // HD % HP == np.arange(HP)[None, :]).astype(f)
    one["c_iota8"] = np.tile(np.arange(EXPERTS, dtype=f), (TT, 1))
    inv = f(10000.0) ** (np.arange(0, C, 2, dtype=f) / f(C))
    ang = np.arange(N, dtype=f)[:, None] / inv
    one["c_pos"] = np.ascontiguousarray(np.concatenate([np.sin(ang), np.cos(ang)], -1).T.astype(f))
    one["c_eps5"], one["c_eps6"] = np.full((C, 1), 1e-5, f), np.full((C, 1), 1e-6, f)
    one["c_zeros"] = np.zeros((B1 - N, HEADS * N), f)
    for name, width, spread in (("c_sel2", 192, 1536), ("c_sel3", 128, 1024)):
        row = (np.arange(EXPERTS)[:, None] == np.arange(spread)[None, :] // width).astype(f)
        one[name] = np.concatenate([row, row])
    return one


def layout(inputs):
    import numpy as np
    a = {k: np.asarray(v) for k, v in inputs.items()}
    a["x"] = a["x"].reshape(IMAGES, C, N)
    side = 7
    rev = a.pop("L0_conv_rel_table")[::-1, ::-1, :]
    win = [rev[i:i + side, j:j + side].transpose(2, 0, 1) for i in reversed(range(side)) for j in reversed(range(side))]
    a["L0_conv_rel_bias"] = np.stack(win).reshape(N, HEADS * N)
    for n in ("wq", "wk", "wv", "wp"):
        a[f"L1_conv_{n}"] = a[f"L1_conv_{n}"].T
    for n, v in list(a.items()):
        if v.ndim == 1 and v.shape[0] == C:
            a[n] = v.reshape(C, 1)
    a["L2_ffn_bg"], a["L3_ffn_br"] = a["L2_ffn_bg"].reshape(1, EXPERTS), a["L3_ffn_br"].reshape(1, EXPERTS)
    a["L3_ffn_Wr"] = a["L3_ffn_Wr"].T
    for n in ("L2_ffn", "L3_ffn"):
        a[f"{n}_W1"] = a[f"{n}_W1"].transpose(1, 0, 2).reshape(C, -1)
        a[f"{n}_W2"] = a[f"{n}_W2"].reshape(-1, C)
        a[f"{n}_b1"] = a[f"{n}_b1"].reshape(-1, C).T
    return {k: np.ascontiguousarray(v) for k, v in a.items()}


def kernel(**inputs):
    import concourse.bacc as _bacc
    from concourse.bass_utils import run_bass_kernel_spmd as _run

    nc = _bacc.Bacc("TRN2", target_bir_lowering=False, num_devices=1)
    arrays = {f"in_{k}": v for k, v in {**layout(inputs), **constants()}.items()}
    args = {k[3:]: nc.dram_tensor(k, v.shape, F32, kind="ExternalInput").ap() for k, v in arrays.items()}
    out = nc.dram_tensor("out_y", (IMAGES, C, N), F32, kind="ExternalOutput").ap()
    build(nc, args, out)
    r = _run(nc, [arrays], core_ids=[0])
    return r.results[0]["out_y"].reshape(IMAGES, C, 7, 7)
```
